# Optimizing a Trainium2 kernel written in Bass

```python
import numpy as np
import jax
import jax.numpy as jnp

def _softmax(x, axis=-1):
    return jax.nn.softmax(x, axis=axis)
def _gelu(x):
    return jax.nn.gelu(x, approximate=True)
def _silu(x):
    return jax.nn.silu(x)
def _sigmoid(x):
    return jax.nn.sigmoid(x)
def _layernorm(x, axis=-1, eps=1e-5):
    m = jnp.mean(x, axis=axis, keepdims=True)
    v = jnp.var(x, axis=axis, keepdims=True)
    return (x - m) / jnp.sqrt(v + eps)
def _scatter_add(tgt, idx, src, axis=0):
    return tgt.at[idx].add(src)
def _segment_sum(src, seg, n):
    return jax.ops.segment_sum(src, seg, n)

kernel_name = 'mk_conv_attn_hybrid_d2_conv_nchw256_bb8e4e'

def setup_inputs(seed: int = 0):
    np.random.seed(seed)
    _w = jnp.asarray
    def _rec_inputs():
        import jax
        import jax.numpy as jnp
        _gk = jax.random.key(seed)
        x = 7.22e-05 + 1 * jax.random.normal(jax.random.fold_in(_gk, 1), (8, 256, 64, 64), jnp.float32)
        return x
    x = _rec_inputs()
    def _L0_conv_setup():
        import jax, jax.numpy as jnp
        import numpy as np
        WINDOW = 7
        EPS = 1e-08

        def _unfold_patches(feat, win):
            b, r, h, w = feat.shape
            pad = win // 2
            fp = jnp.pad(feat, ((0, 0), (0, 0), (pad, pad), (pad, pad)))
            shifts = [fp[:, :, i:i + h, j:j + w] for i in range(win) for j in range(win)]
            return jnp.stack(shifts, axis=2)
        key = jax.random.key(seed)
        k1, k2, k3 = jax.random.split(key, 3)
        b, c, h, w = (8, 256, 64, 64)
        reduced = max(c // 4, 16)
        x = jax.random.normal(k1, (b, c, h, w), dtype=jnp.float32)
        W_reduce = jax.random.normal(k2, (reduced, c), dtype=jnp.float32) * (1.0 / np.sqrt(c))
        W_proj = jax.random.normal(k3, (c, reduced), dtype=jnp.float32) * (1.0 / np.sqrt(reduced))
        return {'x': x, 'W_reduce': W_reduce, 'W_proj': W_proj}
    _L0_conv_all = _L0_conv_setup()
    _L0_conv_in = {k: v for k, v in _L0_conv_all.items() if k in ('W_reduce', 'W_proj', )}
    del _L0_conv_all

    def _L1_attn_setup():
        import jax, jax.numpy as jnp
        import numpy as np
        HEADS = 4
        DIM_HEAD = 32
        key = jax.random.key(seed)
        k1, k2, k3 = jax.random.split(key, 3)
        B, L, D = (16, 8192, 256)
        hidden = HEADS * DIM_HEAD
        x = jax.random.normal(k1, (B, L, D), dtype=jnp.float32)
        W_qkv = jax.random.normal(k2, (D, 3 * hidden), dtype=jnp.float32) * D ** (-0.5)
        W_out = jax.random.normal(k3, (hidden, D), dtype=jnp.float32) * hidden ** (-0.5)
        b_out = jnp.zeros((D,), dtype=jnp.float32)
        return {'x': x, 'W_qkv': W_qkv, 'W_out': W_out, 'b_out': b_out}
    _L1_attn_all = _L1_attn_setup()
    _L1_attn_in = {k: v for k, v in _L1_attn_all.items() if k in ('W_qkv', 'W_out', 'b_out', )}
    del _L1_attn_all

    def _L1_ffn_setup():
        import math
        import jax, jax.numpy as jnp
        import numpy as np
        CAPACITY_FACTOR = 1.25
        key = jax.random.key(seed)
        ks = jax.random.split(key, 5)
        B, L, D, F, E = (8, 8192, 256, 1024, 8)
        h = jax.random.normal(ks[0], (B, L, D), dtype=jnp.float32)
        gate_w = jax.random.normal(ks[1], (D, E), dtype=jnp.float32) * 0.02
        gate_b = jnp.zeros((E,), dtype=jnp.float32)
        w1 = jax.random.normal(ks[2], (E, D, F), dtype=jnp.float32) * (1.0 / math.sqrt(D))
        b1 = jnp.zeros((E, F), dtype=jnp.float32)
        w2 = jax.random.normal(ks[3], (E, F, D), dtype=jnp.float32) * (1.0 / math.sqrt(F))
        b2 = jnp.zeros((E, D), dtype=jnp.float32)
        return {'h': h, 'gate_w': gate_w, 'gate_b': gate_b, 'w1': w1, 'b1': b1, 'w2': w2, 'b2': b2}
    _L1_ffn_all = _L1_ffn_setup()
    _L1_ffn_in = {k: v for k, v in _L1_ffn_all.items() if k in ('gate_w', 'gate_b', 'w1', 'b1', 'w2', 'b2', )}
    del _L1_ffn_all

    return {
        "x": x,
        "L0_conv_W_reduce": _L0_conv_in["W_reduce"],
        "L0_conv_W_proj": _L0_conv_in["W_proj"],
        "L1_attn_W_qkv": _L1_attn_in["W_qkv"],
        "L1_attn_W_out": _L1_attn_in["W_out"],
        "L1_attn_b_out": _L1_attn_in["b_out"],
        "L1_ffn_gate_w": _L1_ffn_in["gate_w"],
        "L1_ffn_gate_b": _L1_ffn_in["gate_b"],
        "L1_ffn_w1": _L1_ffn_in["w1"],
        "L1_ffn_b1": _L1_ffn_in["b1"],
        "L1_ffn_w2": _L1_ffn_in["w2"],
        "L1_ffn_b2": _L1_ffn_in["b2"],
    }

def reference(x, L0_conv_W_reduce, L0_conv_W_proj, L1_attn_W_qkv, L1_attn_W_out, L1_attn_b_out, L1_ffn_gate_w, L1_ffn_gate_b, L1_ffn_w1, L1_ffn_b1, L1_ffn_w2, L1_ffn_b2):
    import jax
    import jax.numpy as jnp
    def _L0_conv_ref(x, W_reduce, W_proj):
        import jax, jax.numpy as jnp
        import numpy as np
        WINDOW = 7
        EPS = 1e-08

        def _unfold_patches(feat, win):
            b, r, h, w = feat.shape
            pad = win // 2
            fp = jnp.pad(feat, ((0, 0), (0, 0), (pad, pad), (pad, pad)))
            shifts = [fp[:, :, i:i + h, j:j + w] for i in range(win) for j in range(win)]
            return jnp.stack(shifts, axis=2)
        b, c, h, w = x.shape
        win = WINDOW
        feat = jnp.einsum('rc,bchw->brhw', W_reduce, x)
        patches = _unfold_patches(feat, win)
        dot = jnp.einsum('brhw,brkhw->bkhw', feat, patches)
        cnorm = jnp.sqrt(jnp.sum(feat * feat, axis=1))
        pnorm = jnp.sqrt(jnp.sum(patches * patches, axis=1))
        sim = dot / (jnp.maximum(cnorm[:, None], EPS) * jnp.maximum(pnorm, EPS))
        att = jax.nn.softmax(sim, axis=1)
        corr = jnp.einsum('bkhw,brkhw->brhw', att, patches)
        enhanced = jnp.einsum('cr,brhw->bchw', W_proj, corr)
        return x + enhanced

    def _L1_attn_ref(x, W_qkv, W_out, b_out):
        import jax, jax.numpy as jnp
        import numpy as np
        HEADS = 4
        DIM_HEAD = 32
        B, L, D = x.shape
        scale = DIM_HEAD ** (-0.5)
        qkv = jnp.einsum('bld,df->blf', x, W_qkv)
        qkv = qkv.reshape(B, L, 3, HEADS, DIM_HEAD)
        q = jnp.transpose(qkv[:, :, 0], (0, 2, 1, 3)) * scale
        k = jax.nn.softmax(jnp.transpose(qkv[:, :, 1], (0, 2, 1, 3)), axis=2)
        v = jnp.transpose(qkv[:, :, 2], (0, 2, 1, 3))
        context = jnp.einsum('bhld,bhle->bhde', k, v)
        out = jnp.einsum('bhde,bhld->bhle', context, q)
        out = jnp.transpose(out, (0, 2, 1, 3)).reshape(B, L, HEADS * DIM_HEAD)
        return jnp.einsum('blf,fd->bld', out, W_out) + b_out

    def _L1_ffn_ref(h, gate_w, gate_b, w1, b1, w2, b2):
        import math
        import jax, jax.numpy as jnp
        import numpy as np
        CAPACITY_FACTOR = 1.25
        B, L, D = h.shape
        E = gate_w.shape[1]
        T = B * L
        C = max(1, math.ceil(CAPACITY_FACTOR * T / E))
        x = h.reshape(T, D)
        logits = x @ gate_w + gate_b
        probs = jax.nn.softmax(logits, axis=-1)
        idx = jnp.argmax(probs, axis=-1)
        prb = jnp.take_along_axis(probs, idx[:, None], axis=1)[:, 0]
        one_hot = jax.nn.one_hot(idx, E, dtype=jnp.float32)
        pos = (jnp.cumsum(one_hot, axis=0) * one_hot).sum(-1).astype(jnp.int32) - 1
        kept = pos < C
        pos_safe = jnp.where(kept, pos, C)
        buf = jnp.zeros((E, C, D), dtype=h.dtype).at[idx, pos_safe].set(x, mode='drop')
        hmid = jax.nn.relu(jnp.einsum('ecd,edf->ecf', buf, w1) + b1[:, None, :])
        ybuf = jnp.einsum('ecf,efd->ecd', hmid, w2) + b2[:, None, :]
        pos_g = jnp.minimum(pos, C - 1)
        y_tok = ybuf[idx, pos_g] * (prb * kept)[:, None]
        y = y_tok.reshape(B, L, D)
        y = jnp.nan_to_num(y, nan=0.0, posinf=10000.0, neginf=-10000.0)
        return y

    def _gn(v, G=32, eps=1e-5):
        B_, C_, H_, W_ = v.shape
        g = v.reshape(B_, G, C_ // G, H_, W_)
        m = jnp.mean(g, axis=(2, 3, 4), keepdims=True)
        s = jnp.var(g, axis=(2, 3, 4), keepdims=True)
        return ((g - m) / jnp.sqrt(s + eps)).reshape(v.shape)

    def _ln_c(v, eps=1e-6):
        m = jnp.mean(v, axis=1, keepdims=True)
        s = jnp.var(v, axis=1, keepdims=True)
        return (v - m) / jnp.sqrt(s + eps)

    def _ln_t(v, eps=1e-5):
        m = jnp.mean(v, axis=-1, keepdims=True)
        s = jnp.var(v, axis=-1, keepdims=True)
        return (v - m) / jnp.sqrt(s + eps)

    def _to_tokens(v):
        B_, C_, H_, W_ = v.shape
        return v.reshape(B_, C_, H_ * W_).transpose(0, 2, 1)
    def _from_tokens(t, like):
        B_, C_, H_, W_ = like.shape
        return t.transpose(0, 2, 1).reshape(B_, C_, H_, W_)

    x = _L0_conv_ref(x, L0_conv_W_reduce, L0_conv_W_proj)
    t = _to_tokens(x)
    t = t + _L1_attn_ref(_ln_t(t), L1_attn_W_qkv, L1_attn_W_out, L1_attn_b_out)
    t = t + _L1_ffn_ref(_ln_t(t), L1_ffn_gate_w, L1_ffn_gate_b, L1_ffn_w1, L1_ffn_b1, L1_ffn_w2, L1_ffn_b2)
    x = _from_tokens(t, x)
    return x


_drawn_inputs = setup_inputs


def setup_inputs(seed=0):
    import zlib

    import numpy as np

    out = dict(_drawn_inputs(seed))
    spreads = {'L1_attn_b_out': (0.0, 0.1),
     'L1_ffn_gate_b': (0.0, 0.1),
     'L1_ffn_b1': (0.0, 0.602),
     'L1_ffn_b2': (0.0, 0.423)}
    factors = {}
    for name, (base, spread) in spreads.items():
        noise = np.random.default_rng([zlib.crc32(name.encode()), seed]).standard_normal(out[name].shape)
        drawn = base * np.exp(spread * noise) if base else spread * noise
        out[name] = jnp.asarray(drawn.astype(out[name].dtype))
    for name, factor in factors.items():
        out[name] = (out[name] * factor).astype(out[name].dtype)
    return out
```

```python
import concourse.bass as bass
from concourse import mybir
from concourse.alu_op_type import AluOpType as ALU
from contextlib import ExitStack
import math

F32 = mybir.dt.float32
I32 = mybir.dt.int32
U32 = mybir.dt.uint32
ACT = mybir.ActivationFunctionType
AX = mybir.AxisListType.X

P = 128
C = 256
HALVES = C // P
R = 64
W = 64
WIN = 7
HD = 128
DH = 32
NE = 8
FF = 1024
FB = FF // P
TILES = 32
GRP = 4
GC = GRP * P
GROUPS = TILES // GRP
PAIRS = TILES // 2
HALO = 3 * W
EROW = 640
ROW = 260
NOWHERE = float(2 ** 22)
PEN = -30000.0
FMAX = 3.4028234663852886e38
STILE = 512
MEAN, RSTD, PRB, TOK = 256, 257, 258, 259


def sizes(nb):
    tokens = nb * TILES * P
    cap = max(1, math.ceil(1.25 * tokens / NE))
    ntile = -(-(tokens + NE * (STILE - 1)) // STILE)
    ntile += ntile % 2
    cp = -(-cap // STILE) * STILE + STILE
    zero = NE * cp
    return dict(nb=nb, tokens=tokens, cap=cap, ntile=ntile, cp=cp, zero=zero, rows=zero + STILE)


K_ID, K_TRI, K_BLK, K_NPAD, K_W8, K_EB, K_TOK, K_SCAN = 0, 128, 256, 384, 416, 424, 432, 464
K_TT, K_EC, K_N = 464 + NE * 33, 464 + NE * 33 + 80, 464 + NE * 33 + 80 + 16


def constants(np, s):
    k = np.zeros((P, K_N), np.float32)
    k[:, K_ID:K_ID + P] = np.eye(P)
    k[:, K_TRI:K_TRI + P] = np.triu(np.ones((P, P)))
    head = np.arange(HD) // DH
    k[:, K_BLK:K_BLK + HD] = (head[:, None] == head[None, :]) * DH ** -0.5
    p = np.arange(P)
    for i in range(TILES):
        y, x = 2 * i + p // W, p % W
        rows = np.minimum(y + 3, 63) - np.maximum(y - 3, 0) + 1
        cols = np.minimum(x + 3, W - 1) - np.maximum(x - 3, 0) + 1
        k[:, K_NPAD + i] = WIN * WIN - rows * cols
        k[:, K_TOK + i] = i * P + p
    k[:, K_W8:K_W8 + NE] = NE - np.arange(NE)
    k[:, K_EB:K_EB + NE] = np.arange(NE) * s["cp"]
    scan = np.ones((NE, TILES + 1))
    scan[:, 0] = 0
    k[:, K_SCAN:K_SCAN + NE * 33] = scan.reshape(-1)
    k[:, K_TT:K_TT + 80] = np.arange(80)
    k[:, K_EC:K_EC + 16] = np.arange(16) * STILE
    col = np.arange(W)
    band = np.zeros((W, 2 * W), np.float32)
    band[:, 0:W] = np.where(np.abs(col[:, None] - col[None, :]) > WIN // 2, PEN, 0)
    band[:, W:] = np.eye(W)
    return k, band


def build(nc, s, x, w_reduce, w_proj, w_qkv, w_out, b_out, gate_w, gate_b, w1, b1, w2, b2, konst, band, out):
    NB, NT, CP, CAP = s["nb"], s["ntile"], s["cp"], s["cap"]
    NPASS = 7
    FHW = P * (TILES + 3) + GC
    ctx = ExitStack()
    with ctx:
        def sem(name):
            return ctx.enter_context(nc.semaphore(name))

        rows = nc.dram_tensor("routed_rows", (s["rows"], ROW), F32).ap()
        primer = nc.dram_tensor("primer", (6, 16), F32).ap()
        toks = nc.dram_tensor("token_rows", (s["tokens"], C), F32).ap()

        def sb(name, shape, dt=F32, to=None):
            return (to or ctx).enter_context(nc.sbuf_tensor(name, shape, dt))

        primed = sb("primed", [1, 16])
        KON = sb("KON", [P, K_N])
        WR = sb("WR", [P, HALVES, R])
        WRr = sb("WRr", [R, C])
        WP = sb("WP", [R, C])
        WPr = sb("WPr", [P, HALVES, R])
        WQ = sb("WQ", [P, HALVES, HD])
        WK = sb("WK", [P, HALVES, HD])
        WV = sb("WV", [P, HALVES, HD])
        WQT = sb("WQT", [HD, C])
        WO = sb("WO", [HD, C])
        BO = sb("BO", [P, C])
        GW = sb("GW", [P, HALVES, NE])
        GB = sb("GB", [P, NE])
        B1R = sb("B1R", [NE * FB, P])
        B1T = sb("B1T", [P, NE * FB])
        ONES = sb("ONES", [P, P])
        ZEROS = sb("ZEROS", [P, C])
        CARRY = sb("CARRY", [P, NE])
        TAB = sb("TAB", [P, 3, 80])
        TABI = sb("TABI", [P, 3, 80], I32)
        NROW = sb("NROW", [P, NE])
        NROWI = sb("NROWI", [P, NE], I32)
        TCNT = sb("TCNT", [P, NE])
        TCUM = sb("TCUM", [P, NE])
        TMP8 = sb("TMP8", [P, NE, 16])
        TT8 = sb("TT8", [P, 80, NE])

        ctx_a = ExitStack()

        def sa(name, shape, dt=F32):
            return sb(name, shape, dt, ctx_a)

        XB = sa("XB", [P, 2, HALVES, GC])
        T = sa("T", [P, TILES, ROW])
        FT = sa("FT", [P, TILES + 4, R + 1])
        FN = sa("FN", [P, 2, GRP, R])
        FH = sa("FH", [P, FHW])
        MS = sa("MS", [P, 4, P])
        ER = sa("ER", [P, 8, EROW])
        CR = sa("CR", [P, 2, 2 * (R + 1)])
        CT = sa("CT", [R, 2, 2 * P])
        RD = sa("RD", [P, 2, 2])
        DEN = sa("DEN", [P, 2, 2])
        SQ = sa("SQ", [P, 8, R])
        SS = sa("SS", [P, TILES])
        SSM = sa("SSM", [P, TILES])
        NRM = sa("NRM", [P, TILES])
        RN = sa("RN", [P, TILES])
        ST = sa("ST", [P, TILES, 6])
        LN = sa("LN", [P, 6, TILES])
        NMR = sa("NMR", [P, TILES])
        XN = sa("XN", [P, 2, GRP, C])
        XT = sa("XT", [P, 2, HALVES, GC])
        KC = sa("KC", [HD, TILES * P])
        KE = sa("KE", [HD, 2, GC])
        KT = sa("KT", [P, 2, GC])
        KMX = sa("KMX", [HD, GROUPS])
        KNM = sa("KNM", [HD, 1])
        KSUM = sa("KSUM", [HD, GROUPS])
        KDEN = sa("KDEN", [HD, 1])
        KRD = sa("KRD", [HD, 1])
        GT = sa("GT", [P, HALVES, HD])
        CTM = sa("CTM", [HD, HD])
        M1 = sa("M1", [HD, C])
        AW = sa("AW", [P, HALVES, C])
        LG = sa("LG", [P, TILES, NE])
        LX = sa("LX", [P, TILES, NE])
        EX = sa("EX", [P, TILES, NE])
        OH = sa("OH", [P, TILES, NE])
        MX = sa("MX", [P, TILES])
        SC = sa("SC", [P, NE * (TILES + 1)])
        SO = sa("SO", [P, NE * (TILES + 1)])
        POS = sa("POS", [P, 4, TILES])
        PRBS = sa("PRBS", [P, TILES])
        SLI = sa("SLI", [P, TILES], I32)
        ctx_a.close()

        W1 = sb("W1", [P, 2, HALVES, FF])
        W2 = sb("W2", [P, 2, FB, C])
        B1 = sb("B1", [P, 2, FB])
        B2 = sb("B2", [P, 2, C])
        XR = sb("XR", [P, 2, GRP, ROW])
        HN = sb("HN", [P, 2, GRP, C])
        HT = sb("HT", [P, 2, HALVES, GC])
        HS = sb("HS", [P, 2, FB, GC])
        YA = sb("YA", [P, 2, C])
        YB = sb("YB", [P, 2, C])
        YF = sb("YF", [P, 2, C])
        YM = sb("YM", [P, 2, C], U32)
        YN = sb("YN", [P, 2, C], U32)
        YO = sb("YO", [P, 2, GRP, C])
        IDX = sb("IDX", [P, 2, GRP], I32)
        YG = sb("YG", [P, 2, GRP, C])
        OB = sb("OB", [P, 2, HALVES, GC])
        ZR = sb("ZR", [P, GRP * ROW])

        B = [ctx.enter_context(nc.psum_tensor(f"bank{i}", [P, 512], F32)) for i in range(8)]

        ident = KON[:, K_ID:K_ID + P]
        tri = KON[:, K_TRI:K_TRI + P]
        blockmask = KON[:, K_BLK:K_BLK + HD]
        npad = KON[:, K_NPAD:K_NPAD + TILES]
        w8 = KON[:, K_W8:K_W8 + NE]
        ebase = KON[:, K_EB:K_EB + NE]
        tok = KON[:, K_TOK:K_TOK + TILES]
        scanmask = KON[:, K_SCAN:K_SCAN + NE * 33]
        ttab = KON[:, K_TT:K_TT + 80]
        ecnt = KON[:, K_EC:K_EC + 16]

        CREDIT = 8
        STORES = 16
        carrier = sem("carrier")
        k_in = sem("k_in")
        x_in = [sem(f"x_in{q}") for q in range(2)]
        pe_prep, dve_prep, pool_prep = sem("pe_prep"), sem("dve_prep"), sem("pool_prep")
        pass_done = {e: sem(f"pass_done_{e}") for e in ("pe", "act", "dve", "pool")}
        pe_feat, act_xt, dve_feat = sem("pe_feat"), sem("act_xt"), sem("dve_feat")
        dve_ssm, act_nrm = sem("dve_ssm"), sem("act_nrm")
        dve_fn, pe_fh, act_fh = sem("dve_fn"), sem("pe_fh"), sem("act_fh")
        pool_ms, pe_gram, act_e, pool_mask = sem("pool_ms"), sem("pe_gram"), sem("act_e"), sem("pool_mask")
        pe_corr, dve_cr, pe_ct, act_ct, pe_proj, dve_t = (sem(n) for n in (
            "pe_corr", "dve_cr", "pe_ct", "act_ct", "pe_proj", "dve_t"))
        dve_var, act_std = sem("dve_var"), sem("act_std")
        xn_done, pe_xt, act_half, dve_half = sem("xn_done"), sem("pe_xt"), sem("act_half"), sem("dve_half")
        pe_k, act_kc, dve_kmx, dve_knm = sem("pe_k"), sem("act_kc"), sem("dve_kmx"), sem("dve_knm")
        act_ke, pe_kt, dve_kt, pe_g = sem("act_ke"), sem("pe_kt"), sem("dve_kt"), sem("pe_g")
        pe_fold, dve_fold = sem("pe_fold"), sem("dve_fold")
        pool_bias, pe_attn, dve_t2 = sem("pool_bias"), sem("pe_attn"), sem("dve_t2")
        pe_logit, dve_lx, act_ex, dve_oh, pe_count, dve_slot = (sem(n) for n in (
            "pe_logit", "dve_lx", "act_ex", "dve_oh", "pe_count", "dve_slot"))
        scat = [sem(f"scat{q}") for q in range(2)]
        tab_done, fill = sem("tab_done"), sem("fill")
        w_in = [sem(f"w_in{q}") for q in range(2)]
        r_in = [sem(f"r_in{q}") for q in range(2)]
        y_out = [sem(f"y_out{q}") for q in range(2)]
        t_out, g_in = sem("t_out"), [sem(f"g_in{q}") for q in range(2)]
        dve_hn, pe_ht, act_ht, dve_ht, pe_h, act_h, pe_y, dve_y = (sem(n) for n in (
            "dve_hn", "pe_ht", "act_ht", "dve_ht", "pe_h", "act_h", "pe_y", "dve_y"))
        pe_ot, act_ot, dve_ot = sem("pe_ot"), sem("act_ot"), sem("dve_ot")
        o_out = [sem(f"o_out{q}") for q in range(2)]

        pe_credit = (pe_feat, pe_fh, pe_gram, pe_corr, pe_ct, pe_proj, pe_xt, pe_k, pe_kt, pe_g, pe_attn,
                     pe_ht, pe_h, pe_y, pe_ot)
        act_credit = (act_xt, act_fh, act_e, act_ct, act_half, act_kc, act_ke, act_ht, act_h, act_ot)
        dve_credit = (dve_feat, dve_fn, dve_cr, dve_t, dve_half, dve_kmx, dve_kt, dve_t2, dve_hn, dve_ht,
                      dve_y, dve_ot)
        pool_credit = (pool_ms, pool_mask, pool_bias)

        def stand_alone(eng):
            eng.sem_inc(carrier, 1)

        def pass_starts(eng, me, n):
            for e, done in pass_done.items():
                if e != me:
                    eng.wait_ge(done, n + 1)
            stand_alone(eng)

        def pass_ends(eng, me):
            eng.drain().then_inc(pass_done[me], 1)

        def prepared(eng):
            eng.wait_ge(k_in, 16 * NCONST)
            eng.wait_ge(pe_prep, 1)
            eng.wait_ge(dve_prep, 2)
            eng.wait_ge(pool_prep, 1)

        x_v = x.rearrange("b (a c) h w -> b c a (h w)", a=HALVES)
        out_v = out.rearrange("b (a c) h w -> b c a (h w)", a=HALVES)
        w1_v = w1.rearrange("e (a c) f -> e c a f", a=HALVES)
        w2_v = w2.rearrange("e (k f) c -> e f k c", f=P)

        block = ctx.enter_context(nc.Block())
        NCONST = 14

        @block.sync
        def _(sp):
            qkv = w_qkv.rearrange("(a c) f -> c a f", a=HALVES)
            sp.dma_start(KON[:, :], konst).then_inc(k_in, 16)
            sp.dma_start(WRr[:, :], w_reduce).then_inc(k_in, 16)
            sp.dma_start(B1R[:, :], b1.rearrange("e (k f) -> (e k) f", f=P)).then_inc(k_in, 16)
            sp.dma_start(WPr[:, :, :], w_proj.rearrange("(a c) r -> c a r", a=HALVES)).then_inc(k_in, 16)
            sp.dma_start(WQ[:, :, :], qkv[:, :, 0:HD]).then_inc(k_in, 16)
            sp.dma_start(WK[:, :, :], qkv[:, :, HD:2 * HD]).then_inc(k_in, 16)
            sp.dma_start(WV[:, :, :], qkv[:, :, 2 * HD:3 * HD]).then_inc(k_in, 16)
            sp.dma_start(WO[:, :], w_out).then_inc(k_in, 16)
            sp.dma_start(BO[:, :], b_out.unsqueeze(0).to_broadcast([P, C])).then_inc(k_in, 16)
            sp.dma_start(GW[:, :, :], gate_w.rearrange("(a c) e -> c a e", a=HALVES)).then_inc(k_in, 16)
            sp.dma_start(GB[:, :], gate_b.unsqueeze(0).to_broadcast([P, NE])).then_inc(k_in, 16)
            sp.dma_start(FH[R:P, :].rearrange("p (n w) -> p n w", w=W),
                         band[:, 0:W].unsqueeze(1).to_broadcast([W, FHW // W, W])).then_inc(k_in, 16)
            for v in range(2):
                sp.dma_start(MS[R:P, :, v * W:(v + 1) * W],
                             band[:, W:].unsqueeze(1).to_broadcast([W, 4, W])).then_inc(k_in, 16)
            with sp.Fori(0, NB) as b:
                with sp.Fori(0, GROUPS // 2) as h:
                    for q in range(2):
                        sp.wait_ge(pe_feat, b * TILES + h * 2 * GRP + (q + 1) * GRP)
                        sp.dma_start(XB[:, q, :, :], x_v[bass.ds(b, 1), :, :, bass.ds(h * 2 * GC + q * GC, GC)]
                                     .rearrange("o c a n -> c (o a) n")).then_inc(x_in[q], 16)
                sp.wait_ge(dve_slot, b + 1)
                sp.dma_start(toks[bass.ds(b * TILES * P, TILES * P), :].rearrange("(i p) c -> p i c", p=P),
                             T[:, :, 0:C]).then_inc(t_out, 16)
            sp.wait_ge(tab_done, 1)
            for e in range(NE):
                n = sp.value_load(NROWI[0:1, e:e + 1], min_val=0, max_val=s["zero"])
                sp.dma_start(rows[bass.ds(n, STILE), :].rearrange("(p k) c -> p (k c)", p=P), ZR[:, :]).then_inc(fill, 16)
            sp.dma_start(rows[s["zero"]:s["zero"] + STILE, :].rearrange("(p k) c -> p (k c)", p=P), ZR[:, :]).then_inc(fill, 16)
            sp.wait_ge(fill, 16 * (NE + 1))

            def load(t, q):
                first = t if isinstance(t, int) else None
                e = sp.value_load(TABI[0:1, 0, bass.ds(t, 1)], min_val=0, max_val=NE - 1)
                r = sp.value_load(TABI[0:1, 1, bass.ds(t, 1)], min_val=0, max_val=s["zero"])
                if first is None:
                    sp.wait_ge(dve_y, CREDIT + (t - 1) * GRP)
                sp.dma_start(XR[:, q, :, :], rows[bass.ds(r, STILE), :].rearrange("(p k) c -> p k c", p=P)).then_inc(r_in[q], 16)
                sp.dma_start(W1[:, q, :, :], w1_v[bass.ds(e, 1), :, :, :].rearrange("o c a f -> c (o a) f")).then_inc(w_in[q], 16)
                sp.dma_start(W2[:, q, :, :], w2_v[bass.ds(e, 1), :, :, :].rearrange("o f k c -> f (o k) c")).then_inc(w_in[q], 16)
                sp.dma_start(B1[:, q, :], B1T[:, bass.ds(e * FB, FB)]).then_inc(w_in[q], 16)
                sp.dma_start(B2[:, q, :], b2[bass.ds(e, 1), :].to_broadcast([P, C])).then_inc(w_in[q], 16)

            load(0, 0)
            load(1, 1)
            with sp.Fori(0, NT // 2 - 1) as h:
                for q in range(2):
                    load(2 * h + q + 2, q)
            for q in range(2):
                sp.wait_ge(y_out[q], STORES + 16 * GRP * NT // 2)
            with sp.Fori(0, NB * GROUPS // 2) as h:
                for q in range(2):
                    sp.wait_ge(pe_ot, CREDIT + 2 * h + q - 1)
                    sp.dma_start(YG[:, q, :, :], toks[bass.ds(h * 2 * GC + q * GC, GC), :]
                                 .rearrange("(k p) c -> p k c", p=P)).then_inc(g_in[q], 16)

        @block.tensor
        def _(pe):
            mm, tr = nc.tensor.matmul, nc.tensor.transpose
            for c in pe_credit:
                pe.sem_inc(c, CREDIT)
            pe.sem_inc(pass_done["pe"], 1)
            pe.wait_ge(k_in, 16 * NCONST)
            for a in range(HALVES):
                tr(B[0][:, a * R:(a + 1) * R], WRr[:, a * P:(a + 1) * P], ident[0:R, 0:R])
                tr(B[1][0:R, a * P:(a + 1) * P], WPr[:, a, :], ident)
                tr(B[2][:, a * P:(a + 1) * P], WQ[:, a, :], ident)
            tr(B[3][:, 0:NE * FB], B1R[:, :], ident[0:NE * FB, 0:NE * FB])
            pe.drain().then_inc(pe_prep, 1)
            prepared(pe)

            def feature_pass(b):
                with pe.Fori(0, GROUPS // 2) as h:
                    for k in range(2 * GRP):
                        q, sl = k // GRP, bass.ts(k % GRP, P)
                        if k % GRP == 0:
                            pe.wait_ge(x_in[q], 16 * (b * (GROUPS // 2) + h + 1))
                        n = b * TILES + h * 2 * GRP + k
                        pe.wait_ge(act_xt, CREDIT + n - 3)
                        pe.wait_ge(dve_feat, CREDIT + n - 3)
                        bank = B[k % 4]
                        for a in range(HALVES):
                            mm(B[4 + k % 4][:, 0:R], XB[:, q, a, sl], WR[:, a, :], start=a == 0, stop=a == 1)
                        for a in range(HALVES):
                            last = tr(bank[:, bass.ts(a, P)], XB[:, q, a, sl], ident)
                        last.then_inc(pe_feat, 1)

            def map_pass(b):
                with pe.Fori(0, GROUPS // 2) as h:
                    for q in range(2):
                        n = b * GROUPS + 2 * h + q
                        pe.wait_ge(dve_fn, CREDIT + n + 1)
                        pe.wait_ge(act_fh, CREDIT + n - 1)
                        stand_alone(pe)
                        for k in range(GRP):
                            last = tr(B[4 + q][0:R, bass.ts(k, P)], FN[:, q, k, :], ident)
                        last.then_inc(pe_fh, 1)

            def window_pass(b):
                nm, npair = TILES + 4, PAIRS

                def gram(m, k):
                    n = b * nm + m
                    pe.wait_ge(pool_ms, CREDIT + n + 1)
                    pe.wait_ge(act_e, CREDIT + n - 1)
                    mm(B[k % 2][:, :], MS[:, k % 4, :], FH[:, bass.ds(m * P, GC)],
                       start=True, stop=True).then_inc(pe_gram, 1)

                for m in range(4):
                    gram(m, m)
                with pe.Fori(0, PAIRS // 4) as h:
                    for j in range(4):
                        p = 4 * h + j
                        n = b * npair + p
                        gram(2 * p + 4, 2 * j + 4)
                        pe.wait_ge(pool_mask, CREDIT + b * nm + 2 * p + 4)
                        pe.wait_ge(dve_cr, CREDIT + n - 1)
                        for t in range(2):
                            for d in range(-2, 3):
                                last = mm(B[2 + j % 2][:, t * (R + 1):(t + 1) * (R + 1)],
                                          ER[:, (2 * j + t + d) % 8, 256 - P * d:256 - P * d + P],
                                          FT[:, bass.ds(2 * p + t + d + 2, 1), :].rearrange("p o c -> p (o c)"),
                                          start=d == -2, stop=d == 2)
                        last.then_inc(pe_corr, 1)
                        gram(2 * p + 5, 2 * j + 5)
                        pe.wait_ge(dve_cr, CREDIT + n + 1)
                        pe.wait_ge(act_ct, CREDIT + n)
                        stand_alone(pe)
                        for t in range(2):
                            last = tr(B[4][0:R, bass.ts(t, P)], CR[:, j % 2, t * (R + 1):t * (R + 1) + R], ident)
                        last.then_inc(pe_ct, 1)
                        pe.wait_ge(act_ct, CREDIT + n + 1)
                        pe.wait_ge(dve_t, CREDIT + n - 1)
                        for t in range(2):
                            last = mm(B[5 + j % 2][:, bass.ts(t, C)], CT[:, j % 2, bass.ts(t, P)], WP[:, :],
                                      start=True, stop=True)
                        last.then_inc(pe_proj, 1)

            def normed_to_channels(n, q):
                for k in range(GRP):
                    pe.wait_ge(xn_done, n * GRP + k + 1)
                    if k == 0:
                        pe.wait_ge(act_half, CREDIT + n - 1)
                        pe.wait_ge(dve_half, CREDIT + n - 1)
                    for a in range(HALVES):
                        last = tr(B[2 * q + a][:, bass.ts(k, P)], XN[:, q, k, bass.ts(a, P)], ident)
                last.then_inc(pe_xt, 1)

            def channels_ready(n):
                pe.wait_ge(act_half, CREDIT + n + 1)
                pe.wait_ge(dve_half, CREDIT + n + 1)

            def key_pass(b):
                with pe.Fori(0, GROUPS // 2) as h:
                    for q in range(2):
                        normed_to_channels(b * 3 * GROUPS + 2 * h + q, q)
                    for q in range(2):
                        channels_ready(b * 3 * GROUPS + 2 * h + q)
                        n = b * GROUPS + 2 * h + q
                        pe.wait_ge(act_kc, CREDIT + n - 1)
                        for a in range(HALVES):
                            last = mm(B[4 + q][:, :], WK[:, a, :], XT[:, q, a, :], start=a == 0, stop=a == 1)
                        last.then_inc(pe_k, 1)

            def context_pass(b):
                mm(B[6][:, 0:HALVES * HD], ZEROS[:, 0:P], ZEROS[:, :], start=True, stop=False, skip_group_check=True)
                with pe.Fori(0, GROUPS // 2) as h:
                    for q in range(2):
                        n = b * GROUPS + 2 * h + q
                        pe.wait_ge(act_ke, CREDIT + n + 1)
                        pe.wait_ge(dve_kt, CREDIT + n - 1)
                        for k in range(GRP):
                            last = tr(B[q][:, bass.ts(k, P)], KE[:, q, bass.ts(k, P)], ident)
                        last.then_inc(pe_kt, 1)
                    for q in range(2):
                        n = b * GROUPS + 2 * h + q
                        pe.wait_ge(dve_kt, CREDIT + n + 1)
                        for k in range(GRP):
                            for a in range(HALVES):
                                last = mm(B[6][:, bass.ts(a, HD)], XN[:, q, k, bass.ts(a, P)], KT[:, q, bass.ts(k, P)],
                                          start=False, stop=False, skip_group_check=True)
                        last.then_inc(pe_g, 1)
                pe.wait_ge(dve_fold, 3 * b + 1)
                for a in range(HALVES):
                    last = mm(B[0][:, 0:HD], WV[:, a, :], GT[:, a, :], start=a == 0, stop=a == 1)
                last.then_inc(pe_fold, 1)
                pe.wait_ge(dve_fold, 3 * b + 2)
                mm(B[1][:, 0:C], CTM[:, :], WO[:, :], start=True, stop=True).then_inc(pe_fold, 1)
                pe.wait_ge(dve_fold, 3 * b + 3)
                for a in range(HALVES):
                    last = mm(B[2][:, bass.ts(a, C)], WQT[:, bass.ts(a, P)], M1[:, :], start=True, stop=True)
                last.then_inc(pe_fold, 1)

            def attention_pass(b):
                with pe.Fori(0, GROUPS // 2) as h:
                    for q in range(2):
                        normed_to_channels(b * 3 * GROUPS + GROUPS + 2 * h + q, q)
                    for q in range(2):
                        channels_ready(b * 3 * GROUPS + GROUPS + 2 * h + q)
                        for k in range(GRP):
                            if k % 2 == 0:
                                pe.wait_ge(dve_t2, CREDIT + b * TILES + h * 2 * GRP + q * GRP + k - 6)
                            for a in range(HALVES):
                                last = mm(B[4 + 2 * q + k // 2][:, bass.ts(k % 2, C)], XT[:, q, a, bass.ts(k, P)],
                                          AW[:, a, :], start=a == 0, stop=a == 1)
                            last.then_inc(pe_attn, 1)

            def routing_pass(b):
                with pe.Fori(0, GROUPS // 2) as h:
                    for q in range(2):
                        normed_to_channels(b * 3 * GROUPS + 2 * GROUPS + 2 * h + q, q)
                    for q in range(2):
                        channels_ready(b * 3 * GROUPS + 2 * GROUPS + 2 * h + q)
                        for k in range(GRP):
                            i = h * 2 * GRP + q * GRP + k
                            for a in range(HALVES):
                                last = mm(B[4][:, bass.ds(i * NE, NE)], XT[:, q, a, bass.ts(k, P)], GW[:, a, :],
                                          start=a == 0, stop=a == 1)
                        last.then_inc(pe_logit, 1)
                pe.wait_ge(dve_oh, b + 1)
                oh = OH[:, :, :].rearrange("p i e -> p (i e)")
                mm(B[5][:, 0:TILES * NE], tri, oh, start=True, stop=True)
                mm(B[6][:, 0:TILES * NE], ONES[:, :], oh, start=True, stop=True).then_inc(pe_count, 1)

            with pe.Fori(0, NB) as b:
                for n, stage in enumerate((feature_pass, map_pass, window_pass, key_pass, context_pass,
                                           attention_pass, routing_pass)):
                    pass_starts(pe, "pe", b * NPASS + n)
                    stage(b)
                    pass_ends(pe, "pe")

            with pe.Fori(0, NT // 2) as h:
                for q in range(2):
                    t = 2 * h + q
                    for k in range(GRP):
                        pe.wait_ge(dve_hn, CREDIT + t * GRP + k + 1)
                        if k == 0:
                            pe.wait_ge(act_ht, CREDIT + t)
                            pe.wait_ge(dve_ht, CREDIT + t)
                        for a in range(HALVES):
                            last = tr(B[a][:, bass.ts(k, P)], HN[:, q, k, bass.ts(a, P)], ident)
                    last.then_inc(pe_ht, 1)
                    pe.wait_ge(w_in[q], 64 * (h + 1))
                    pe.wait_ge(act_ht, CREDIT + t + 1)
                    pe.wait_ge(dve_ht, CREDIT + t + 1)
                    for f in range(FB):
                        pe.wait_ge(act_h, CREDIT + t * FB + f - 3)
                        for a in range(HALVES):
                            last = mm(B[(2, 3, 4, 7)[f % 4]][:, :], W1[:, q, a, bass.ts(f, P)], HT[:, q, a, :],
                                      start=a == 0, stop=a == 1)
                        last.then_inc(pe_h, 1)
                    for k in range(GRP):
                        pe.wait_ge(act_h, CREDIT + (t + 1) * FB)
                        pe.wait_ge(dve_y, CREDIT + t * GRP + k - 1)
                        for f in range(FB):
                            last = mm(B[5 + k % 2][:, 0:C], HS[:, q, f, bass.ts(k, P)], W2[:, q, f, :],
                                      start=f == 0, stop=f == FB - 1)
                        last.then_inc(pe_y, 1)

            with pe.Fori(0, NB * GROUPS // 2) as h:
                for q in range(2):
                    n = 2 * h + q
                    pe.wait_ge(act_ot, CREDIT + n - 1)
                    pe.wait_ge(dve_ot, CREDIT + n - 1)
                    pe.wait_ge(g_in[q], 16 * (h + 1))
                    for k in range(GRP):
                        for a in range(HALVES):
                            last = tr(B[2 * q + a][:, bass.ts(k, P)], YG[:, q, k, bass.ts(a, P)], ident)
                    last.then_inc(pe_ot, 1)

        @block.scalar
        def _(act):
            A = nc.scalar.activation
            for c in act_credit:
                act.sem_inc(c, CREDIT)
            act.sem_inc(pass_done["act"], 1)
            prepared(act)

            def feature_pass(b):
                with act.Fori(0, GROUPS // 2) as h:
                    for k in range(2 * GRP):
                        i = h * 2 * GRP + k
                        act.wait_ge(pe_feat, CREDIT + b * TILES + i + 1)
                        A(T[:, bass.ds(i, 1), 0:C].rearrange("p o c -> p (o c)"), B[k % 4][:, 0:C], ACT.Copy)
                        act.wait_ge(dve_feat, CREDIT + b * TILES + i + 1)
                        act.wait_ge(act_xt, b * TILES + i + 1)
                        A(SQ[:, k, :], FT[:, bass.ds(i + 2, 1), 0:R].rearrange("p o c -> p (o c)"), ACT.Square, accum_out=SS[:, bass.ds(i, 1)]).then_inc(act_xt, 1)
                act.wait_ge(dve_ssm, b + 1)
                A(NRM[:, :], SSM[:, :], ACT.Sqrt).then_inc(act_nrm, 1)

            def map_pass(b):
                with act.Fori(0, GROUPS // 2) as h:
                    for q in range(2):
                        act.wait_ge(pe_fh, CREDIT + b * GROUPS + 2 * h + q + 1)
                        A(FH[0:R, bass.ds(h * 2 * GC + q * GC + HALO, GC)], B[4 + q][0:R, :], ACT.Copy).then_inc(act_fh, 1)

            def window_pass(b):
                nm = TILES + 4

                def weights(m, k):
                    act.wait_ge(pe_gram, CREDIT + b * nm + m + 1)
                    A(ER[:, k % 8, W:W + GC], B[k % 2][:, :], ACT.Exp).then_inc(act_e, 1)

                for m in range(4):
                    weights(m, m)
                with act.Fori(0, PAIRS // 4) as h:
                    for j in range(4):
                        p = 4 * h + j
                        act.wait_ge(pe_corr, CREDIT + b * PAIRS + p)
                        weights(2 * p + 4, 2 * j + 4)
                        weights(2 * p + 5, 2 * j + 5)
                        act.wait_ge(pe_ct, CREDIT + b * PAIRS + p + 1)
                        act.wait_ge(pe_proj, CREDIT + b * PAIRS + p - 1)
                        A(CT[:, j % 2, :], B[4][0:R, 0:2 * P], ACT.Copy).then_inc(act_ct, 1)
                act.wait_ge(dve_var, 2 * b + 1)
                A(LN[:, 4, :], LN[:, 3, :], ACT.Sqrt).then_inc(act_std, 1)

            def half(n, q):
                act.wait_ge(pe_xt, CREDIT + n + 1)
                A(XT[:, q, 1, :], B[2 * q + 1][:, :], ACT.Copy).then_inc(act_half, 1)

            def key_pass(b):
                with act.Fori(0, GROUPS // 2) as h:
                    for q in range(2):
                        half(b * 3 * GROUPS + 2 * h + q, q)
                    for q in range(2):
                        act.wait_ge(pe_k, CREDIT + b * GROUPS + 2 * h + q + 1)
                        A(KC[:, bass.ds(h * 2 * GC + q * GC, GC)], B[4 + q][:, :], ACT.Copy).then_inc(act_kc, 1)

            def context_pass(b):
                act.wait_ge(dve_knm, b + 1)
                stand_alone(act)
                with act.Fori(0, GROUPS // 2) as h:
                    for q in range(2):
                        n = b * GROUPS + 2 * h + q
                        act.wait_ge(pe_kt, CREDIT + n - 1)
                        A(KE[:, q, :], KC[:, bass.ds(h * 2 * GC + q * GC, GC)], ACT.Exp, bias=KNM[:, :],
                          accum_out=KSUM[:, bass.ds(2 * h + q, 1)]).then_inc(act_ke, 1)

            def attention_pass(b):
                with act.Fori(0, GROUPS // 2) as h:
                    for q in range(2):
                        n = b * 3 * GROUPS + GROUPS + 2 * h + q
                        act.wait_ge(pe_xt, CREDIT + n - 1)
                        for k in range(GRP):
                            i = h * 2 * GRP + q * GRP + k
                            A(XN[:, q, k, :], T[:, bass.ds(i, 1), 0:C].rearrange("p o c -> p (o c)"), ACT.Identity,
                              bias=NMR[:, bass.ds(i, 1)], scale=LN[:, 5, bass.ds(i, 1)]).then_inc(xn_done, 1)
                    for q in range(2):
                        half(b * 3 * GROUPS + GROUPS + 2 * h + q, q)
                act.wait_ge(dve_var, 2 * b + 2)
                A(LN[:, 4, :], LN[:, 3, :], ACT.Sqrt).then_inc(act_std, 1)

            def routing_pass(b):
                with act.Fori(0, GROUPS // 2) as h:
                    for q in range(2):
                        half(b * 3 * GROUPS + 2 * GROUPS + 2 * h + q, q)
                act.wait_ge(dve_lx, b + 1)
                A(EX[:, :, :].rearrange("p i e -> p (i e)"), LX[:, :, :].rearrange("p i e -> p (i e)"),
                  ACT.Exp).then_inc(act_ex, 1)

            with act.Fori(0, NB) as b:
                for n, stage in enumerate((feature_pass, map_pass, window_pass, key_pass, context_pass,
                                           attention_pass, routing_pass)):
                    pass_starts(act, "act", b * NPASS + n)
                    stage(b)
                    pass_ends(act, "act")

            with act.Fori(0, NT // 2) as h:
                for q in range(2):
                    t = 2 * h + q
                    act.wait_ge(pe_ht, CREDIT + t + 1)
                    A(HT[:, q, 1, :], B[1][:, :], ACT.Copy).then_inc(act_ht, 1)
                    act.wait_ge(w_in[q], 64 * (h + 1))
                    act.wait_ge(pe_y, CREDIT + (t - 1) * GRP)
                    for f in range(FB):
                        act.wait_ge(pe_h, CREDIT + t * FB + f + 1)
                        A(HS[:, q, f, :], B[(2, 3, 4, 7)[f % 4]][:, :], ACT.Relu, bias=B1[:, q, f:f + 1]).then_inc(act_h, 1)

            with act.Fori(0, NB * GROUPS // 2) as h:
                for q in range(2):
                    act.wait_ge(pe_ot, CREDIT + 2 * h + q + 1)
                    act.wait_ge(o_out[q], STORES + 16 * h)
                    A(OB[:, q, 1, :], B[2 * q + 1][:, :], ACT.Copy).then_inc(act_ot, 1)

        @block.vector
        def _(dve):
            V = nc.vector
            for c in dve_credit:
                dve.sem_inc(c, CREDIT)
            dve.sem_inc(pass_done["dve"], 1)
            V.memset(ONES[:, :], 1.0)
            V.memset(ZEROS[:, :], 0.0)
            V.memset(FT[:, :, :], 0.0)
            V.memset(FH[0:R, :], 0.0)
            V.memset(ER[:, :, :], 0.0)
            V.memset(CARRY[:, :], 0.0)
            V.memset(T[:, :, C:ROW], 0.0)
            dve.drain()
            V.memset(FT[:, 2:TILES + 2, R:R + 1], 1.0)
            dve.drain().then_inc(dve_prep, 1)
            dve.wait_ge(k_in, 16 * NCONST)
            dve.wait_ge(pe_prep, 1)
            V.tensor_copy(WR[:, :, :].rearrange("p a r -> p (a r)"), B[0][:, 0:HALVES * R])
            V.tensor_copy(WP[:, :], B[1][0:R, 0:C])
            V.tensor_copy(WQT[:, :], B[2][:, 0:C])
            V.tensor_copy(B1T[:, :], B[3][:, 0:NE * FB])
            dve.drain().then_inc(dve_prep, 1)
            prepared(dve)

            def tile_of(i):
                return T[:, bass.ds(i, 1), 0:C].rearrange("p o c -> p (o c)")

            def feature_pass(b):
                with dve.Fori(0, GROUPS // 2) as h:
                    for k in range(2 * GRP):
                        i = h * 2 * GRP + k
                        dve.wait_ge(pe_feat, CREDIT + b * TILES + i + 1)
                        V.tensor_copy(FT[:, bass.ds(i + 2, 1), 0:R].rearrange("p o c -> p (o c)"),
                                      B[4 + k % 4][:, 0:R]).then_inc(dve_feat, 1)
                dve.wait_ge(act_xt, CREDIT + (b + 1) * TILES)
                V.tensor_scalar_max(SSM[:, :], SS[:, :], 1e-16).then_inc(dve_ssm, 1)
                dve.wait_ge(act_nrm, b + 1)
                V.reciprocal(RN[:, :], NRM[:, :])
                dve.drain()

            def map_pass(b):
                with dve.Fori(0, GROUPS // 2) as h:
                    for q in range(2):
                        dve.wait_ge(pe_fh, CREDIT + b * GROUPS + 2 * h + q - 1)
                        i = h * 2 * GRP + q * GRP
                        V.tensor_tensor(FN[:, q, :, :], FT[:, bass.ds(i + 2, GRP), 0:R],
                                        RN[:, bass.ds(i, GRP)].unsqueeze(2).to_broadcast([P, GRP, R]),
                                        ALU.mult).then_inc(dve_fn, 1)

            def statistics(b, which):
                eps = 1e-5
                dve.drain()
                V.tensor_tensor(LN[:, 0, :], ST[:, :, 1], ST[:, :, 4], ALU.add)
                V.tensor_tensor(LN[:, 1, :], ST[:, :, 1], ST[:, :, 4], ALU.subtract)
                V.tensor_tensor(LN[:, 2, :], ST[:, :, 2], ST[:, :, 5], ALU.add)
                dve.drain()
                V.scalar_tensor_tensor(LN[:, 1, :], LN[:, 1, :], 0.25, LN[:, 1, :], ALU.mult, ALU.mult)
                V.tensor_scalar(LN[:, 2, :], LN[:, 2, :], 1.0 / C, eps, ALU.mult, ALU.add)
                V.tensor_scalar_mul(LN[:, 0, :], LN[:, 0, :], 0.5)
                dve.drain()
                V.tensor_tensor(LN[:, 3, :], LN[:, 1, :], LN[:, 2, :], ALU.add).then_inc(dve_var, 1)
                dve.wait_ge(act_std, 2 * b + which + 1)
                V.reciprocal(LN[:, 5, :], LN[:, 4, :])
                dve.drain()
                V.scalar_tensor_tensor(NMR[:, :], LN[:, 0, :], -1.0, LN[:, 5, :], ALU.mult, ALU.mult)
                dve.drain()

            def window_pass(b):
                with dve.Fori(0, PAIRS // 4) as h:
                    for j in range(4):
                        p = 4 * h + j
                        n = b * PAIRS + p
                        dve.wait_ge(pe_corr, CREDIT + n + 1)
                        dve.wait_ge(pe_ct, CREDIT + n - 1)
                        V.tensor_copy(CR[:, j % 2, :], B[2 + j % 2][:, 0:2 * (R + 1)]).then_inc(dve_cr, 1)
                        dve.drain()
                        V.tensor_tensor(DEN[:, j % 2, :],
                                        CR[:, j % 2, :].rearrange("p (t c) -> p t c", t=2)[:, :, R],
                                        npad[:, bass.ds(2 * p, 2)], ALU.add)
                        dve.drain()
                        V.reciprocal(RD[:, j % 2, :], DEN[:, j % 2, :])
                        dve.drain()
                        dve.wait_ge(pe_proj, CREDIT + n + 1)
                        for t in range(2):
                            i = 2 * p + t
                            V.scalar_tensor_tensor(tile_of(i), B[5 + j % 2][:, bass.ts(t, C)], RD[:, j % 2, t:t + 1],
                                                   tile_of(i), ALU.mult, ALU.add)
                        dve.drain().then_inc(dve_t, 1)
                        for t in range(2):
                            i = 2 * p + t
                            V.bn_stats(ST[:, bass.ds(i, 1), :].rearrange("p o c -> p (o c)"), tile_of(i))
                statistics(b, 0)

            def half(n, q):
                dve.wait_ge(pe_xt, CREDIT + n + 1)
                V.tensor_copy(XT[:, q, 0, :], B[2 * q][:, :]).then_inc(dve_half, 1)

            def norm(h, q, n, counted):
                for k in range(GRP):
                    i = h * 2 * GRP + q * GRP + k
                    x_n = V.tensor_scalar(XN[:, q, k, :], tile_of(i), LN[:, 0, bass.ds(i, 1)], LN[:, 5, bass.ds(i, 1)],
                                          ALU.subtract, ALU.mult)
                    if counted:
                        x_n.then_inc(xn_done, 1)

            def key_pass(b):
                with dve.Fori(0, GROUPS // 2) as h:
                    for q in range(2):
                        n = b * 3 * GROUPS + 2 * h + q
                        dve.wait_ge(pe_xt, CREDIT + n - 1)
                        norm(h, q, n, True)
                    for q in range(2):
                        half(b * 3 * GROUPS + 2 * h + q, q)
                    for q in range(2):
                        dve.wait_ge(act_kc, CREDIT + b * GROUPS + 2 * h + q + 1)
                        V.reduce_max(KMX[:, bass.ds(2 * h + q, 1)], KC[:, bass.ds(h * 2 * GC + q * GC, GC)], AX).then_inc(dve_kmx, 1)
                dve.drain()
                V.reduce_max(KNM[:, :], KMX[:, :], AX)
                dve.drain()
                V.tensor_scalar_mul(KNM[:, :], KNM[:, :], -1.0).then_inc(dve_knm, 1)

            def context_pass(b):
                with dve.Fori(0, GROUPS // 2) as h:
                    for q in range(2):
                        n = b * GROUPS + 2 * h + q
                        dve.wait_ge(pe_g, CREDIT + n - 1)
                        norm(h, q, n, False)
                        dve.wait_ge(pe_kt, CREDIT + n + 1)
                        V.tensor_copy(KT[:, q, :], B[q][:, :])
                        dve.drain().then_inc(dve_kt, 1)
                dve.wait_ge(pe_g, CREDIT + (b + 1) * GROUPS)
                V.tensor_copy(GT[:, :, :].rearrange("p a d -> p (a d)"), B[6][:, 0:HALVES * HD]).then_inc(dve_fold, 1)
                dve.wait_ge(act_ke, CREDIT + (b + 1) * GROUPS)
                V.reduce_sum(KDEN[:, :], KSUM[:, :], AX)
                dve.drain()
                V.reciprocal(KRD[:, :], KDEN[:, :])
                dve.wait_ge(pe_fold, 3 * b + 1)
                V.tensor_tensor(CTM[:, :], B[0][:, 0:HD], blockmask, ALU.mult).then_inc(dve_fold, 1)
                dve.drain()
                dve.wait_ge(pe_fold, 3 * b + 2)
                V.tensor_scalar_mul(M1[:, :], B[1][:, 0:C], KRD[:, :]).then_inc(dve_fold, 1)
                dve.wait_ge(pe_fold, 3 * b + 3)
                V.tensor_copy(AW[:, :, :].rearrange("p a c -> p (a c)"), B[2][:, :])

            def attention_pass(b):
                with dve.Fori(0, GROUPS // 2) as h:
                    for q in range(2):
                        half(b * 3 * GROUPS + GROUPS + 2 * h + q, q)
                    for q in range(2):
                        for k in range(GRP):
                            i = h * 2 * GRP + q * GRP + k
                            if k % 2 == 0:
                                dve.wait_ge(pe_attn, CREDIT + b * TILES + i + 2)
                            dve.wait_ge(pool_bias, CREDIT + b * TILES + i + 1)
                            V.tensor_tensor(tile_of(i), B[4 + 2 * q + k // 2][:, bass.ts(k % 2, C)], tile_of(i),
                                            ALU.add).then_inc(dve_t2, 1)
                            if k % 2 == 1:
                                dve.drain()
                                for j in (i - 1, i):
                                    V.bn_stats(ST[:, bass.ds(j, 1), :].rearrange("p o c -> p (o c)"), tile_of(j))
                statistics(b, 1)

            def routing_pass(b):
                with dve.Fori(0, GROUPS // 2) as h:
                    for q in range(2):
                        n = b * 3 * GROUPS + 2 * GROUPS + 2 * h + q
                        dve.wait_ge(pe_xt, CREDIT + n - 1)
                        norm(h, q, n, True)
                    for q in range(2):
                        half(b * 3 * GROUPS + 2 * GROUPS + 2 * h + q, q)
                dve.wait_ge(pe_logit, (b + 1) * GROUPS)
                wide = [P, TILES, NE]
                V.tensor_tensor(LG[:, :, :], B[4][:, 0:TILES * NE].rearrange("p (i e) -> p i e", e=NE),
                                GB[:, :].unsqueeze(1).to_broadcast(wide), ALU.add)
                dve.drain()
                V.reduce_max(MX[:, :], LG[:, :, :], AX)
                dve.drain()
                top = MX[:, :].unsqueeze(2).to_broadcast(wide)
                V.tensor_tensor(LX[:, :, :], LG[:, :, :], top, ALU.subtract).then_inc(dve_lx, 1)
                V.tensor_tensor(OH[:, :, :], LG[:, :, :], top, ALU.is_ge)
                dve.drain()
                V.tensor_tensor(LG[:, :, :], OH[:, :, :], w8.unsqueeze(1).to_broadcast(wide), ALU.mult)
                dve.drain()
                V.reduce_max(MX[:, :], LG[:, :, :], AX)
                dve.drain()
                V.tensor_tensor(OH[:, :, :], LG[:, :, :], top, ALU.is_equal).then_inc(dve_oh, 1)
                dve.wait_ge(act_ex, b + 1)
                V.reduce_sum(PRBS[:, :], EX[:, :, :], AX)
                dve.drain()
                V.reciprocal(T[:, :, PRB], PRBS[:, :])
                V.tensor_copy(T[:, :, MEAN], LN[:, 0, :])
                V.tensor_copy(T[:, :, RSTD], LN[:, 5, :])
                sc = SC[:, :].rearrange("p (e j) -> p e j", e=NE)
                so = SO[:, :].rearrange("p (e j) -> p e j", e=NE)
                V.tensor_copy(sc[:, :, 0], CARRY[:, :])
                dve.wait_ge(pe_count, b + 1)
                V.tensor_copy(sc[:, :, 1:TILES + 1], B[6][:, 0:TILES * NE].rearrange("p (i e) -> p e i", e=NE))
                dve.drain()
                V.tensor_tensor_scan(SO[:, :], scanmask, SC[:, :], 0.0, ALU.mult, ALU.add)
                dve.drain()
                V.tensor_copy(CARRY[:, :], so[:, :, TILES])
                V.tensor_tensor(LX[:, :, :], B[5][:, 0:TILES * NE].rearrange("p (i e) -> p i e", e=NE),
                                so[:, :, 0:TILES].rearrange("p e i -> p i e"), ALU.add)
                dve.drain()
                V.tensor_tensor(LX[:, :, :], LX[:, :, :], OH[:, :, :], ALU.mult)
                V.tensor_tensor(LG[:, :, :], OH[:, :, :], ebase.unsqueeze(1).to_broadcast(wide), ALU.mult)
                dve.drain()
                V.reduce_sum(POS[:, 0, :], LX[:, :, :], AX)
                V.reduce_sum(POS[:, 1, :], LG[:, :, :], AX)
                dve.drain()
                V.tensor_scalar(POS[:, 2, :], POS[:, 0, :], float(CAP) + 0.5, None, ALU.is_lt)
                V.scalar_tensor_tensor(POS[:, 3, :], POS[:, 0, :], -1.0, POS[:, 1, :], ALU.add, ALU.add)
                dve.drain()
                V.tensor_scalar_add(POS[:, 3, :], POS[:, 3, :], -NOWHERE)
                dve.drain()
                V.tensor_tensor(POS[:, 3, :], POS[:, 3, :], POS[:, 2, :], ALU.mult)
                dve.drain()
                V.tensor_scalar_add(POS[:, 3, :], POS[:, 3, :], NOWHERE)
                dve.drain()
                V.tensor_copy(SLI[:, :], POS[:, 3, :])
                V.tensor_copy(T[:, :, TOK], tok)
                dve.drain()
                V.tensor_scalar_add(tok, tok, float(TILES * P))
                dve.drain().then_inc(dve_slot, 1)

            with dve.Fori(0, NB) as b:
                for n, stage in enumerate((feature_pass, map_pass, window_pass, key_pass, context_pass,
                                           attention_pass, routing_pass)):
                    pass_starts(dve, "dve", b * NPASS + n)
                    stage(b)
                    pass_ends(dve, "dve")

            V.tensor_scalar_min(NROW[:, :], CARRY[:, :], float(CAP))
            dve.drain()
            V.tensor_tensor(TMP8[:, :, :], NROW[:, :].unsqueeze(2).to_broadcast([P, NE, 16]),
                            ecnt.unsqueeze(1).to_broadcast([P, NE, 16]), ALU.is_gt)
            dve.drain()
            V.reduce_sum(TCNT[:, :], TMP8[:, :, :], AX)
            V.tensor_tensor(NROW[:, :], NROW[:, :], ebase, ALU.add)
            dve.drain()
            V.tensor_copy(NROWI[:, :], NROW[:, :])
            V.tensor_tensor_scan(TCUM[:, :], ONES[:, 0:NE], TCNT[:, :], 0.0, ALU.mult, ALU.add)
            dve.drain()
            V.tensor_tensor(TT8[:, :, :], ttab.unsqueeze(2).to_broadcast([P, 80, NE]),
                            TCUM[:, :].unsqueeze(1).to_broadcast([P, 80, NE]), ALU.is_ge)
            V.tensor_scalar(TCNT[:, :], TCNT[:, :], -float(STILE), float(CP), ALU.mult, ALU.add)
            dve.drain()
            V.reduce_sum(TAB[:, 0, :], TT8[:, :, :], AX)
            V.tensor_copy(TAB[:, 1, :], TT8[:, :, NE - 1])
            dve.drain()
            V.tensor_tensor(TT8[:, :, :], TT8[:, :, :], TCNT[:, :].unsqueeze(1).to_broadcast([P, 80, NE]), ALU.mult)
            dve.drain()
            V.reduce_sum(TAB[:, 2, :], TT8[:, :, :], AX)
            V.tensor_scalar_min(TAB[:, 0, :], TAB[:, 0, :], float(NE - 1))
            dve.drain()
            V.scalar_tensor_tensor(TAB[:, 2, :], ttab, float(STILE), TAB[:, 2, :], ALU.mult, ALU.add)
            dve.drain()
            V.tensor_scalar(TT8[:, :, 0], TAB[:, 2, :], -1.0, float(s["zero"]), ALU.mult, ALU.add)
            dve.drain()
            V.tensor_tensor(TAB[:, 1, :], TAB[:, 1, :], TT8[:, :, 0], ALU.mult)
            dve.drain()
            V.tensor_tensor(TAB[:, 1, :], TAB[:, 1, :], TAB[:, 2, :], ALU.add)
            dve.drain()
            V.tensor_copy(TABI[:, :, :].rearrange("p a t -> p (a t)"), TAB[:, :, :].rearrange("p a t -> p (a t)"))
            for q in range(2):
                dve.wait_ge(scat[q], STORES + 16 * GRP * NB * GROUPS // 2)
            for e in ("pe", "act", "pool"):
                dve.wait_ge(pass_done[e], NB * NPASS + 1)
            dve.wait_ge(t_out, 16 * NB)
            V.memset(ZR[:, :], 0.0)
            dve.drain()
            V.memset(ZR[:, :].rearrange("p (k c) -> p k c", c=ROW)[:, :, TOK], NOWHERE)
            dve.drain().then_inc(tab_done, 1)

            with dve.Fori(0, NT // 2) as h:
                for q in range(2):
                    t = 2 * h + q
                    dve.wait_ge(r_in[q], 16 * (h + 1))
                    dve.wait_ge(pe_ht, CREDIT + t - 1)
                    for k in range(GRP):
                        V.tensor_scalar(HN[:, q, k, :], XR[:, q, k, 0:C], XR[:, q, k, MEAN:MEAN + 1],
                                        XR[:, q, k, RSTD:RSTD + 1], ALU.subtract, ALU.mult).then_inc(dve_hn, 1)
                    dve.wait_ge(pe_ht, CREDIT + t + 1)
                    V.tensor_copy(HT[:, q, 0, :], B[0][:, :]).then_inc(dve_ht, 1)
                    dve.wait_ge(w_in[q], 64 * (h + 1))
                    dve.wait_ge(y_out[q], STORES + 16 * GRP * h)
                    V.tensor_copy(IDX[:, q, :], XR[:, q, :, TOK])
                    for k in range(GRP):
                        dve.wait_ge(pe_y, CREDIT + t * GRP + k + 1)
                        z = k % 2
                        V.tensor_tensor(YA[:, z, :], B[5 + z][:, 0:C], B2[:, q, :], ALU.add)
                        dve.drain()
                        V.tensor_scalar_mul(YB[:, z, :], YA[:, z, :], XR[:, q, k, PRB:PRB + 1])
                        dve.drain()
                        V.tensor_scalar(YA[:, z, :], YB[:, z, :], 10000.0, -10000.0, ALU.min, ALU.max)
                        V.tensor_tensor(YN[:, z, :], YB[:, z, :], YB[:, z, :], ALU.not_equal)
                        V.tensor_scalar(YF[:, z, :], YB[:, z, :], FMAX, -FMAX, ALU.min, ALU.max)
                        dve.drain()
                        V.tensor_tensor(YM[:, z, :], YF[:, z, :], YB[:, z, :], ALU.is_equal)
                        dve.drain()
                        V.copy_predicated(YA[:, z, :], YM[:, z, :], YB[:, z, :])
                        dve.drain()
                        V.copy_predicated(YA[:, z, :], YN[:, z, :], ZEROS[:, :])
                        dve.drain()
                        V.tensor_tensor(YO[:, q, k, :], YA[:, z, :], XR[:, q, k, 0:C], ALU.add)
                        dve.drain().then_inc(dve_y, 1)

            with dve.Fori(0, NB * GROUPS // 2) as h:
                for q in range(2):
                    dve.wait_ge(pe_ot, CREDIT + 2 * h + q + 1)
                    dve.wait_ge(o_out[q], STORES + 16 * h)
                    V.tensor_copy(OB[:, q, 0, :], B[2 * q][:, :]).then_inc(dve_ot, 1)

        @block.gpsimd
        def _(pool):
            G = nc.gpsimd
            for c in pool_credit:
                pool.sem_inc(c, CREDIT)
            pool.memset(primed[:, :], 0.0)
            pool.drain()
            pool.sem_inc(pass_done["pool"], 1)
            pool.sem_inc(pool_prep, 1)
            for n, c in enumerate((*scat, *y_out, *o_out)):
                pool.dma_start(primer[n:n + 1, :], primed[0:1, :]).then_inc(c, STORES)
            prepared(pool)

            def window_pass(b):
                nm = TILES + 4

                def centre(m, k):
                    n = b * nm + m
                    pool.wait_ge(pe_gram, CREDIT + n - 3)
                    stand_alone(pool)
                    G.tensor_copy(MS[0:R, k % 4, :], FH[0:R, bass.ds(m * P + HALO, P)]).then_inc(pool_ms, 1)

                def cut(m, k):
                    pool.wait_ge(act_e, CREDIT + b * nm + m + 1)
                    stand_alone(pool)
                    G.memset(ER[0:W, k % 8, 512:512 + W], 0.0)
                    G.memset(ER[W:P, k % 8, W:2 * W], 0.0)
                    pool.drain().then_inc(pool_mask, 1)

                for m in range(4):
                    centre(m, m)
                for m in range(4):
                    cut(m, m)
                with pool.Fori(0, PAIRS // 4) as h:
                    for j in range(4):
                        m = 8 * h + 2 * j + 4
                        for t in range(2):
                            centre(m + t, 2 * j + 4 + t)
                        for t in range(2):
                            cut(m + t, 2 * j + 4 + t)

            def attention_pass(b):
                with pool.Fori(0, GROUPS // 2) as h:
                    for k in range(2 * GRP):
                        i = h * 2 * GRP + k
                        pool.wait_ge(xn_done, (b * 3 + 1) * TILES + i + 1)
                        tile = T[:, bass.ds(i, 1), 0:C].rearrange("p o c -> p (o c)")
                        G.tensor_tensor(tile, tile, BO[:, :], ALU.add).then_inc(pool_bias, 1)

            def scatter(b):
                pool.wait_ge(dve_slot, b + 1)
                for g in range(GROUPS):
                    q = g % 2
                    pool.wait_ge(scat[q], STORES + 16 * GRP * (b * (GROUPS // 2) + g // 2))
                    stand_alone(pool)
                    for k in range(GRP):
                        i = g * GRP + k
                        G.indirect_dma_start(rows, bass.IndirectOffsetOnAxis(ap=SLI[:, i:i + 1].bitcast(U32), axis=0),
                                             T[:, i, :], None, bounds_check=s["rows"] - 1, oob_is_err=False).then_inc(scat[q], 16)
                for q in range(2):
                    pool.wait_ge(scat[q], STORES + 16 * GRP * (b + 1) * (GROUPS // 2))
                stand_alone(pool)

            with pool.Fori(0, NB) as b:
                for n, stage in enumerate((None, None, window_pass, None, None, attention_pass, scatter)):
                    pass_starts(pool, "pool", b * NPASS + n)
                    if stage:
                        stage(b)
                    pass_ends(pool, "pool")

            with pool.Fori(0, NT // 2) as h:
                for q in range(2):
                    for k in range(GRP):
                        pool.wait_ge(dve_y, CREDIT + (2 * h + q) * GRP + k + 1)
                        stand_alone(pool)
                        G.indirect_dma_start(toks, bass.IndirectOffsetOnAxis(ap=IDX[:, q, k:k + 1].bitcast(U32), axis=0),
                                             YO[:, q, k, :], None, bounds_check=s["tokens"] - 1,
                                             oob_is_err=False).then_inc(y_out[q], 16)
            with pool.Fori(0, NB) as b:
                with pool.Fori(0, GROUPS // 2) as h:
                    for q in range(2):
                        pool.wait_ge(act_ot, b * GROUPS + 2 * h + q + 1 + CREDIT)
                        pool.wait_ge(dve_ot, b * GROUPS + 2 * h + q + 1 + CREDIT)
                        stand_alone(pool)
                        pool.dma_start(out_v[bass.ds(b, 1), :, :, bass.ds(h * 2 * GC + q * GC, GC)]
                                       .rearrange("o c a n -> c (o a) n"), OB[:, q, :, :]).then_inc(o_out[q], 16)
            for q in range(2):
                pool.wait_ge(o_out[q], STORES + 16 * NB * GROUPS // 2)


_INS = ["x", "L0_conv_W_reduce", "L0_conv_W_proj", "L1_attn_W_qkv", "L1_attn_W_out", "L1_attn_b_out",
        "L1_ffn_gate_w", "L1_ffn_gate_b", "L1_ffn_w1", "L1_ffn_b1", "L1_ffn_w2", "L1_ffn_b2"]


def kernel(**inputs):
    import numpy as _np
    import concourse.bacc as _bacc
    from concourse import mybir as _mybir
    from concourse.bass_utils import run_bass_kernel_spmd as _run

    nc = _bacc.Bacc("TRN2", target_bir_lowering=False, num_devices=1)
    s = sizes(inputs["x"].shape[0])
    arrays, args = {}, []
    named = [(n, _np.ascontiguousarray(inputs[n])) for n in _INS]
    named += list(zip(("konst", "band"), constants(_np, s)))
    for name, a in named:
        arrays[f"in_{name}_dram"] = a
        args.append(nc.dram_tensor(f"in_{name}_dram", a.shape, _mybir.dt.from_np(a.dtype), kind="ExternalInput").ap())
    out = nc.dram_tensor("out_0_dram", inputs["x"].shape, _mybir.dt.float32, kind="ExternalOutput").ap()
    build(nc, s, *args, out)
    r = _run(nc, [arrays], core_ids=[0])
    return r.results[0]["out_0_dram"]
```

```python
import concourse.bass as bass
from concourse import mybir
from concourse.alu_op_type import AluOpType as ALU
from contextlib import ExitStack
import math

F32 = mybir.dt.float32
F32R = mybir.dt.float32r
I32 = mybir.dt.int32
U32 = mybir.dt.uint32
ACT = mybir.ActivationFunctionType
AX = mybir.AxisListType.X

P = 128
C = 256
HALVES = C // P
R = 64
W = 64
WIN = 7
HD = 128
DH = 32
NE = 8
FF = 1024
FB = FF // P
TILES = 32
GRP = 4
GC = GRP * P
GROUPS = TILES // GRP
PAIRS = TILES // 2
HALO = 3 * W
EROW = 640
ROW = 260
NOWHERE = float(2 ** 22)
PEN = -30000.0
FMAX = 3.4028234663852886e38
STILE = 512
SHIFT, RSTD, PRB, TOK = 256, 257, 258, 259


def sizes(nb):
    tokens = nb * TILES * P
    cap = max(1, math.ceil(1.25 * tokens / NE))
    ntile = -(-(tokens + NE * (STILE - 1)) // STILE)
    ntile += ntile % 2
    cp = -(-cap // STILE) * STILE + STILE
    zero = NE * cp
    return dict(nb=nb, tokens=tokens, cap=cap, ntile=ntile, cp=cp, zero=zero, rows=zero + STILE)


K_ID, K_TRI, K_BLK, K_NPAD, K_W8, K_EB, K_TOK, K_SCAN = 0, 128, 256, 384, 416, 424, 432, 464
K_TT, K_EC, K_N = 464 + NE * 33, 464 + NE * 33 + 80, 464 + NE * 33 + 80 + 16


def constants(np, s):
    k = np.zeros((P, K_N), np.float32)
    k[:, K_ID:K_ID + P] = np.eye(P)
    k[:, K_TRI:K_TRI + P] = np.triu(np.ones((P, P)))
    head = np.arange(HD) // DH
    k[:, K_BLK:K_BLK + HD] = (head[:, None] == head[None, :]) * DH ** -0.5
    p = np.arange(P)
    for i in range(TILES):
        y, x = 2 * i + p // W, p % W
        rows = np.minimum(y + 3, 63) - np.maximum(y - 3, 0) + 1
        cols = np.minimum(x + 3, W - 1) - np.maximum(x - 3, 0) + 1
        k[:, K_NPAD + i] = WIN * WIN - rows * cols
        k[:, K_TOK + i] = i * P + p
    k[:, K_W8:K_W8 + NE] = NE - np.arange(NE)
    k[:, K_EB:K_EB + NE] = np.arange(NE) * s["cp"]
    scan = np.ones((NE, TILES + 1))
    scan[:, 0] = 0
    k[:, K_SCAN:K_SCAN + NE * 33] = scan.reshape(-1)
    k[:, K_TT:K_TT + 80] = np.arange(80)
    k[:, K_EC:K_EC + 16] = np.arange(16) * STILE
    col = np.arange(W)
    band = np.zeros((W, 2 * W), np.float32)
    band[:, 0:W] = np.where(np.abs(col[:, None] - col[None, :]) > WIN // 2, PEN, 0)
    band[:, W:] = np.eye(W)
    return k, band


def build(nc, s, x, w_reduce, w_proj, w_qkv, w_out, b_out, gate_w, gate_b, w1, b1, w2, b2, konst, band, out):
    NB, NT, CP, CAP = s["nb"], s["ntile"], s["cp"], s["cap"]
    NPASS = 7
    FHW = P * (TILES + 3) + GC
    ctx = ExitStack()
    with ctx:
        def sem(name):
            return ctx.enter_context(nc.semaphore(name))

        rows = nc.dram_tensor("routed_rows", (s["rows"], ROW), F32).ap()
        primer = nc.dram_tensor("primer", (6, 16), F32).ap()
        toks = nc.dram_tensor("token_rows", (s["tokens"], C), F32).ap()

        def sb(name, shape, dt=F32, to=None):
            return (to or ctx).enter_context(nc.sbuf_tensor(name, shape, dt))

        primed = sb("primed", [1, 16])
        KON = sb("KON", [P, K_N])
        WR = sb("WR", [P, HALVES, R])
        WRr = sb("WRr", [R, C])
        WP = sb("WP", [R, C])
        WPr = sb("WPr", [P, HALVES, R])
        WQ = sb("WQ", [P, HALVES, HD])
        WK = sb("WK", [P, HALVES, HD])
        WV = sb("WV", [P, HALVES, HD])
        WQT = sb("WQT", [HD, C])
        WO = sb("WO", [HD, C])
        BO = sb("BO", [P, C])
        GW = sb("GW", [P, HALVES, NE])
        GB = sb("GB", [P, NE])
        B1R = sb("B1R", [NE * FB, P])
        B1T = sb("B1T", [P, NE * FB])
        ONES = sb("ONES", [P, P])
        ZEROS = sb("ZEROS", [P, C])
        CARRY = sb("CARRY", [P, NE])
        TAB = sb("TAB", [P, 3, 80])
        TABI = sb("TABI", [P, 3, 80], I32)
        NROW = sb("NROW", [P, NE])
        NROWI = sb("NROWI", [P, NE], I32)
        TCNT = sb("TCNT", [P, NE])
        TCUM = sb("TCUM", [P, NE])
        TMP8 = sb("TMP8", [P, NE, 16])
        TT8 = sb("TT8", [P, 80, NE])

        ctx_a = ExitStack()

        def sa(name, shape, dt=F32):
            return sb(name, shape, dt, ctx_a)

        XB = sa("XB", [P, 2, HALVES, GC])
        T = sa("T", [P, TILES, ROW])
        FT = sa("FT", [P, TILES + 4, R + 1])
        FN = sa("FN", [P, 2, GRP, R])
        FH = sa("FH", [P, FHW])
        MS = sa("MS", [P, 4, P])
        ER = sa("ER", [P, 8, EROW])
        CR = sa("CR", [P, 2, 2 * (R + 1)])
        CT = sa("CT", [R, 2, 2 * P])
        RD = sa("RD", [P, 2, 2])
        DEN = sa("DEN", [P, 2, 2])
        SQ = sa("SQ", [P, 8, R])
        SS = sa("SS", [P, TILES])
        SSM = sa("SSM", [P, TILES])
        NRM = sa("NRM", [P, TILES])
        RN = sa("RN", [P, TILES])
        ST = sa("ST", [P, TILES, 6])
        LN = sa("LN", [P, 6, TILES])
        NMR = sa("NMR", [P, TILES])
        XN = sa("XN", [P, 2, GRP, C])
        XT = sa("XT", [P, 2, HALVES, GC])
        KC = sa("KC", [HD, TILES * P])
        KE = sa("KE", [HD, 2, GC])
        KT = sa("KT", [P, 2, GC])
        KMX = sa("KMX", [HD, GROUPS])
        KNM = sa("KNM", [HD, 1])
        KSUM = sa("KSUM", [HD, GROUPS])
        KDEN = sa("KDEN", [HD, 1])
        KRD = sa("KRD", [HD, 1])
        GT = sa("GT", [P, HALVES, HD])
        CTM = sa("CTM", [HD, HD])
        M1 = sa("M1", [HD, C])
        AW = sa("AW", [P, HALVES, C])
        LG = sa("LG", [P, TILES, NE])
        LX = sa("LX", [P, TILES, NE])
        EX = sa("EX", [P, TILES, NE])
        OH = sa("OH", [P, TILES, NE])
        MX = sa("MX", [P, TILES])
        SC = sa("SC", [P, NE * (TILES + 1)])
        SO = sa("SO", [P, NE * (TILES + 1)])
        POS = sa("POS", [P, 4, TILES])
        PRBS = sa("PRBS", [P, TILES])
        SLI = sa("SLI", [P, TILES], I32)
        ctx_a.close()

        W1R = sb("W1R", [P, HALVES, FF])
        W2R = sb("W2R", [P, FB, C])
        W1H = sb("W1H", [P, 2, HALVES, FF], F32R)
        W1L = sb("W1L", [P, 2, HALVES, FF], F32R)
        W2H = sb("W2H", [P, 2, FB, C], F32R)
        W2L = sb("W2L", [P, 2, FB, C], F32R)
        B1 = sb("B1", [P, 2, FB])
        B2 = sb("B2", [P, 2, C])
        XR = sb("XR", [P, 2, GRP, ROW])
        HN = sb("HN", [P, GRP, C])
        HTH = sb("HTH", [P, 2, HALVES, GC], F32R)
        HTL = sb("HTL", [P, 2, HALVES, GC], F32R)
        HSF = sb("HSF", [P, FB, GC])
        HSH = sb("HSH", [P, FB, GC], F32R)
        HSL = sb("HSL", [P, FB, GC], F32R)
        YU = sb("YU", [P, 2, 2, C])
        YV = sb("YV", [P, 2, 2, C])
        YW = sb("YW", [P, 2, 2, C])
        YM = sb("YM", [P, 2, 2, C], U32)
        YO = sb("YO", [P, 2, GRP, C])
        IDX = sb("IDX", [P, 2, GRP], I32)
        spread = HSF[:, :, :].rearrange("p (q f) n -> p q (f n)", q=2)
        ZR = spread[:, 0, 0:GRP * ROW]
        YG = spread[:, :, 0:GRP * C].rearrange("p q (k c) -> p q k c", c=C)
        OB = spread[:, :, GRP * C:2 * GRP * C].rearrange("p q (a n) -> p q a n", a=HALVES)

        B = [ctx.enter_context(nc.psum_tensor(f"bank{i}", [P, 512], F32)) for i in range(8)]

        ident = KON[:, K_ID:K_ID + P]
        tri = KON[:, K_TRI:K_TRI + P]
        blockmask = KON[:, K_BLK:K_BLK + HD]
        npad = KON[:, K_NPAD:K_NPAD + TILES]
        w8 = KON[:, K_W8:K_W8 + NE]
        ebase = KON[:, K_EB:K_EB + NE]
        tok = KON[:, K_TOK:K_TOK + TILES]
        scanmask = KON[:, K_SCAN:K_SCAN + NE * 33]
        ttab = KON[:, K_TT:K_TT + 80]
        ecnt = KON[:, K_EC:K_EC + 16]

        CREDIT = 8
        STORES = 16
        carrier = sem("carrier")
        k_in = sem("k_in")
        x_in = [sem(f"x_in{q}") for q in range(2)]
        pe_prep, dve_prep, pool_prep = sem("pe_prep"), sem("dve_prep"), sem("pool_prep")
        pass_done = {e: sem(f"pass_done_{e}") for e in ("pe", "act", "dve", "pool")}
        pe_feat, act_xt, dve_feat = sem("pe_feat"), sem("act_xt"), sem("dve_feat")
        dve_ssm, act_nrm = sem("dve_ssm"), sem("act_nrm")
        dve_fn, pe_fh, act_fh = sem("dve_fn"), sem("pe_fh"), sem("act_fh")
        pool_ms, pe_gram, act_e, pool_mask = sem("pool_ms"), sem("pe_gram"), sem("act_e"), sem("pool_mask")
        pe_corr, dve_cr, pe_ct, act_ct, pe_proj, dve_t = (sem(n) for n in (
            "pe_corr", "dve_cr", "pe_ct", "act_ct", "pe_proj", "dve_t"))
        dve_var, act_std = sem("dve_var"), sem("act_std")
        xn_done, pe_xt, act_half, dve_half = sem("xn_done"), sem("pe_xt"), sem("act_half"), sem("dve_half")
        pe_k, act_kc, dve_kmx, dve_knm = sem("pe_k"), sem("act_kc"), sem("dve_kmx"), sem("dve_knm")
        act_ke, pe_kt, dve_kt, pe_g = sem("act_ke"), sem("pe_kt"), sem("dve_kt"), sem("pe_g")
        pe_fold, dve_fold = sem("pe_fold"), sem("dve_fold")
        pool_bias, pe_attn, dve_t2 = sem("pool_bias"), sem("pe_attn"), sem("dve_t2")
        pe_logit, dve_lx, act_ex, dve_oh, pe_count, dve_slot = (sem(n) for n in (
            "pe_logit", "dve_lx", "act_ex", "dve_oh", "pe_count", "dve_slot"))
        scat = [sem(f"scat{q}") for q in range(2)]
        tab_done, fill = sem("tab_done"), sem("fill")
        raw_in = sem("raw_in")
        r_in = [sem(f"r_in{q}") for q in range(2)]
        y_out = [sem(f"y_out{q}") for q in range(2)]
        t_out, g_in = sem("t_out"), [sem(f"g_in{q}") for q in range(2)]
        act_w1, act_w2, dve_w1, pool_w2 = sem("act_w1"), sem("act_w2"), sem("dve_w1"), sem("pool_w2")
        act_hn, pe_ht, act_ht, dve_ht, pe_h, act_h, dve_hl, pe_y, dve_yp, dve_y = (sem(n) for n in (
            "act_hn", "pe_ht", "act_ht", "dve_ht", "pe_h", "act_h", "dve_hl", "pe_y", "dve_yp", "dve_y"))
        pe_ot, act_ot, dve_ot = sem("pe_ot"), sem("act_ot"), sem("dve_ot")
        o_out = [sem(f"o_out{q}") for q in range(2)]

        pe_credit = (pe_feat, pe_fh, pe_gram, pe_corr, pe_ct, pe_proj, pe_xt, pe_k, pe_kt, pe_g, pe_attn,
                     pe_ht, pe_h, pe_y, pe_ot)
        act_credit = (act_xt, act_fh, act_e, act_ct, act_half, act_kc, act_ke, act_w1, act_w2, act_hn, act_ht, act_h, act_ot)
        dve_credit = (dve_feat, dve_fn, dve_cr, dve_t, dve_half, dve_kmx, dve_kt, dve_t2, dve_ht,
                      dve_w1, dve_hl, dve_yp, dve_y, dve_ot)
        pool_credit = (pool_ms, pool_mask, pool_bias, pool_w2)

        def stand_alone(eng):
            eng.sem_inc(carrier, 1)

        def pass_starts(eng, me, n):
            for e, done in pass_done.items():
                if e != me:
                    eng.wait_ge(done, n + 1)
            stand_alone(eng)

        def pass_ends(eng, me):
            eng.drain().then_inc(pass_done[me], 1)

        def prepared(eng):
            eng.wait_ge(k_in, 16 * NCONST)
            eng.wait_ge(pe_prep, 1)
            eng.wait_ge(dve_prep, 2)
            eng.wait_ge(pool_prep, 1)

        x_v = x.rearrange("b (a c) h w -> b c a (h w)", a=HALVES)
        out_v = out.rearrange("b (a c) h w -> b c a (h w)", a=HALVES)
        w1_v = w1.rearrange("e (a c) f -> e c a f", a=HALVES)
        w2_v = w2.rearrange("e (k f) c -> e f k c", f=P)

        block = ctx.enter_context(nc.Block())
        NCONST = 14

        @block.sync
        def _(sp):
            qkv = w_qkv.rearrange("(a c) f -> c a f", a=HALVES)
            sp.dma_start(KON[:, :], konst).then_inc(k_in, 16)
            sp.dma_start(WRr[:, :], w_reduce).then_inc(k_in, 16)
            sp.dma_start(B1R[:, :], b1.rearrange("e (k f) -> (e k) f", f=P)).then_inc(k_in, 16)
            sp.dma_start(WPr[:, :, :], w_proj.rearrange("(a c) r -> c a r", a=HALVES)).then_inc(k_in, 16)
            sp.dma_start(WQ[:, :, :], qkv[:, :, 0:HD]).then_inc(k_in, 16)
            sp.dma_start(WK[:, :, :], qkv[:, :, HD:2 * HD]).then_inc(k_in, 16)
            sp.dma_start(WV[:, :, :], qkv[:, :, 2 * HD:3 * HD]).then_inc(k_in, 16)
            sp.dma_start(WO[:, :], w_out).then_inc(k_in, 16)
            sp.dma_start(BO[:, :], b_out.unsqueeze(0).to_broadcast([P, C])).then_inc(k_in, 16)
            sp.dma_start(GW[:, :, :], gate_w.rearrange("(a c) e -> c a e", a=HALVES)).then_inc(k_in, 16)
            sp.dma_start(GB[:, :], gate_b.unsqueeze(0).to_broadcast([P, NE])).then_inc(k_in, 16)
            sp.dma_start(FH[R:P, :].rearrange("p (n w) -> p n w", w=W),
                         band[:, 0:W].unsqueeze(1).to_broadcast([W, FHW // W, W])).then_inc(k_in, 16)
            for v in range(2):
                sp.dma_start(MS[R:P, :, v * W:(v + 1) * W],
                             band[:, W:].unsqueeze(1).to_broadcast([W, 4, W])).then_inc(k_in, 16)
            with sp.Fori(0, NB) as b:
                with sp.Fori(0, GROUPS // 2) as h:
                    for q in range(2):
                        sp.wait_ge(pe_feat, b * TILES + h * 2 * GRP + (q + 1) * GRP)
                        sp.dma_start(XB[:, q, :, :], x_v[bass.ds(b, 1), :, :, bass.ds(h * 2 * GC + q * GC, GC)]
                                     .rearrange("o c a n -> c (o a) n")).then_inc(x_in[q], 16)
                sp.wait_ge(dve_slot, b + 1)
                sp.dma_start(toks[bass.ds(b * TILES * P, TILES * P), :].rearrange("(i p) c -> p i c", p=P),
                             T[:, :, 0:C]).then_inc(t_out, 16)
            sp.wait_ge(tab_done, 1)
            for e in range(NE):
                n = sp.value_load(NROWI[0:1, e:e + 1], min_val=0, max_val=s["zero"])
                sp.dma_start(rows[bass.ds(n, STILE), :].rearrange("(p k) c -> p (k c)", p=P), ZR).then_inc(fill, 16)
            sp.dma_start(rows[s["zero"]:s["zero"] + STILE, :].rearrange("(p k) c -> p (k c)", p=P), ZR).then_inc(fill, 16)
            sp.wait_ge(fill, 16 * (NE + 1))

            def load_weights(t):
                e = sp.value_load(TABI[0:1, 0, bass.ds(t, 1)], min_val=0, max_val=NE - 1)
                for split in (act_w1, act_w2, dve_w1, pool_w2):
                    sp.wait_ge(split, CREDIT + t)
                sp.dma_start(W1R[:, :, :], w1_v[bass.ds(e, 1), :, :, :].rearrange("o c a f -> c (o a) f")).then_inc(raw_in, 16)
                sp.dma_start(W2R[:, :, :], w2_v[bass.ds(e, 1), :, :, :].rearrange("o f k c -> f (o k) c")).then_inc(raw_in, 16)

            def load_rows(t, q):
                e = sp.value_load(TABI[0:1, 0, bass.ds(t, 1)], min_val=0, max_val=NE - 1)
                r = sp.value_load(TABI[0:1, 1, bass.ds(t, 1)], min_val=0, max_val=s["zero"])
                sp.wait_ge(dve_y, CREDIT + (t - 1) * 2)
                sp.dma_start(XR[:, q, :, :], rows[bass.ds(r, STILE), :].rearrange("(p k) c -> p k c", p=P)).then_inc(r_in[q], 16)
                sp.dma_start(B1[:, q, :], B1T[:, bass.ds(e * FB, FB)]).then_inc(r_in[q], 16)
                sp.dma_start(B2[:, q, :], b2[bass.ds(e, 1), :].to_broadcast([P, C])).then_inc(r_in[q], 16)

            load_weights(0)
            load_rows(0, 0)
            load_weights(1)
            load_rows(1, 1)
            with sp.Fori(0, NT // 2) as h:
                for q in range(2):
                    t = 2 * h + q
                    load_weights(t + 2)
                    load_rows(t + 2, q)
            for q in range(2):
                sp.wait_ge(y_out[q], STORES + 16 * GRP * NT // 2)
            with sp.Fori(0, NB * GROUPS // 2) as h:
                for q in range(2):
                    sp.wait_ge(pe_ot, CREDIT + 2 * h + q - 1)
                    sp.dma_start(YG[:, q, :, :], toks[bass.ds(h * 2 * GC + q * GC, GC), :]
                                 .rearrange("(k p) c -> p k c", p=P)).then_inc(g_in[q], 16)

        @block.tensor
        def _(pe):
            mm, tr = nc.tensor.matmul, nc.tensor.transpose
            for c in pe_credit:
                pe.sem_inc(c, CREDIT)
            pe.sem_inc(pass_done["pe"], 1)
            pe.wait_ge(k_in, 16 * NCONST)
            for a in range(HALVES):
                tr(B[0][:, a * R:(a + 1) * R], WRr[:, a * P:(a + 1) * P], ident[0:R, 0:R])
                tr(B[1][0:R, a * P:(a + 1) * P], WPr[:, a, :], ident)
                tr(B[2][:, a * P:(a + 1) * P], WQ[:, a, :], ident)
            tr(B[3][:, 0:NE * FB], B1R[:, :], ident[0:NE * FB, 0:NE * FB])
            pe.drain().then_inc(pe_prep, 1)
            prepared(pe)

            def feature_pass(b):
                with pe.Fori(0, GROUPS // 2) as h:
                    for k in range(2 * GRP):
                        q, sl = k // GRP, bass.ts(k % GRP, P)
                        if k % GRP == 0:
                            pe.wait_ge(x_in[q], 16 * (b * (GROUPS // 2) + h + 1))
                        n = b * TILES + h * 2 * GRP + k
                        pe.wait_ge(act_xt, CREDIT + n - 3)
                        pe.wait_ge(dve_feat, CREDIT + n - 3)
                        bank = B[k % 4]
                        for a in range(HALVES):
                            mm(B[4 + k % 4][:, 0:R], XB[:, q, a, sl], WR[:, a, :], start=a == 0, stop=a == 1)
                        for a in range(HALVES):
                            last = tr(bank[:, bass.ts(a, P)], XB[:, q, a, sl], ident)
                        last.then_inc(pe_feat, 1)

            def map_pass(b):
                with pe.Fori(0, GROUPS // 2) as h:
                    for q in range(2):
                        n = b * GROUPS + 2 * h + q
                        pe.wait_ge(dve_fn, CREDIT + n + 1)
                        pe.wait_ge(act_fh, CREDIT + n - 1)
                        stand_alone(pe)
                        for k in range(GRP):
                            last = tr(B[4 + q][0:R, bass.ts(k, P)], FN[:, q, k, :], ident)
                        last.then_inc(pe_fh, 1)

            def window_pass(b):
                nm, npair = TILES + 4, PAIRS

                def gram(m, k):
                    n = b * nm + m
                    pe.wait_ge(pool_ms, CREDIT + n + 1)
                    pe.wait_ge(act_e, CREDIT + n - 1)
                    mm(B[k % 2][:, :], MS[:, k % 4, :], FH[:, bass.ds(m * P, GC)],
                       start=True, stop=True).then_inc(pe_gram, 1)

                for m in range(4):
                    gram(m, m)
                with pe.Fori(0, PAIRS // 4) as h:
                    for j in range(4):
                        p = 4 * h + j
                        n = b * npair + p
                        gram(2 * p + 4, 2 * j + 4)
                        pe.wait_ge(pool_mask, CREDIT + b * nm + 2 * p + 4)
                        pe.wait_ge(dve_cr, CREDIT + n - 1)
                        for t in range(2):
                            for d in range(-2, 3):
                                last = mm(B[2 + j % 2][:, t * (R + 1):(t + 1) * (R + 1)],
                                          ER[:, (2 * j + t + d) % 8, 256 - P * d:256 - P * d + P],
                                          FT[:, bass.ds(2 * p + t + d + 2, 1), :].rearrange("p o c -> p (o c)"),
                                          start=d == -2, stop=d == 2)
                        last.then_inc(pe_corr, 1)
                        gram(2 * p + 5, 2 * j + 5)
                        pe.wait_ge(dve_cr, CREDIT + n + 1)
                        pe.wait_ge(act_ct, CREDIT + n)
                        stand_alone(pe)
                        for t in range(2):
                            last = tr(B[4][0:R, bass.ts(t, P)], CR[:, j % 2, t * (R + 1):t * (R + 1) + R], ident)
                        last.then_inc(pe_ct, 1)
                        pe.wait_ge(act_ct, CREDIT + n + 1)
                        pe.wait_ge(dve_t, CREDIT + n - 1)
                        for t in range(2):
                            last = mm(B[5 + j % 2][:, bass.ts(t, C)], CT[:, j % 2, bass.ts(t, P)], WP[:, :],
                                      start=True, stop=True)
                        last.then_inc(pe_proj, 1)

            def normed_to_channels(n, q):
                for k in range(GRP):
                    pe.wait_ge(xn_done, n * GRP + k + 1)
                    if k == 0:
                        pe.wait_ge(act_half, CREDIT + n - 1)
                        pe.wait_ge(dve_half, CREDIT + n - 1)
                    for a in range(HALVES):
                        last = tr(B[2 * q + a][:, bass.ts(k, P)], XN[:, q, k, bass.ts(a, P)], ident)
                last.then_inc(pe_xt, 1)

            def channels_ready(n):
                pe.wait_ge(act_half, CREDIT + n + 1)
                pe.wait_ge(dve_half, CREDIT + n + 1)

            def key_pass(b):
                with pe.Fori(0, GROUPS // 2) as h:
                    for q in range(2):
                        normed_to_channels(b * 3 * GROUPS + 2 * h + q, q)
                    for q in range(2):
                        channels_ready(b * 3 * GROUPS + 2 * h + q)
                        n = b * GROUPS + 2 * h + q
                        pe.wait_ge(act_kc, CREDIT + n - 1)
                        for a in range(HALVES):
                            last = mm(B[4 + q][:, :], WK[:, a, :], XT[:, q, a, :], start=a == 0, stop=a == 1)
                        last.then_inc(pe_k, 1)

            def context_pass(b):
                mm(B[6][:, 0:HALVES * HD], ZEROS[:, 0:P], ZEROS[:, :], start=True, stop=False, skip_group_check=True)
                with pe.Fori(0, GROUPS // 2) as h:
                    for q in range(2):
                        n = b * GROUPS + 2 * h + q
                        pe.wait_ge(act_ke, CREDIT + n + 1)
                        pe.wait_ge(dve_kt, CREDIT + n - 1)
                        for k in range(GRP):
                            last = tr(B[q][:, bass.ts(k, P)], KE[:, q, bass.ts(k, P)], ident)
                        last.then_inc(pe_kt, 1)
                    for q in range(2):
                        n = b * GROUPS + 2 * h + q
                        pe.wait_ge(dve_kt, CREDIT + n + 1)
                        for k in range(GRP):
                            for a in range(HALVES):
                                last = mm(B[6][:, bass.ts(a, HD)], XN[:, q, k, bass.ts(a, P)], KT[:, q, bass.ts(k, P)],
                                          start=False, stop=False, skip_group_check=True)
                        last.then_inc(pe_g, 1)
                pe.wait_ge(dve_fold, 3 * b + 1)
                for a in range(HALVES):
                    last = mm(B[0][:, 0:HD], WV[:, a, :], GT[:, a, :], start=a == 0, stop=a == 1)
                last.then_inc(pe_fold, 1)
                pe.wait_ge(dve_fold, 3 * b + 2)
                mm(B[1][:, 0:C], CTM[:, :], WO[:, :], start=True, stop=True).then_inc(pe_fold, 1)
                pe.wait_ge(dve_fold, 3 * b + 3)
                for a in range(HALVES):
                    last = mm(B[2][:, bass.ts(a, C)], WQT[:, bass.ts(a, P)], M1[:, :], start=True, stop=True)
                last.then_inc(pe_fold, 1)

            def attention_pass(b):
                with pe.Fori(0, GROUPS // 2) as h:
                    for q in range(2):
                        normed_to_channels(b * 3 * GROUPS + GROUPS + 2 * h + q, q)
                    for q in range(2):
                        channels_ready(b * 3 * GROUPS + GROUPS + 2 * h + q)
                        for k in range(GRP):
                            if k % 2 == 0:
                                pe.wait_ge(dve_t2, CREDIT + b * TILES + h * 2 * GRP + q * GRP + k - 6)
                            for a in range(HALVES):
                                last = mm(B[4 + 2 * q + k // 2][:, bass.ts(k % 2, C)], XT[:, q, a, bass.ts(k, P)],
                                          AW[:, a, :], start=a == 0, stop=a == 1)
                            last.then_inc(pe_attn, 1)

            def routing_pass(b):
                with pe.Fori(0, GROUPS // 2) as h:
                    for q in range(2):
                        normed_to_channels(b * 3 * GROUPS + 2 * GROUPS + 2 * h + q, q)
                    for q in range(2):
                        channels_ready(b * 3 * GROUPS + 2 * GROUPS + 2 * h + q)
                        for k in range(GRP):
                            i = h * 2 * GRP + q * GRP + k
                            for a in range(HALVES):
                                last = mm(B[4][:, bass.ds(i * NE, NE)], XT[:, q, a, bass.ts(k, P)], GW[:, a, :],
                                          start=a == 0, stop=a == 1)
                        last.then_inc(pe_logit, 1)
                pe.wait_ge(dve_oh, b + 1)
                oh = OH[:, :, :].rearrange("p i e -> p (i e)")
                mm(B[5][:, 0:TILES * NE], tri, oh, start=True, stop=True)
                mm(B[6][:, 0:TILES * NE], ONES[:, :], oh, start=True, stop=True).then_inc(pe_count, 1)

            with pe.Fori(0, NB) as b:
                for n, stage in enumerate((feature_pass, map_pass, window_pass, key_pass, context_pass,
                                           attention_pass, routing_pass)):
                    pass_starts(pe, "pe", b * NPASS + n)
                    stage(b)
                    pass_ends(pe, "pe")

            def rows_to_channels(t, q):
                pe.wait_ge(act_hn, CREDIT + t + 1)
                pe.wait_ge(act_ht, CREDIT + t)
                pe.wait_ge(dve_ht, CREDIT + t)
                for k in range(GRP):
                    for a in range(HALVES):
                        last = tr(B[a][:, bass.ts(k, P)], HN[:, k, bass.ts(a, P)], ident)
                last.then_inc(pe_ht, 1)

            def split_product(out, terms, first, last):
                for n, (a, b) in enumerate(terms):
                    r = mm(out, a, b, start=first and n == 0, stop=last and n == len(terms) - 1)
                return r

            rows_to_channels(0, 0)
            with pe.Fori(0, NT // 2) as h:
                for q in range(2):
                    t = 2 * h + q
                    pe.wait_ge(act_w1, CREDIT + t + 1)
                    pe.wait_ge(dve_w1, CREDIT + t + 1)
                    pe.wait_ge(act_ht, CREDIT + t + 1)
                    pe.wait_ge(dve_ht, CREDIT + t + 1)
                    for f in range(FB):
                        pe.wait_ge(act_h, CREDIT + t * FB + f - 3)
                        for a in range(HALVES):
                            wh, wl = W1H[:, q, a, bass.ts(f, P)], W1L[:, q, a, bass.ts(f, P)]
                            last = split_product(B[(2, 3, 4, 7)[f % 4]][:, :],
                                                 ((wh, HTH[:, q, a, :]), (wh, HTL[:, q, a, :]), (wl, HTH[:, q, a, :])),
                                                 a == 0, a == HALVES - 1)
                        last.then_inc(pe_h, 1)
                    for k in range(GRP):
                        if k == 2:
                            rows_to_channels(t + 1, 1 - q)
                        if k % 2 == 0:
                            pe.wait_ge(dve_yp, CREDIT + 2 * t + k // 2 - 1)
                        if k == 0:
                            pe.wait_ge(act_w2, CREDIT + t + 1)
                            pe.wait_ge(pool_w2, CREDIT + t + 1)
                        for f in range(FB):
                            if k == 0:
                                pe.wait_ge(dve_hl, CREDIT + t * FB + f + 1)
                            hh, hl = HSH[:, f, bass.ts(k, P)], HSL[:, f, bass.ts(k, P)]
                            last = split_product(B[5 + k // 2][:, bass.ts(k % 2, C)],
                                                 ((hh, W2H[:, q, f, :]), (hh, W2L[:, q, f, :]), (hl, W2H[:, q, f, :])),
                                                 f == 0, f == FB - 1)
                        if k % 2 == 1:
                            last.then_inc(pe_y, 1)

            with pe.Fori(0, NB * GROUPS // 2) as h:
                for q in range(2):
                    n = 2 * h + q
                    pe.wait_ge(act_ot, CREDIT + n - 1)
                    pe.wait_ge(dve_ot, CREDIT + n - 1)
                    pe.wait_ge(g_in[q], 16 * (h + 1))
                    for k in range(GRP):
                        for a in range(HALVES):
                            last = tr(B[2 * q + a][:, bass.ts(k, P)], YG[:, q, k, bass.ts(a, P)], ident)
                    last.then_inc(pe_ot, 1)

        @block.scalar
        def _(act):
            A = nc.scalar.activation
            for c in act_credit:
                act.sem_inc(c, CREDIT)
            act.sem_inc(pass_done["act"], 1)
            prepared(act)

            def feature_pass(b):
                with act.Fori(0, GROUPS // 2) as h:
                    for k in range(2 * GRP):
                        i = h * 2 * GRP + k
                        act.wait_ge(pe_feat, CREDIT + b * TILES + i + 1)
                        A(T[:, bass.ds(i, 1), 0:C].rearrange("p o c -> p (o c)"), B[k % 4][:, 0:C], ACT.Copy)
                        act.wait_ge(dve_feat, CREDIT + b * TILES + i + 1)
                        act.wait_ge(act_xt, b * TILES + i + 1)
                        A(SQ[:, k, :], FT[:, bass.ds(i + 2, 1), 0:R].rearrange("p o c -> p (o c)"), ACT.Square, accum_out=SS[:, bass.ds(i, 1)]).then_inc(act_xt, 1)
                act.wait_ge(dve_ssm, b + 1)
                A(NRM[:, :], SSM[:, :], ACT.Sqrt).then_inc(act_nrm, 1)

            def map_pass(b):
                with act.Fori(0, GROUPS // 2) as h:
                    for q in range(2):
                        act.wait_ge(pe_fh, CREDIT + b * GROUPS + 2 * h + q + 1)
                        A(FH[0:R, bass.ds(h * 2 * GC + q * GC + HALO, GC)], B[4 + q][0:R, :], ACT.Copy).then_inc(act_fh, 1)

            def window_pass(b):
                nm = TILES + 4

                def weights(m, k):
                    act.wait_ge(pe_gram, CREDIT + b * nm + m + 1)
                    A(ER[:, k % 8, W:W + GC], B[k % 2][:, :], ACT.Exp).then_inc(act_e, 1)

                for m in range(4):
                    weights(m, m)
                with act.Fori(0, PAIRS // 4) as h:
                    for j in range(4):
                        p = 4 * h + j
                        act.wait_ge(pe_corr, CREDIT + b * PAIRS + p)
                        weights(2 * p + 4, 2 * j + 4)
                        weights(2 * p + 5, 2 * j + 5)
                        act.wait_ge(pe_ct, CREDIT + b * PAIRS + p + 1)
                        act.wait_ge(pe_proj, CREDIT + b * PAIRS + p - 1)
                        A(CT[:, j % 2, :], B[4][0:R, 0:2 * P], ACT.Copy).then_inc(act_ct, 1)
                act.wait_ge(dve_var, 2 * b + 1)
                A(LN[:, 4, :], LN[:, 3, :], ACT.Sqrt).then_inc(act_std, 1)

            def half(n, q):
                act.wait_ge(pe_xt, CREDIT + n + 1)
                A(XT[:, q, 1, :], B[2 * q + 1][:, :], ACT.Copy).then_inc(act_half, 1)

            def key_pass(b):
                with act.Fori(0, GROUPS // 2) as h:
                    for q in range(2):
                        half(b * 3 * GROUPS + 2 * h + q, q)
                    for q in range(2):
                        act.wait_ge(pe_k, CREDIT + b * GROUPS + 2 * h + q + 1)
                        A(KC[:, bass.ds(h * 2 * GC + q * GC, GC)], B[4 + q][:, :], ACT.Copy).then_inc(act_kc, 1)

            def context_pass(b):
                act.wait_ge(dve_knm, b + 1)
                stand_alone(act)
                with act.Fori(0, GROUPS // 2) as h:
                    for q in range(2):
                        n = b * GROUPS + 2 * h + q
                        act.wait_ge(pe_kt, CREDIT + n - 1)
                        A(KE[:, q, :], KC[:, bass.ds(h * 2 * GC + q * GC, GC)], ACT.Exp, bias=KNM[:, :],
                          accum_out=KSUM[:, bass.ds(2 * h + q, 1)]).then_inc(act_ke, 1)

            def attention_pass(b):
                with act.Fori(0, GROUPS // 2) as h:
                    for q in range(2):
                        n = b * 3 * GROUPS + GROUPS + 2 * h + q
                        act.wait_ge(pe_xt, CREDIT + n - 1)
                        for k in range(GRP):
                            i = h * 2 * GRP + q * GRP + k
                            A(XN[:, q, k, :], T[:, bass.ds(i, 1), 0:C].rearrange("p o c -> p (o c)"), ACT.Identity,
                              bias=NMR[:, bass.ds(i, 1)], scale=LN[:, 5, bass.ds(i, 1)]).then_inc(xn_done, 1)
                    for q in range(2):
                        half(b * 3 * GROUPS + GROUPS + 2 * h + q, q)
                act.wait_ge(dve_var, 2 * b + 2)
                A(LN[:, 4, :], LN[:, 3, :], ACT.Sqrt).then_inc(act_std, 1)

            def routing_pass(b):
                with act.Fori(0, GROUPS // 2) as h:
                    for q in range(2):
                        half(b * 3 * GROUPS + 2 * GROUPS + 2 * h + q, q)
                act.wait_ge(dve_lx, b + 1)
                A(EX[:, :, :].rearrange("p i e -> p (i e)"), LX[:, :, :].rearrange("p i e -> p (i e)"),
                  ACT.Exp).then_inc(act_ex, 1)

            with act.Fori(0, NB) as b:
                for n, stage in enumerate((feature_pass, map_pass, window_pass, key_pass, context_pass,
                                           attention_pass, routing_pass)):
                    pass_starts(act, "act", b * NPASS + n)
                    stage(b)
                    pass_ends(act, "act")

            def high_part(out, raw, done, used, n):
                act.wait_ge(used, n)
                A(out, raw, ACT.Copy).then_inc(done, 1)

            def normed_rows(t, q):
                act.wait_ge(r_in[q], 48 * (t // 2 + 1) if isinstance(t, int) else 24 * (t + 2 - q))
                act.wait_ge(pe_ht, CREDIT + t)
                for k in range(GRP):
                    last = A(HN[:, k, :], XR[:, q, k, 0:C], ACT.Identity, bias=XR[:, q, k, SHIFT:SHIFT + 1],
                             scale=XR[:, q, k, RSTD:RSTD + 1])
                act.drain().then_inc(act_hn, 1)

            def high_w1(t, q):
                act.wait_ge(raw_in, 32 * (t + 1))
                high_part(W1H[:, q, :, :].rearrange("p a f -> p (a f)"), W1R[:, :, :].rearrange("p a f -> p (a f)"),
                          act_w1, pe_h, CREDIT + (t - 1) * FB)

            def high_w2(t, q):
                high_part(W2H[:, q, :, :].rearrange("p a f -> p (a f)"), W2R[:, :, :].rearrange("p a f -> p (a f)"),
                          act_w2, pe_y, CREDIT + (t - 1) * 2)

            def high_rows(t, q):
                act.wait_ge(pe_ht, CREDIT + t + 1)
                for a in range(HALVES):
                    A(HTH[:, q, a, :], B[a][:, :], ACT.Copy)
                act.drain().then_inc(act_ht, 1)

            normed_rows(0, 0)
            high_w1(0, 0)
            high_rows(0, 0)
            high_w2(0, 0)
            with act.Fori(0, NT // 2) as h:
                for q in range(2):
                    t = 2 * h + q
                    for f in range(FB):
                        act.wait_ge(pe_h, CREDIT + t * FB + f + 1)
                        bank = B[(2, 3, 4, 7)[f % 4]][:, :]
                        A(HSF[:, f, :], bank, ACT.Relu, bias=B1[:, q, f:f + 1])
                        A(HSH[:, f, :], bank, ACT.Relu, bias=B1[:, q, f:f + 1]).then_inc(act_h, 1)
                    normed_rows(t + 1, 1 - q)
                    high_w1(t + 1, 1 - q)
                    high_rows(t + 1, 1 - q)
                    high_w2(t + 1, 1 - q)

            with act.Fori(0, NB * GROUPS // 2) as h:
                for q in range(2):
                    act.wait_ge(pe_ot, CREDIT + 2 * h + q + 1)
                    act.wait_ge(o_out[q], STORES + 16 * h)
                    A(OB[:, q, 1, :], B[2 * q + 1][:, :], ACT.Copy).then_inc(act_ot, 1)

        @block.vector
        def _(dve):
            V = nc.vector
            for c in dve_credit:
                dve.sem_inc(c, CREDIT)
            dve.sem_inc(pass_done["dve"], 1)
            V.memset(ONES[:, :], 1.0)
            V.memset(ZEROS[:, :], 0.0)
            V.memset(FT[:, :, :], 0.0)
            V.memset(FH[0:R, :], 0.0)
            V.memset(ER[:, :, :], 0.0)
            V.memset(CARRY[:, :], 0.0)
            V.memset(T[:, :, C:ROW], 0.0)
            dve.drain()
            V.memset(FT[:, 2:TILES + 2, R:R + 1], 1.0)
            dve.drain().then_inc(dve_prep, 1)
            dve.wait_ge(k_in, 16 * NCONST)
            dve.wait_ge(pe_prep, 1)
            V.tensor_copy(WR[:, :, :].rearrange("p a r -> p (a r)"), B[0][:, 0:HALVES * R])
            V.tensor_copy(WP[:, :], B[1][0:R, 0:C])
            V.tensor_copy(WQT[:, :], B[2][:, 0:C])
            V.tensor_copy(B1T[:, :], B[3][:, 0:NE * FB])
            dve.drain().then_inc(dve_prep, 1)
            prepared(dve)

            def tile_of(i):
                return T[:, bass.ds(i, 1), 0:C].rearrange("p o c -> p (o c)")

            def feature_pass(b):
                with dve.Fori(0, GROUPS // 2) as h:
                    for k in range(2 * GRP):
                        i = h * 2 * GRP + k
                        dve.wait_ge(pe_feat, CREDIT + b * TILES + i + 1)
                        V.tensor_copy(FT[:, bass.ds(i + 2, 1), 0:R].rearrange("p o c -> p (o c)"),
                                      B[4 + k % 4][:, 0:R]).then_inc(dve_feat, 1)
                dve.wait_ge(act_xt, CREDIT + (b + 1) * TILES)
                V.tensor_scalar_max(SSM[:, :], SS[:, :], 1e-16).then_inc(dve_ssm, 1)
                dve.wait_ge(act_nrm, b + 1)
                V.reciprocal(RN[:, :], NRM[:, :])
                dve.drain()

            def map_pass(b):
                with dve.Fori(0, GROUPS // 2) as h:
                    for q in range(2):
                        dve.wait_ge(pe_fh, CREDIT + b * GROUPS + 2 * h + q - 1)
                        i = h * 2 * GRP + q * GRP
                        V.tensor_tensor(FN[:, q, :, :], FT[:, bass.ds(i + 2, GRP), 0:R],
                                        RN[:, bass.ds(i, GRP)].unsqueeze(2).to_broadcast([P, GRP, R]),
                                        ALU.mult).then_inc(dve_fn, 1)

            def statistics(b, which):
                eps = 1e-5
                dve.drain()
                V.tensor_tensor(LN[:, 0, :], ST[:, :, 1], ST[:, :, 4], ALU.add)
                V.tensor_tensor(LN[:, 1, :], ST[:, :, 1], ST[:, :, 4], ALU.subtract)
                V.tensor_tensor(LN[:, 2, :], ST[:, :, 2], ST[:, :, 5], ALU.add)
                dve.drain()
                V.scalar_tensor_tensor(LN[:, 1, :], LN[:, 1, :], 0.25, LN[:, 1, :], ALU.mult, ALU.mult)
                V.tensor_scalar(LN[:, 2, :], LN[:, 2, :], 1.0 / C, eps, ALU.mult, ALU.add)
                V.tensor_scalar_mul(LN[:, 0, :], LN[:, 0, :], 0.5)
                dve.drain()
                V.tensor_tensor(LN[:, 3, :], LN[:, 1, :], LN[:, 2, :], ALU.add).then_inc(dve_var, 1)
                dve.wait_ge(act_std, 2 * b + which + 1)
                V.reciprocal(LN[:, 5, :], LN[:, 4, :])
                dve.drain()
                V.scalar_tensor_tensor(NMR[:, :], LN[:, 0, :], -1.0, LN[:, 5, :], ALU.mult, ALU.mult)
                dve.drain()

            def window_pass(b):
                with dve.Fori(0, PAIRS // 4) as h:
                    for j in range(4):
                        p = 4 * h + j
                        n = b * PAIRS + p
                        dve.wait_ge(pe_corr, CREDIT + n + 1)
                        dve.wait_ge(pe_ct, CREDIT + n - 1)
                        V.tensor_copy(CR[:, j % 2, :], B[2 + j % 2][:, 0:2 * (R + 1)]).then_inc(dve_cr, 1)
                        dve.drain()
                        V.tensor_tensor(DEN[:, j % 2, :],
                                        CR[:, j % 2, :].rearrange("p (t c) -> p t c", t=2)[:, :, R],
                                        npad[:, bass.ds(2 * p, 2)], ALU.add)
                        dve.drain()
                        V.reciprocal(RD[:, j % 2, :], DEN[:, j % 2, :])
                        dve.drain()
                        dve.wait_ge(pe_proj, CREDIT + n + 1)
                        for t in range(2):
                            i = 2 * p + t
                            V.scalar_tensor_tensor(tile_of(i), B[5 + j % 2][:, bass.ts(t, C)], RD[:, j % 2, t:t + 1],
                                                   tile_of(i), ALU.mult, ALU.add)
                        dve.drain().then_inc(dve_t, 1)
                        for t in range(2):
                            i = 2 * p + t
                            V.bn_stats(ST[:, bass.ds(i, 1), :].rearrange("p o c -> p (o c)"), tile_of(i))
                statistics(b, 0)

            def half(n, q):
                dve.wait_ge(pe_xt, CREDIT + n + 1)
                V.tensor_copy(XT[:, q, 0, :], B[2 * q][:, :]).then_inc(dve_half, 1)

            def norm(h, q, n, counted):
                for k in range(GRP):
                    i = h * 2 * GRP + q * GRP + k
                    x_n = V.tensor_scalar(XN[:, q, k, :], tile_of(i), LN[:, 0, bass.ds(i, 1)], LN[:, 5, bass.ds(i, 1)],
                                          ALU.subtract, ALU.mult)
                    if counted:
                        x_n.then_inc(xn_done, 1)

            def key_pass(b):
                with dve.Fori(0, GROUPS // 2) as h:
                    for q in range(2):
                        n = b * 3 * GROUPS + 2 * h + q
                        dve.wait_ge(pe_xt, CREDIT + n - 1)
                        norm(h, q, n, True)
                    for q in range(2):
                        half(b * 3 * GROUPS + 2 * h + q, q)
                    for q in range(2):
                        dve.wait_ge(act_kc, CREDIT + b * GROUPS + 2 * h + q + 1)
                        V.reduce_max(KMX[:, bass.ds(2 * h + q, 1)], KC[:, bass.ds(h * 2 * GC + q * GC, GC)], AX).then_inc(dve_kmx, 1)
                dve.drain()
                V.reduce_max(KNM[:, :], KMX[:, :], AX)
                dve.drain()
                V.tensor_scalar_mul(KNM[:, :], KNM[:, :], -1.0).then_inc(dve_knm, 1)

            def context_pass(b):
                with dve.Fori(0, GROUPS // 2) as h:
                    for q in range(2):
                        n = b * GROUPS + 2 * h + q
                        dve.wait_ge(pe_g, CREDIT + n - 1)
                        norm(h, q, n, False)
                        dve.wait_ge(pe_kt, CREDIT + n + 1)
                        V.tensor_copy(KT[:, q, :], B[q][:, :])
                        dve.drain().then_inc(dve_kt, 1)
                dve.wait_ge(pe_g, CREDIT + (b + 1) * GROUPS)
                V.tensor_copy(GT[:, :, :].rearrange("p a d -> p (a d)"), B[6][:, 0:HALVES * HD]).then_inc(dve_fold, 1)
                dve.wait_ge(act_ke, CREDIT + (b + 1) * GROUPS)
                V.reduce_sum(KDEN[:, :], KSUM[:, :], AX)
                dve.drain()
                V.reciprocal(KRD[:, :], KDEN[:, :])
                dve.wait_ge(pe_fold, 3 * b + 1)
                V.tensor_tensor(CTM[:, :], B[0][:, 0:HD], blockmask, ALU.mult).then_inc(dve_fold, 1)
                dve.drain()
                dve.wait_ge(pe_fold, 3 * b + 2)
                V.tensor_scalar_mul(M1[:, :], B[1][:, 0:C], KRD[:, :]).then_inc(dve_fold, 1)
                dve.wait_ge(pe_fold, 3 * b + 3)
                V.tensor_copy(AW[:, :, :].rearrange("p a c -> p (a c)"), B[2][:, :])

            def attention_pass(b):
                with dve.Fori(0, GROUPS // 2) as h:
                    for q in range(2):
                        half(b * 3 * GROUPS + GROUPS + 2 * h + q, q)
                    for q in range(2):
                        for k in range(GRP):
                            i = h * 2 * GRP + q * GRP + k
                            if k % 2 == 0:
                                dve.wait_ge(pe_attn, CREDIT + b * TILES + i + 2)
                            dve.wait_ge(pool_bias, CREDIT + b * TILES + i + 1)
                            V.tensor_tensor(tile_of(i), B[4 + 2 * q + k // 2][:, bass.ts(k % 2, C)], tile_of(i),
                                            ALU.add).then_inc(dve_t2, 1)
                            if k % 2 == 1:
                                dve.drain()
                                for j in (i - 1, i):
                                    V.bn_stats(ST[:, bass.ds(j, 1), :].rearrange("p o c -> p (o c)"), tile_of(j))
                statistics(b, 1)

            def routing_pass(b):
                with dve.Fori(0, GROUPS // 2) as h:
                    for q in range(2):
                        n = b * 3 * GROUPS + 2 * GROUPS + 2 * h + q
                        dve.wait_ge(pe_xt, CREDIT + n - 1)
                        norm(h, q, n, True)
                    for q in range(2):
                        half(b * 3 * GROUPS + 2 * GROUPS + 2 * h + q, q)
                dve.wait_ge(pe_logit, (b + 1) * GROUPS)
                wide = [P, TILES, NE]
                V.tensor_tensor(LG[:, :, :], B[4][:, 0:TILES * NE].rearrange("p (i e) -> p i e", e=NE),
                                GB[:, :].unsqueeze(1).to_broadcast(wide), ALU.add)
                dve.drain()
                V.reduce_max(MX[:, :], LG[:, :, :], AX)
                dve.drain()
                top = MX[:, :].unsqueeze(2).to_broadcast(wide)
                V.tensor_tensor(LX[:, :, :], LG[:, :, :], top, ALU.subtract).then_inc(dve_lx, 1)
                V.tensor_tensor(OH[:, :, :], LG[:, :, :], top, ALU.is_ge)
                dve.drain()
                V.tensor_tensor(LG[:, :, :], OH[:, :, :], w8.unsqueeze(1).to_broadcast(wide), ALU.mult)
                dve.drain()
                V.reduce_max(MX[:, :], LG[:, :, :], AX)
                dve.drain()
                V.tensor_tensor(OH[:, :, :], LG[:, :, :], top, ALU.is_equal).then_inc(dve_oh, 1)
                dve.wait_ge(act_ex, b + 1)
                V.reduce_sum(PRBS[:, :], EX[:, :, :], AX)
                dve.drain()
                V.reciprocal(T[:, :, PRB], PRBS[:, :])
                V.tensor_copy(T[:, :, SHIFT], NMR[:, :])
                V.tensor_copy(T[:, :, RSTD], LN[:, 5, :])
                sc = SC[:, :].rearrange("p (e j) -> p e j", e=NE)
                so = SO[:, :].rearrange("p (e j) -> p e j", e=NE)
                V.tensor_copy(sc[:, :, 0], CARRY[:, :])
                dve.wait_ge(pe_count, b + 1)
                V.tensor_copy(sc[:, :, 1:TILES + 1], B[6][:, 0:TILES * NE].rearrange("p (i e) -> p e i", e=NE))
                dve.drain()
                V.tensor_tensor_scan(SO[:, :], scanmask, SC[:, :], 0.0, ALU.mult, ALU.add)
                dve.drain()
                V.tensor_copy(CARRY[:, :], so[:, :, TILES])
                V.tensor_tensor(LX[:, :, :], B[5][:, 0:TILES * NE].rearrange("p (i e) -> p i e", e=NE),
                                so[:, :, 0:TILES].rearrange("p e i -> p i e"), ALU.add)
                dve.drain()
                V.tensor_tensor(LX[:, :, :], LX[:, :, :], OH[:, :, :], ALU.mult)
                V.tensor_tensor(LG[:, :, :], OH[:, :, :], ebase.unsqueeze(1).to_broadcast(wide), ALU.mult)
                dve.drain()
                V.reduce_sum(POS[:, 0, :], LX[:, :, :], AX)
                V.reduce_sum(POS[:, 1, :], LG[:, :, :], AX)
                dve.drain()
                V.tensor_scalar(POS[:, 2, :], POS[:, 0, :], float(CAP) + 0.5, None, ALU.is_lt)
                V.scalar_tensor_tensor(POS[:, 3, :], POS[:, 0, :], -1.0, POS[:, 1, :], ALU.add, ALU.add)
                dve.drain()
                V.tensor_scalar_add(POS[:, 3, :], POS[:, 3, :], -NOWHERE)
                dve.drain()
                V.tensor_tensor(POS[:, 3, :], POS[:, 3, :], POS[:, 2, :], ALU.mult)
                dve.drain()
                V.tensor_scalar_add(POS[:, 3, :], POS[:, 3, :], NOWHERE)
                dve.drain()
                V.tensor_copy(SLI[:, :], POS[:, 3, :])
                V.tensor_copy(T[:, :, TOK], tok)
                dve.drain()
                V.tensor_scalar_add(tok, tok, float(TILES * P))
                dve.drain().then_inc(dve_slot, 1)

            with dve.Fori(0, NB) as b:
                for n, stage in enumerate((feature_pass, map_pass, window_pass, key_pass, context_pass,
                                           attention_pass, routing_pass)):
                    pass_starts(dve, "dve", b * NPASS + n)
                    stage(b)
                    pass_ends(dve, "dve")

            V.tensor_scalar_min(NROW[:, :], CARRY[:, :], float(CAP))
            dve.drain()
            V.tensor_tensor(TMP8[:, :, :], NROW[:, :].unsqueeze(2).to_broadcast([P, NE, 16]),
                            ecnt.unsqueeze(1).to_broadcast([P, NE, 16]), ALU.is_gt)
            dve.drain()
            V.reduce_sum(TCNT[:, :], TMP8[:, :, :], AX)
            V.tensor_tensor(NROW[:, :], NROW[:, :], ebase, ALU.add)
            dve.drain()
            V.tensor_copy(NROWI[:, :], NROW[:, :])
            V.tensor_tensor_scan(TCUM[:, :], ONES[:, 0:NE], TCNT[:, :], 0.0, ALU.mult, ALU.add)
            dve.drain()
            V.tensor_tensor(TT8[:, :, :], ttab.unsqueeze(2).to_broadcast([P, 80, NE]),
                            TCUM[:, :].unsqueeze(1).to_broadcast([P, 80, NE]), ALU.is_ge)
            V.tensor_scalar(TCNT[:, :], TCNT[:, :], -float(STILE), float(CP), ALU.mult, ALU.add)
            dve.drain()
            V.reduce_sum(TAB[:, 0, :], TT8[:, :, :], AX)
            V.tensor_copy(TAB[:, 1, :], TT8[:, :, NE - 1])
            dve.drain()
            V.tensor_tensor(TT8[:, :, :], TT8[:, :, :], TCNT[:, :].unsqueeze(1).to_broadcast([P, 80, NE]), ALU.mult)
            dve.drain()
            V.reduce_sum(TAB[:, 2, :], TT8[:, :, :], AX)
            V.tensor_scalar_min(TAB[:, 0, :], TAB[:, 0, :], float(NE - 1))
            dve.drain()
            V.scalar_tensor_tensor(TAB[:, 2, :], ttab, float(STILE), TAB[:, 2, :], ALU.mult, ALU.add)
            dve.drain()
            V.tensor_scalar(TT8[:, :, 0], TAB[:, 2, :], -1.0, float(s["zero"]), ALU.mult, ALU.add)
            dve.drain()
            V.tensor_tensor(TAB[:, 1, :], TAB[:, 1, :], TT8[:, :, 0], ALU.mult)
            dve.drain()
            V.tensor_tensor(TAB[:, 1, :], TAB[:, 1, :], TAB[:, 2, :], ALU.add)
            dve.drain()
            V.tensor_copy(TABI[:, :, :].rearrange("p a t -> p (a t)"), TAB[:, :, :].rearrange("p a t -> p (a t)"))
            for q in range(2):
                dve.wait_ge(scat[q], STORES + 16 * GRP * NB * GROUPS // 2)
            for e in ("pe", "act", "pool"):
                dve.wait_ge(pass_done[e], NB * NPASS + 1)
            dve.wait_ge(t_out, 16 * NB)
            V.memset(ZR, 0.0)
            dve.drain()
            V.memset(ZR.rearrange("p (k c) -> p k c", c=ROW)[:, :, TOK], NOWHERE)
            dve.drain().then_inc(tab_done, 1)

            def low_w1(t, q):
                dve.wait_ge(act_w1, CREDIT + t + 1)
                V.tensor_tensor(W1L[:, q, :, :].rearrange("p a f -> p (a f)"), W1R[:, :, :].rearrange("p a f -> p (a f)"),
                                W1H[:, q, :, :].bitcast(F32).rearrange("p a f -> p (a f)"),
                                ALU.subtract).then_inc(dve_w1, 1)

            def low_rows(t, q):
                dve.wait_ge(act_ht, CREDIT + t + 1)
                for a in range(HALVES):
                    V.tensor_tensor(HTL[:, q, a, :], B[a][:, :], HTH[:, q, a, :].bitcast(F32), ALU.subtract)
                dve.drain().then_inc(dve_ht, 1)

            def outputs(t, q, g, h):
                pair = [P, 2, C]
                dve.wait_ge(pe_y, CREDIT + 2 * t + g + 1)
                V.tensor_tensor(YU[:, g, :, :], B[5 + g][:, :].rearrange("p (k c) -> p k c", c=C),
                                B2[:, q, :].unsqueeze(1).to_broadcast(pair), ALU.add).then_inc(dve_yp, 1)
                dve.drain()
                for k in range(2):
                    V.tensor_scalar_mul(YU[:, g, k, :], YU[:, g, k, :], XR[:, q, 2 * g + k, PRB:PRB + 1])
                dve.drain()
                V.tensor_scalar(YV[:, g, :, :], YU[:, g, :, :], 5000.0, -5000.0, ALU.min, ALU.max)
                V.tensor_scalar(YW[:, g, :, :], YU[:, g, :, :], -5000.0, 5000.0, ALU.max, ALU.min)
                V.tensor_scalar(YM[:, g, :, :], YU[:, g, :, :].bitcast(U32), 0xFFFFFFFF, 0x7F800000,
                                ALU.bitwise_xor, ALU.bitwise_and)
                dve.drain()
                V.tensor_tensor(YV[:, g, :, :], YV[:, g, :, :], YW[:, g, :, :], ALU.add)
                dve.drain()
                V.copy_predicated(YV[:, g, :, :], YM[:, g, :, :], YU[:, g, :, :])
                if g == 0:
                    dve.wait_ge(y_out[q], STORES + 16 * GRP * h)
                    V.tensor_copy(IDX[:, q, :], XR[:, q, :, TOK])
                dve.drain()
                V.tensor_tensor(YO[:, q, 2 * g:2 * g + 2, :], YV[:, g, :, :], XR[:, q, 2 * g:2 * g + 2, 0:C], ALU.add)
                dve.drain().then_inc(dve_y, 1)

            low_w1(0, 0)
            low_rows(0, 0)
            with dve.Fori(0, NT // 2) as h:
                for q in range(2):
                    t = 2 * h + q
                    for f in range(FB):
                        dve.wait_ge(act_h, CREDIT + t * FB + f + 1)
                        V.tensor_tensor(HSL[:, f, :], HSF[:, f, :], HSH[:, f, :].bitcast(F32),
                                        ALU.subtract).then_inc(dve_hl, 1)
                    low_w1(t + 1, 1 - q)
                    low_rows(t + 1, 1 - q)
                    for g in range(2):
                        outputs(t, q, g, h)

            with dve.Fori(0, NB * GROUPS // 2) as h:
                for q in range(2):
                    dve.wait_ge(pe_ot, CREDIT + 2 * h + q + 1)
                    dve.wait_ge(o_out[q], STORES + 16 * h)
                    V.tensor_copy(OB[:, q, 0, :], B[2 * q][:, :]).then_inc(dve_ot, 1)

        @block.gpsimd
        def _(pool):
            G = nc.gpsimd
            for c in pool_credit:
                pool.sem_inc(c, CREDIT)
            pool.memset(primed[:, :], 0.0)
            pool.drain()
            pool.sem_inc(pass_done["pool"], 1)
            pool.sem_inc(pool_prep, 1)
            for n, c in enumerate((*scat, *y_out, *o_out)):
                pool.dma_start(primer[n:n + 1, :], primed[0:1, :]).then_inc(c, STORES)
            prepared(pool)

            def window_pass(b):
                nm = TILES + 4

                def centre(m, k):
                    n = b * nm + m
                    pool.wait_ge(pe_gram, CREDIT + n - 3)
                    stand_alone(pool)
                    G.tensor_copy(MS[0:R, k % 4, :], FH[0:R, bass.ds(m * P + HALO, P)]).then_inc(pool_ms, 1)

                def cut(m, k):
                    pool.wait_ge(act_e, CREDIT + b * nm + m + 1)
                    stand_alone(pool)
                    G.memset(ER[0:W, k % 8, 512:512 + W], 0.0)
                    G.memset(ER[W:P, k % 8, W:2 * W], 0.0)
                    pool.drain().then_inc(pool_mask, 1)

                for m in range(4):
                    centre(m, m)
                for m in range(4):
                    cut(m, m)
                with pool.Fori(0, PAIRS // 4) as h:
                    for j in range(4):
                        m = 8 * h + 2 * j + 4
                        for t in range(2):
                            centre(m + t, 2 * j + 4 + t)
                        for t in range(2):
                            cut(m + t, 2 * j + 4 + t)

            def attention_pass(b):
                with pool.Fori(0, GROUPS // 2) as h:
                    for k in range(2 * GRP):
                        i = h * 2 * GRP + k
                        pool.wait_ge(xn_done, (b * 3 + 1) * TILES + i + 1)
                        tile = T[:, bass.ds(i, 1), 0:C].rearrange("p o c -> p (o c)")
                        G.tensor_tensor(tile, tile, BO[:, :], ALU.add).then_inc(pool_bias, 1)

            def scatter(b):
                pool.wait_ge(dve_slot, b + 1)
                for g in range(GROUPS):
                    q = g % 2
                    pool.wait_ge(scat[q], STORES + 16 * GRP * (b * (GROUPS // 2) + g // 2))
                    stand_alone(pool)
                    for k in range(GRP):
                        i = g * GRP + k
                        G.indirect_dma_start(rows, bass.IndirectOffsetOnAxis(ap=SLI[:, i:i + 1].bitcast(U32), axis=0),
                                             T[:, i, :], None, bounds_check=s["rows"] - 1, oob_is_err=False).then_inc(scat[q], 16)
                for q in range(2):
                    pool.wait_ge(scat[q], STORES + 16 * GRP * (b + 1) * (GROUPS // 2))
                stand_alone(pool)

            with pool.Fori(0, NB) as b:
                for n, stage in enumerate((None, None, window_pass, None, None, attention_pass, scatter)):
                    pass_starts(pool, "pool", b * NPASS + n)
                    if stage:
                        stage(b)
                    pass_ends(pool, "pool")

            def low_w2(t, q):
                pool.wait_ge(act_w2, CREDIT + t + 1)
                stand_alone(pool)
                G.tensor_tensor(W2L[:, q, :, :].rearrange("p a f -> p (a f)"), W2R[:, :, :].rearrange("p a f -> p (a f)"),
                                W2H[:, q, :, :].bitcast(F32).rearrange("p a f -> p (a f)"),
                                ALU.subtract).then_inc(pool_w2, 1)

            low_w2(0, 0)
            with pool.Fori(0, NT // 2) as h:
                for q in range(2):
                    t = 2 * h + q
                    low_w2(t + 1, 1 - q)
                    for k in range(GRP):
                        if k % 2 == 0:
                            pool.wait_ge(dve_y, CREDIT + t * 2 + k // 2 + 1)
                            stand_alone(pool)
                        G.indirect_dma_start(toks, bass.IndirectOffsetOnAxis(ap=IDX[:, q, k:k + 1].bitcast(U32), axis=0),
                                             YO[:, q, k, :], None, bounds_check=s["tokens"] - 1,
                                             oob_is_err=False).then_inc(y_out[q], 16)
            with pool.Fori(0, NB) as b:
                with pool.Fori(0, GROUPS // 2) as h:
                    for q in range(2):
                        pool.wait_ge(act_ot, b * GROUPS + 2 * h + q + 1 + CREDIT)
                        pool.wait_ge(dve_ot, b * GROUPS + 2 * h + q + 1 + CREDIT)
                        stand_alone(pool)
                        pool.dma_start(out_v[bass.ds(b, 1), :, :, bass.ds(h * 2 * GC + q * GC, GC)]
                                       .rearrange("o c a n -> c (o a) n"), OB[:, q, :, :]).then_inc(o_out[q], 16)
            for q in range(2):
                pool.wait_ge(o_out[q], STORES + 16 * NB * GROUPS // 2)


_INS = ["x", "L0_conv_W_reduce", "L0_conv_W_proj", "L1_attn_W_qkv", "L1_attn_W_out", "L1_attn_b_out",
        "L1_ffn_gate_w", "L1_ffn_gate_b", "L1_ffn_w1", "L1_ffn_b1", "L1_ffn_w2", "L1_ffn_b2"]


def kernel(**inputs):
    import numpy as _np
    import concourse.bacc as _bacc
    from concourse import mybir as _mybir
    from concourse.bass_utils import run_bass_kernel_spmd as _run

    nc = _bacc.Bacc("TRN2", target_bir_lowering=False, num_devices=1)
    s = sizes(inputs["x"].shape[0])
    arrays, args = {}, []
    named = [(n, _np.ascontiguousarray(inputs[n])) for n in _INS]
    named += list(zip(("konst", "band"), constants(_np, s)))
    for name, a in named:
        arrays[f"in_{name}_dram"] = a
        args.append(nc.dram_tensor(f"in_{name}_dram", a.shape, _mybir.dt.from_np(a.dtype), kind="ExternalInput").ap())
    out = nc.dram_tensor("out_0_dram", inputs["x"].shape, _mybir.dt.float32, kind="ExternalOutput").ap()
    build(nc, s, *args, out)
    r = _run(nc, [arrays], core_ids=[0])
    return r.results[0]["out_0_dram"]
```

```python
import concourse.bass as bass
from concourse import mybir
from concourse.alu_op_type import AluOpType as ALU
from contextlib import ExitStack
import math

F32 = mybir.dt.float32
F32R = mybir.dt.float32r
I32 = mybir.dt.int32
U32 = mybir.dt.uint32
ACT = mybir.ActivationFunctionType
AX = mybir.AxisListType.X

P = 128
C = 256
HALVES = C // P
R = 64
W = 64
WIN = 7
HD = 128
DH = 32
NE = 8
FF = 1024
FB = FF // P
TILES = 32
GRP = 4
GC = GRP * P
GROUPS = TILES // GRP
PAIRS = TILES // 2
HALO = 3 * W
EROW = 640
ROW = 260
NOWHERE = float(2 ** 22)
PEN = -30000.0
FMAX = 3.4028234663852886e38
CX = C + 2 * NE
STILE = 512
SHIFT, RSTD, PRB, TOK = 256, 257, 258, 259


def sizes(nb):
    tokens = nb * TILES * P
    cap = max(1, math.ceil(1.25 * tokens / NE))
    ntile = -(-(tokens + NE * (STILE - 1)) // STILE)
    ntile += ntile % 2
    cp = -(-cap // STILE) * STILE + STILE
    zero = NE * cp
    return dict(nb=nb, tokens=tokens, cap=cap, ntile=ntile, cp=cp, zero=zero, rows=zero + STILE)


K_ID, K_TRI, K_BLK, K_NPAD, K_W8, K_EB, K_TOK, K_SCAN = 0, 128, 256, 384, 416, 424, 432, 464
K_TT, K_EC, K_N = 464 + NE * 33, 464 + NE * 33 + 80, 464 + NE * 33 + 80 + 16


def constants(np, s):
    k = np.zeros((P, K_N), np.float32)
    k[:, K_ID:K_ID + P] = np.eye(P)
    k[:, K_TRI:K_TRI + P] = np.triu(np.ones((P, P)))
    head = np.arange(HD) // DH
    k[:, K_BLK:K_BLK + HD] = (head[:, None] == head[None, :]) * DH ** -0.5
    p = np.arange(P)
    for i in range(TILES):
        y, x = 2 * i + p // W, p % W
        rows = np.minimum(y + 3, 63) - np.maximum(y - 3, 0) + 1
        cols = np.minimum(x + 3, W - 1) - np.maximum(x - 3, 0) + 1
        k[:, K_NPAD + i] = WIN * WIN - rows * cols
        k[:, K_TOK + i] = i * P + p
    k[:, K_W8:K_W8 + NE] = NE - np.arange(NE)
    k[:, K_EB:K_EB + NE] = np.arange(NE) * s["cp"]
    scan = np.ones((NE, TILES + 1))
    scan[:, 0] = 0
    k[:, K_SCAN:K_SCAN + NE * 33] = scan.reshape(-1)
    k[:, K_TT:K_TT + 80] = np.arange(80)
    k[:, K_EC:K_EC + 16] = np.arange(16) * STILE
    col = np.arange(W)
    band = np.zeros((W, 2 * W), np.float32)
    band[:, 0:W] = np.where(np.abs(col[:, None] - col[None, :]) > WIN // 2, PEN, 0)
    band[:, W:] = np.eye(W)
    return k, band


def build(nc, s, x, w_reduce, w_proj, w_qkv, w_out, b_out, gate_w, gate_b, w1, b1, w2, b2, konst, band, out):
    NB, NT, CP, CAP = s["nb"], s["ntile"], s["cp"], s["cap"]
    NPASS = 7
    FHW = P * (TILES + 3) + GC
    ctx = ExitStack()
    with ctx:
        def sem(name):
            return ctx.enter_context(nc.semaphore(name))

        rows = nc.dram_tensor("routed_rows", (s["rows"], ROW), F32).ap()
        primer = nc.dram_tensor("primer", (6, 16), F32).ap()
        toks = nc.dram_tensor("token_rows", (s["tokens"], C), F32).ap()

        def sb(name, shape, dt=F32, to=None):
            return (to or ctx).enter_context(nc.sbuf_tensor(name, shape, dt))

        primed = sb("primed", [1, 16])
        KON = sb("KON", [P, K_N])
        WR = sb("WR", [P, HALVES, R])
        WRr = sb("WRr", [R, C])
        WP = sb("WP", [R, C])
        WPr = sb("WPr", [P, HALVES, R])
        WQ = sb("WQ", [P, HALVES, HD])
        WK = sb("WK", [P, HALVES, HD])
        WV = sb("WV", [P, HALVES, HD])
        WQT = sb("WQT", [HD, C])
        WO = sb("WO", [HD, C + NE])
        BG = sb("BG", [P, NE])
        CG = sb("CG", [P, NE])
        BO = sb("BO", [P, C])
        GW = sb("GW", [P, HALVES, NE])
        GB = sb("GB", [P, NE])
        B1R = sb("B1R", [NE * FB, P])
        B1T = sb("B1T", [P, NE * FB])
        ONES = sb("ONES", [P, P])
        ZEROS = sb("ZEROS", [P, C])
        CARRY = sb("CARRY", [P, NE])
        TAB = sb("TAB", [P, 3, 80])
        TABI = sb("TABI", [P, 3, 80], I32)
        NROW = sb("NROW", [P, NE])
        NROWI = sb("NROWI", [P, NE], I32)
        TCNT = sb("TCNT", [P, NE])
        TCUM = sb("TCUM", [P, NE])
        TMP8 = sb("TMP8", [P, NE, 16])
        TT8 = sb("TT8", [P, 80, NE])

        ctx_a = ExitStack()

        def sa(name, shape, dt=F32):
            return sb(name, shape, dt, ctx_a)

        XB = sa("XB", [P, 2, HALVES, GC])
        TT = sa("TT", [P, 2, TILES, ROW])
        FT = sa("FT", [P, TILES + 4, R + 1])
        FN = sa("FN", [P, 2, GRP, R])
        FH = sa("FH", [P, FHW])
        MS = sa("MS", [P, 4, P])
        ER = sa("ER", [P, 8, EROW])
        CR = sa("CR", [P, 2, 2 * (R + 1)])
        CT = sa("CT", [R, 2, 2 * P])
        RD = sa("RD", [P, 2, 2])
        DEN = sa("DEN", [P, 2, 2])
        SS = sa("SS", [P, TILES])
        SSM = sa("SSM", [P, TILES])
        NRM = sa("NRM", [P, TILES])
        RN = sa("RN", [P, TILES])
        ST = sa("ST", [P, TILES, 6])
        LN = sa("LN", [P, 6, TILES])
        NMR = sa("NMR", [P, TILES])
        XN = sa("XN", [P, 2, GRP, C])
        XT = sa("XT", [P, 2, HALVES, GC])
        KC = sa("KC", [HD, TILES * P])
        KE = sa("KE", [HD, 2, GC])
        KT = sa("KT", [P, 2, GC])
        KMX = sa("KMX", [HD, GROUPS])
        KNM = sa("KNM", [HD, 1])
        KSUM = sa("KSUM", [HD, GROUPS])
        KDEN = sa("KDEN", [HD, 1])
        KRD = sa("KRD", [HD, 1])
        GT = sa("GT", [P, HALVES, HD])
        CTM = sa("CTM", [HD, HD])
        M1 = sa("M1", [HD, C + NE])
        AW = sa("AW", [P, HALVES, CX])
        LN1 = sa("LN1", [P, 2, TILES])
        GP = sa("GP", [P, TILES, 2 * NE])
        LG = sa("LG", [P, TILES, NE])
        LX = sa("LX", [P, TILES, NE])
        EX = sa("EX", [P, TILES, NE])
        OH = sa("OH", [P, TILES, NE])
        MX = sa("MX", [P, TILES])
        SC = sa("SC", [P, NE * (TILES + 1)])
        SO = sa("SO", [P, NE * (TILES + 1)])
        POS = sa("POS", [P, 4, TILES])
        PRBS = sa("PRBS", [P, TILES])
        SLI = sa("SLI", [P, TILES], I32)
        WOT, BOT = ([XT[:, q, a, :] for a in range(HALVES)] for q in range(2))
        SQ = KC[:, 0:TILES * R].rearrange("p (i r) -> p i r", r=R)
        ctx_a.close()

        W1R = sb("W1R", [P, HALVES, FF])
        W2R = sb("W2R", [P, FB, C])
        W1H = sb("W1H", [P, 2, HALVES, FF], F32R)
        W1L = sb("W1L", [P, 2, HALVES, FF], F32R)
        W2H = sb("W2H", [P, 2, FB, C], F32R)
        W2L = sb("W2L", [P, 2, FB, C], F32R)
        B1 = sb("B1", [P, 2, FB])
        B2 = sb("B2", [P, 2, C])
        XR = sb("XR", [P, 2, GRP, ROW])
        HN = sb("HN", [P, GRP, C])
        HTH = sb("HTH", [P, 2, HALVES, GC], F32R)
        HTL = sb("HTL", [P, 2, HALVES, GC], F32R)
        HSF = sb("HSF", [P, FB, GC])
        HSH = sb("HSH", [P, FB, GC], F32R)
        HSL = sb("HSL", [P, FB, GC], F32R)
        YU = sb("YU", [P, 2, 2, C])
        YV = sb("YV", [P, 2, 2, C])
        YW = sb("YW", [P, 2, 2, C])
        YM = sb("YM", [P, 2, 2, C], U32)
        YO = sb("YO", [P, 2, GRP, C])
        IDX = sb("IDX", [P, 2, GRP], I32)
        spread = HSF[:, :, :].rearrange("p (q f) n -> p q (f n)", q=2)
        ZR = spread[:, 0, 0:GRP * ROW]
        YG = spread[:, :, 0:GRP * C].rearrange("p q (k c) -> p q k c", c=C)
        OB = spread[:, :, GRP * C:2 * GRP * C].rearrange("p q (a n) -> p q a n", a=HALVES)

        PS = ctx.enter_context(nc.psum_tensor("PS", [P, 8 * GC], F32))
        B = [PS[:, i * GC:(i + 1) * GC] for i in range(8)]

        ident = KON[:, K_ID:K_ID + P]
        tri = KON[:, K_TRI:K_TRI + P]
        blockmask = KON[:, K_BLK:K_BLK + HD]
        npad = KON[:, K_NPAD:K_NPAD + TILES]
        w8 = KON[:, K_W8:K_W8 + NE]
        ebase = KON[:, K_EB:K_EB + NE]
        tok = KON[:, K_TOK:K_TOK + TILES]
        scanmask = KON[:, K_SCAN:K_SCAN + NE * 33]
        ttab = KON[:, K_TT:K_TT + 80]
        ecnt = KON[:, K_EC:K_EC + 16]

        CREDIT = 8
        STORES = 16
        carrier = sem("carrier")
        k_in = sem("k_in")
        x_in = [sem(f"x_in{q}") for q in range(2)]
        pe_prep, dve_prep, pool_prep = sem("pe_prep"), sem("dve_prep"), sem("pool_prep")
        pass_done = {e: sem(f"pass_done_{e}") for e in ("pe", "act", "dve")}
        bank_free = sem("bank_free")
        pe_feat, act_xt, dve_feat = sem("pe_feat"), sem("act_xt"), sem("dve_feat")
        act_sq, dve_ssm, act_nrm = sem("act_sq"), sem("dve_ssm"), sem("act_nrm")
        dve_fn, pe_fh, act_fh = sem("dve_fn"), sem("pe_fh"), sem("act_fh")
        pool_ms, pe_gram, act_e, pool_mask = sem("pool_ms"), sem("pe_gram"), sem("act_e"), sem("pool_mask")
        pe_corr, dve_cr, pe_ct, act_ct, pe_proj, dve_t = (sem(n) for n in (
            "pe_corr", "dve_cr", "pe_ct", "act_ct", "pe_proj", "dve_t"))
        dve_var, act_std = sem("dve_var"), sem("act_std")
        xn_done, pe_xt, xt_high, xt_low = sem("xn_done"), sem("pe_xt"), sem("xt_high"), sem("xt_low")
        pe_k, act_kc, dve_knm = sem("pe_k"), sem("act_kc"), sem("dve_knm")
        act_cn, act_ke, pe_kt, dve_kt, pe_g = sem("act_cn"), sem("act_ke"), sem("pe_kt"), sem("dve_kt"), sem("pe_g")
        pe_fold, dve_fold = sem("pe_fold"), sem("dve_fold")
        pool_bias, pe_attn, dve_t2 = sem("pool_bias"), sem("pe_attn"), sem("dve_t2")
        dve_lx, act_ex, dve_oh, pe_count, dve_slot = (sem(n) for n in (
            "dve_lx", "act_ex", "dve_oh", "pe_count", "dve_slot"))
        scat = [sem(f"scat{q}") for q in range(2)]
        tab_done, fill = sem("tab_done"), sem("fill")
        raw_in = sem("raw_in")
        r_in = [sem(f"r_in{q}") for q in range(2)]
        y_out = [sem(f"y_out{q}") for q in range(2)]
        t_out = [sem(f"t_out{v}") for v in range(2)]
        g_in = [sem(f"g_in{q}") for q in range(2)]
        act_w1, act_w2, pool_w1, pool_w2 = sem("act_w1"), sem("act_w2"), sem("pool_w1"), sem("pool_w2")
        act_hn, pe_ht, act_ht, dve_ht, pe_h, act_h, dve_hl, pe_y, dve_yp, dve_y = (sem(n) for n in (
            "act_hn", "pe_ht", "act_ht", "dve_ht", "pe_h", "act_h", "dve_hl", "pe_y", "dve_yp", "dve_y"))
        pe_ot, act_ot, dve_ot = sem("pe_ot"), sem("act_ot"), sem("dve_ot")
        o_out = [sem(f"o_out{q}") for q in range(2)]

        pe_credit = (pe_feat, pe_fh, pe_gram, pe_corr, pe_ct, pe_proj, pe_xt, pe_k, pe_kt, pe_g, pe_attn,
                     pe_ht, pe_h, pe_y, pe_ot)
        act_credit = (act_cn, act_xt, act_sq, act_fh, act_e, act_ct, xt_high, act_kc, act_ke, act_w1, act_w2, act_hn, act_ht, act_h, act_ot)
        dve_credit = (dve_feat, dve_fn, dve_cr, dve_t, xt_low, dve_kt, dve_t2, dve_ht,
                      dve_hl, dve_yp, dve_y, dve_ot)
        pool_credit = (pool_ms, pool_mask, pool_bias, pool_w1, pool_w2)

        QUARTERS = 4

        def store_tokens(eng, b, v, h):
            part = TILES // QUARTERS
            eng.dma_start(toks[bass.ds(b * TILES * P + h * part * P, part * P), :].rearrange("(i p) c -> p i c", p=P),
                          TT[:, v, bass.ds(h * part, part), 0:C]).then_inc(t_out[v], 16)

        def stand_alone(eng):
            eng.sem_inc(carrier, 1)

        def pass_starts(eng, me, n):
            for e, done in pass_done.items():
                if e != me:
                    eng.wait_ge(done, n + 1)
            stand_alone(eng)

        def pass_ends(eng, me):
            eng.drain().then_inc(pass_done[me], 1)

        def groups(eng, item):
            with eng.Fori(0, GROUPS // 2 - 1) as h:
                for q in range(2):
                    item(2 * h + q, q, 2)
            for q in range(2):
                item(GROUPS - 2 + q, q, 1 - q)

        def prepared(eng):
            eng.wait_ge(k_in, 16 * NCONST)
            eng.wait_ge(pe_prep, 2)
            eng.wait_ge(dve_prep, 3)
            eng.wait_ge(pool_prep, 1)

        x_v = x.rearrange("b (a c) h w -> b c a (h w)", a=HALVES)
        out_v = out.rearrange("b (a c) h w -> b c a (h w)", a=HALVES)
        w1_v = w1.rearrange("e (a c) f -> e c a f", a=HALVES)
        w2_v = w2.rearrange("e (k f) c -> e f k c", f=P)

        block = ctx.enter_context(nc.Block())
        NCONST = 14

        @block.sync
        def _(sp):
            qkv = w_qkv.rearrange("(a c) f -> c a f", a=HALVES)
            sp.dma_start(KON[:, :], konst).then_inc(k_in, 16)
            sp.dma_start(WRr[:, :], w_reduce).then_inc(k_in, 16)
            sp.dma_start(B1R[:, :], b1.rearrange("e (k f) -> (e k) f", f=P)).then_inc(k_in, 16)
            sp.dma_start(WPr[:, :, :], w_proj.rearrange("(a c) r -> c a r", a=HALVES)).then_inc(k_in, 16)
            sp.dma_start(WQ[:, :, :], qkv[:, :, 0:HD]).then_inc(k_in, 16)
            sp.dma_start(WK[:, :, :], qkv[:, :, HD:2 * HD]).then_inc(k_in, 16)
            sp.dma_start(WV[:, :, :], qkv[:, :, 2 * HD:3 * HD]).then_inc(k_in, 16)
            sp.dma_start(WO[:, 0:C], w_out).then_inc(k_in, 16)
            sp.dma_start(BO[:, :], b_out.unsqueeze(0).to_broadcast([P, C])).then_inc(k_in, 16)
            sp.dma_start(GW[:, :, :], gate_w.rearrange("(a c) e -> c a e", a=HALVES)).then_inc(k_in, 16)
            sp.dma_start(GB[:, :], gate_b.unsqueeze(0).to_broadcast([P, NE])).then_inc(k_in, 16)
            sp.dma_start(FH[R:P, :].rearrange("p (n w) -> p n w", w=W),
                         band[:, 0:W].unsqueeze(1).to_broadcast([W, FHW // W, W])).then_inc(k_in, 16)
            for v in range(2):
                sp.dma_start(MS[R:P, :, v * W:(v + 1) * W],
                             band[:, W:].unsqueeze(1).to_broadcast([W, 4, W])).then_inc(k_in, 16)
            with sp.Fori(0, NB // 2) as bb:
                for v in range(2):
                    b = 2 * bb + v
                    with sp.Fori(0, GROUPS // 2) as h:
                        for q in range(2):
                            sp.wait_ge(pe_feat, b * TILES + h * 2 * GRP + (q + 1) * GRP)
                            sp.dma_start(XB[:, q, :, :], x_v[bass.ds(b, 1), :, :, bass.ds(h * 2 * GC + q * GC, GC)]
                                         .rearrange("o c a n -> c (o a) n")).then_inc(x_in[q], 16)
                    with sp.Fori(0, QUARTERS - 1) as h:
                        sp.wait_ge(dve_t2, CREDIT + b * TILES + (h + 1) * (TILES // QUARTERS))
                        store_tokens(sp, b, v, h)
            sp.wait_ge(tab_done, 1)
            for e in range(NE):
                n = sp.value_load(NROWI[0:1, e:e + 1], min_val=0, max_val=s["zero"])
                sp.dma_start(rows[bass.ds(n, STILE), :].rearrange("(p k) c -> p (k c)", p=P), ZR).then_inc(fill, 16)
            sp.dma_start(rows[s["zero"]:s["zero"] + STILE, :].rearrange("(p k) c -> p (k c)", p=P), ZR).then_inc(fill, 16)
            sp.wait_ge(fill, 16 * (NE + 1))

            def load_weights(t):
                e = sp.value_load(TABI[0:1, 0, bass.ds(t, 1)], min_val=0, max_val=NE - 1)
                for split in (act_w1, act_w2, pool_w1, pool_w2):
                    sp.wait_ge(split, CREDIT + t)
                sp.dma_start(W1R[:, :, :], w1_v[bass.ds(e, 1), :, :, :].rearrange("o c a f -> c (o a) f")).then_inc(raw_in, 16)
                sp.dma_start(W2R[:, :, :], w2_v[bass.ds(e, 1), :, :, :].rearrange("o f k c -> f (o k) c")).then_inc(raw_in, 16)

            def load_rows(t, q):
                e = sp.value_load(TABI[0:1, 0, bass.ds(t, 1)], min_val=0, max_val=NE - 1)
                r = sp.value_load(TABI[0:1, 1, bass.ds(t, 1)], min_val=0, max_val=s["zero"])
                sp.wait_ge(dve_y, CREDIT + (t - 1) * 2)
                sp.dma_start(XR[:, q, :, :], rows[bass.ds(r, STILE), :].rearrange("(p k) c -> p k c", p=P)).then_inc(r_in[q], 16)
                sp.dma_start(B1[:, q, :], B1T[:, bass.ds(e * FB, FB)]).then_inc(r_in[q], 16)
                sp.dma_start(B2[:, q, :], b2[bass.ds(e, 1), :].to_broadcast([P, C])).then_inc(r_in[q], 16)

            load_weights(0)
            load_rows(0, 0)
            load_weights(1)
            load_rows(1, 1)
            with sp.Fori(0, NT // 2) as h:
                for q in range(2):
                    t = 2 * h + q
                    load_weights(t + 2)
                    load_rows(t + 2, q)
            for q in range(2):
                sp.wait_ge(y_out[q], STORES + 16 * GRP * NT // 2)
            with sp.Fori(0, NB * GROUPS // 2) as h:
                for q in range(2):
                    sp.wait_ge(pe_ot, CREDIT + 2 * h + q - 1)
                    sp.dma_start(YG[:, q, :, :], toks[bass.ds(h * 2 * GC + q * GC, GC), :]
                                 .rearrange("(k p) c -> p k c", p=P)).then_inc(g_in[q], 16)

        @block.tensor
        def _(pe):
            mm, tr = nc.tensor.matmul, nc.tensor.transpose
            for c in pe_credit:
                pe.sem_inc(c, CREDIT)
            pe.sem_inc(pass_done["pe"], 1)
            pe.wait_ge(k_in, 16 * NCONST)
            tr(B[3][:, 0:NE * FB], B1R[:, :], ident[0:NE * FB, 0:NE * FB])
            for a in range(HALVES):
                tr(B[0][:, a * R:(a + 1) * R], WRr[:, a * P:(a + 1) * P], ident[0:R, 0:R])
                tr(B[1][0:R, a * P:(a + 1) * P], WPr[:, a, :], ident)
                tr(B[2][:, a * P:(a + 1) * P], WQ[:, a, :], ident)
                tr(B[4][:, a * P:(a + 1) * P], WO[:, a * P:(a + 1) * P], ident)
                tr(B[5][:, a * P:(a + 1) * P], BO[:, a * P:(a + 1) * P], ident)
            pe.drain().then_inc(pe_prep, 1)
            pe.wait_ge(dve_prep, 2)
            for n, lhs in enumerate((WOT, BOT, (ONES, ONES))):
                for a in range(HALVES):
                    mm(B[6][:, n * NE:(n + 1) * NE], lhs[a][:, 0:P], GW[:, a, :], start=a == 0, stop=a == 1)
            pe.drain().then_inc(pe_prep, 1)
            prepared(pe)

            def counts(b):
                pe.wait_ge(dve_oh, b + 1)
                stand_alone(pe)
                oh = OH[:, :, :].rearrange("p i e -> p (i e)")
                mm(B[7][:, 0:TILES * NE], tri, oh, start=True, stop=True)
                mm(B[7][:, TILES * NE:2 * TILES * NE], ONES[:, :], oh, start=True, stop=True).then_inc(pe_count, 1)

            def feature_pass(b, v):
                def tiles(h):
                    for k in range(2 * GRP):
                        q, sl = k // GRP, bass.ts(k % GRP, P)
                        if k == 0:
                            pe.wait_ge(bank_free, b * (GROUPS // 2) + h + 1)
                        if k % GRP == 0:
                            pe.wait_ge(x_in[q], 16 * (b * (GROUPS // 2) + h + 1))
                        if k % 2 == 0:
                            pe.wait_ge(act_xt, CREDIT + b * PAIRS + h * GRP + k // 2 - 3)
                        for a in range(HALVES):
                            mm(PS[:, bass.ds(h * GC + 4 * GC + k * R, R)], XB[:, q, a, sl], WR[:, a, :], start=a == 0, stop=a == 1)
                        for a in range(HALVES):
                            last = tr(B[k // 2][:, bass.ds((k % 2) * C + a * P, P)], XB[:, q, a, sl], ident)
                        last.then_inc(pe_feat, 1)

                tiles(0)
                counts(b)
                with pe.Fori(0, GROUPS // 2 - 1) as h:
                    tiles(h + 1)

            def map_pass(b, v):
                with pe.Fori(0, GROUPS // 2) as h:
                    for q in range(2):
                        n = b * GROUPS + 2 * h + q
                        pe.wait_ge(dve_fn, CREDIT + n + 1)
                        pe.wait_ge(act_fh, CREDIT + n - 1)
                        stand_alone(pe)
                        for k in range(GRP):
                            last = tr(B[4 + q][0:R, bass.ts(k, P)], FN[:, q, k, :], ident)
                        last.then_inc(pe_fh, 1)

            def window_pass(b, v):
                nm, npair = TILES + 4, PAIRS

                def gram(m, k):
                    n = b * nm + m
                    pe.wait_ge(pool_ms, CREDIT + n + 1)
                    pe.wait_ge(act_e, CREDIT + n - 1)
                    mm(B[k % 2][:, :], MS[:, k % 4, :], FH[:, bass.ds(m * P, GC)],
                       start=True, stop=True).then_inc(pe_gram, 1)

                def project(n, j):
                    pe.wait_ge(act_ct, CREDIT + n + 1)
                    pe.wait_ge(dve_t, CREDIT + n - 1)
                    for t in range(2):
                        last = mm(B[5 + j % 2][:, bass.ts(t, C)], CT[:, j % 2, bass.ts(t, P)], WP[:, :],
                                  start=True, stop=True)
                    last.then_inc(pe_proj, 1)

                def pairs(h, peeled):
                    for j in range(4):
                        p = 4 * h + j
                        n = b * npair + p
                        gram(2 * p + 4, 2 * j + 4)
                        gram(2 * p + 5, 2 * j + 5)
                        pe.wait_ge(pool_mask, CREDIT + b * nm + 2 * p + 4)
                        pe.wait_ge(dve_cr, CREDIT + n - 1)
                        for t in range(2):
                            for d in range(-2, 3):
                                last = mm(B[2 + j % 2][:, t * (R + 1):(t + 1) * (R + 1)],
                                          ER[:, (2 * j + t + d) % 8, 256 - P * d:256 - P * d + P],
                                          FT[:, bass.ds(2 * p + t + d + 2, 1), :].rearrange("p o c -> p (o c)"),
                                          start=d == -2, stop=d == 2)
                        last.then_inc(pe_corr, 1)
                        if j or not peeled:
                            project(n - 1, j + 1)
                        pe.wait_ge(dve_cr, CREDIT + n + 1)
                        stand_alone(pe)
                        for t in range(2):
                            last = tr(B[4][0:R, bass.ts(t, P)], CR[:, j % 2, t * (R + 1):t * (R + 1) + R], ident)
                        last.then_inc(pe_ct, 1)

                for m in range(4):
                    gram(m, m)
                pairs(0, True)
                with pe.Fori(0, PAIRS // 4 - 1) as h:
                    pairs(h + 1, False)
                project(b * npair + PAIRS - 1, 3)

            def normed_to_channels(n, q):
                for k in range(GRP):
                    pe.wait_ge(xn_done, n * GRP + k + 1)
                    if k == 0:
                        pe.wait_ge(xt_high, CREDIT + n - 1)
                        pe.wait_ge(xt_low, CREDIT + n - 1)
                    for a in range(HALVES):
                        last = tr(B[2 * q + a][:, bass.ts(k, P)], XN[:, q, k, bass.ts(a, P)], ident)
                last.then_inc(pe_xt, 1)

            def channels_ready(n):
                pe.wait_ge(xt_high, CREDIT + n + 1)
                pe.wait_ge(xt_low, CREDIT + n + 1)

            def key_pass(b, v):
                first = b * 2 * GROUPS

                def keys(g, q, left):
                    if left:
                        normed_to_channels(first + g + 1, 1 - q)
                    channels_ready(first + g)
                    pe.wait_ge(act_kc, CREDIT + b * GROUPS + g - 1)
                    for a in range(HALVES):
                        last = mm(B[4 + q][:, :], WK[:, a, :], XT[:, q, a, :], start=a == 0, stop=a == 1)
                    last.then_inc(pe_k, 1)

                normed_to_channels(first, 0)
                groups(pe, keys)

            def context_pass(b, v):
                mm(B[6][:, 0:HALVES * HD], ZEROS[:, 0:P], ZEROS[:, :], start=True, stop=False, skip_group_check=True)

                def weights(g, q):
                    n = b * GROUPS + g
                    pe.wait_ge(act_ke, CREDIT + n + 1)
                    pe.wait_ge(dve_kt, CREDIT + n - 1)
                    for k in range(GRP):
                        last = tr(B[q][:, bass.ts(k, P)], KE[:, q, bass.ts(k, P)], ident)
                    last.then_inc(pe_kt, 1)

                def sums(g, q, left):
                    if left:
                        weights(g + 1, 1 - q)
                    pe.wait_ge(dve_kt, CREDIT + b * GROUPS + g + 1)
                    pe.wait_ge(act_cn, CREDIT + b * GROUPS + g + 1)
                    for k in range(GRP):
                        for a in range(HALVES):
                            last = mm(B[6][:, bass.ts(a, HD)], XN[:, q, k, bass.ts(a, P)], KT[:, q, bass.ts(k, P)],
                                      start=False, stop=False, skip_group_check=True)
                    last.then_inc(pe_g, 1)

                weights(0, 0)
                groups(pe, sums)
                pe.wait_ge(dve_fold, 4 * b + 1)
                for a in range(HALVES):
                    last = mm(B[4][:, 0:HD], WV[:, a, :], GT[:, a, :], start=a == 0, stop=a == 1)
                last.then_inc(pe_fold, 1)
                normed_to_channels(b * 2 * GROUPS + GROUPS, 0)
                pe.wait_ge(dve_fold, 4 * b + 2)
                mm(B[5][:, 0:C + NE], CTM[:, :], WO[:, :], start=True, stop=True).then_inc(pe_fold, 1)
                pe.wait_ge(dve_fold, 4 * b + 3)
                for a in range(HALVES):
                    last = mm(B[(7, 4)[a]][:, 0:C + NE], WQT[:, bass.ts(a, P)], M1[:, :], start=True, stop=True)
                last.then_inc(pe_fold, 1)

            def attention_pass(b, v):
                first = b * 2 * GROUPS + GROUPS

                def attention(g, q, left):
                    if left:
                        normed_to_channels(first + g + 1, 1 - q)
                    channels_ready(first + g)
                    for k in range(GRP):
                        pe.wait_ge(dve_t2, CREDIT + b * TILES + g * GRP + k - 3)
                        for a in range(HALVES):
                            last = mm(B[4 + k][:, 0:CX], XT[:, q, a, bass.ts(k, P)],
                                      AW[:, a, :], start=a == 0, stop=a == 1)
                        last.then_inc(pe_attn, 1)

                pe.wait_ge(dve_fold, 4 * b + 4)
                stand_alone(pe)
                groups(pe, attention)

            with pe.Fori(0, NB // 2) as bb:
                for v in range(2):
                    for n, stage in enumerate((feature_pass, map_pass, window_pass, key_pass, context_pass,
                                               attention_pass)):
                        if n not in (0, 5):
                            pass_starts(pe, "pe", (2 * bb + v) * NPASS + n)
                        stage(2 * bb + v, v)
                        pass_ends(pe, "pe")
                    pass_ends(pe, "pe")
            counts(NB)

            def rows_to_channels(t, q):
                pe.wait_ge(act_hn, CREDIT + t + 1)
                pe.wait_ge(act_ht, CREDIT + t)
                pe.wait_ge(dve_ht, CREDIT + t)
                for k in range(GRP):
                    for a in range(HALVES):
                        last = tr(B[a][:, bass.ts(k, P)], HN[:, k, bass.ts(a, P)], ident)
                last.then_inc(pe_ht, 1)

            def split_product(out, terms, first, last):
                for n, (a, b) in enumerate(terms):
                    r = mm(out, a, b, start=first and n == 0, stop=last and n == len(terms) - 1)
                return r

            rows_to_channels(0, 0)
            with pe.Fori(0, NT // 2) as h:
                for q in range(2):
                    t = 2 * h + q
                    pe.wait_ge(act_w1, CREDIT + t + 1)
                    pe.wait_ge(pool_w1, CREDIT + t + 1)
                    pe.wait_ge(act_ht, CREDIT + t + 1)
                    pe.wait_ge(dve_ht, CREDIT + t + 1)
                    for f in range(FB):
                        pe.wait_ge(act_h, CREDIT + t * FB + f - 3)
                        for a in range(HALVES):
                            wh, wl = W1H[:, q, a, bass.ts(f, P)], W1L[:, q, a, bass.ts(f, P)]
                            last = split_product(B[(2, 3, 4, 7)[f % 4]][:, :],
                                                 ((wh, HTH[:, q, a, :]), (wh, HTL[:, q, a, :]), (wl, HTH[:, q, a, :])),
                                                 a == 0, a == HALVES - 1)
                        last.then_inc(pe_h, 1)
                    for k in range(GRP):
                        if k == 2:
                            rows_to_channels(t + 1, 1 - q)
                        if k % 2 == 0:
                            pe.wait_ge(dve_yp, CREDIT + 2 * t + k // 2 - 1)
                        if k == 0:
                            pe.wait_ge(act_w2, CREDIT + t + 1)
                            pe.wait_ge(pool_w2, CREDIT + t + 1)
                        for f in range(FB):
                            if k == 0:
                                pe.wait_ge(dve_hl, CREDIT + t * FB + f + 1)
                            hh, hl = HSH[:, f, bass.ts(k, P)], HSL[:, f, bass.ts(k, P)]
                            last = split_product(B[5 + k // 2][:, bass.ts(k % 2, C)],
                                                 ((hh, W2H[:, q, f, :]), (hh, W2L[:, q, f, :]), (hl, W2H[:, q, f, :])),
                                                 f == 0, f == FB - 1)
                        if k % 2 == 1:
                            last.then_inc(pe_y, 1)

            with pe.Fori(0, NB * GROUPS // 2) as h:
                for q in range(2):
                    n = 2 * h + q
                    pe.wait_ge(act_ot, CREDIT + n - 1)
                    pe.wait_ge(dve_ot, CREDIT + n - 1)
                    pe.wait_ge(g_in[q], 16 * (h + 1))
                    for k in range(GRP):
                        for a in range(HALVES):
                            last = tr(B[2 * q + a][:, bass.ts(k, P)], YG[:, q, k, bass.ts(a, P)], ident)
                    last.then_inc(pe_ot, 1)

        @block.scalar
        def _(act):
            A = nc.scalar.activation
            for c in act_credit:
                act.sem_inc(c, CREDIT)
            act.sem_inc(pass_done["act"], 1)
            for c in t_out:
                act.sem_inc(c, STORES)
            prepared(act)

            def feature_pass(b, v):
                act.wait_ge(t_out[v], STORES + 8 * QUARTERS * (b - v))
                stand_alone(act)
                with act.Fori(0, GROUPS // 2) as h:
                    for k in range(GRP):
                        i = h * 2 * GRP + 2 * k
                        act.wait_ge(pe_feat, CREDIT + b * TILES + i + 2)
                        A(TT[:, v, bass.ds(i, 2), 0:C], B[k].rearrange("p (o c) -> p o c", c=C),
                          ACT.Copy).then_inc(act_xt, 1)
                with act.Fori(0, GROUPS // 2) as h:
                    act.wait_ge(dve_feat, CREDIT + b * (GROUPS // 2) + h + 1)
                    A(SQ[:, bass.ds(h * 2 * GRP, 2 * GRP), :], FT[:, bass.ds(h * 2 * GRP + 2, 2 * GRP), 0:R],
                      ACT.Square).then_inc(act_sq, 1)
                act.wait_ge(dve_ssm, b + 1)
                A(NRM[:, :], SSM[:, :], ACT.Sqrt).then_inc(act_nrm, 1)

            def map_pass(b, v):
                with act.Fori(0, GROUPS // 2) as h:
                    for q in range(2):
                        act.wait_ge(pe_fh, CREDIT + b * GROUPS + 2 * h + q + 1)
                        A(FH[0:R, bass.ds(h * 2 * GC + q * GC + HALO, GC)], B[4 + q][0:R, :], ACT.Copy).then_inc(act_fh, 1)

            def window_pass(b, v):
                nm = TILES + 4

                def weights(m, k):
                    act.wait_ge(pe_gram, CREDIT + b * nm + m + 1)
                    A(ER[:, k % 8, W:W + GC], B[k % 2][:, :], ACT.Exp).then_inc(act_e, 1)

                for m in range(4):
                    weights(m, m)
                with act.Fori(0, PAIRS // 4) as h:
                    for j in range(4):
                        p = 4 * h + j
                        act.wait_ge(pe_corr, CREDIT + b * PAIRS + p)
                        weights(2 * p + 4, 2 * j + 4)
                        weights(2 * p + 5, 2 * j + 5)
                        act.wait_ge(pe_ct, CREDIT + b * PAIRS + p + 1)
                        act.wait_ge(pe_proj, CREDIT + b * PAIRS + p - 1)
                        A(CT[:, j % 2, :], B[4][0:R, 0:2 * P], ACT.Copy).then_inc(act_ct, 1)
                act.wait_ge(dve_var, 2 * b + 1)
                A(LN[:, 4, :], LN[:, 3, :], ACT.Sqrt).then_inc(act_std, 1)

            def to_xt(n, q, a, copied):
                act.wait_ge(pe_xt, CREDIT + n + 1)
                A(XT[:, q, a, :], B[2 * q + a][:, :], ACT.Copy).then_inc(copied, 1)

            def both_halves(n, q):
                to_xt(n, q, 0, xt_low)
                to_xt(n, q, 1, xt_high)

            def normed(v, g, q, k):
                i = g * GRP + k
                return A(XN[:, q, k, :], TT[:, v, bass.ds(i, 1), 0:C].rearrange("p o c -> p (o c)"), ACT.Identity,
                         bias=NMR[:, bass.ds(i, 1)], scale=LN[:, 5, bass.ds(i, 1)])

            def key_pass(b, v):
                first = b * 2 * GROUPS

                def keys(g, q, left):
                    if left:
                        both_halves(first + g + 1, 1 - q)
                    act.wait_ge(pe_k, CREDIT + b * GROUPS + g + 1)
                    A(KC[:, bass.ds(g * GC, GC)], B[4 + q][:, :], ACT.Copy).then_inc(act_kc, 1)

                both_halves(first, 0)
                groups(act, keys)

            def context_pass(b, v):
                act.wait_ge(dve_knm, b + 1)
                stand_alone(act)

                def weights(g, q):
                    act.wait_ge(pe_kt, CREDIT + b * GROUPS + g - 1)
                    A(KE[:, q, :], KC[:, bass.ds(g * GC, GC)], ACT.Exp, bias=KNM[:, :],
                      accum_out=KSUM[:, bass.ds(g, 1)]).then_inc(act_ke, 1)

                def tiles(g, q, left):
                    if left:
                        weights(g + 1, 1 - q)
                    act.wait_ge(pe_g, CREDIT + b * GROUPS + g - 1)
                    normed(v, g, q, 2)
                    normed(v, g, q, 3)
                    act.drain().then_inc(act_cn, 1)

                weights(0, 0)
                groups(act, tiles)

            def attention_pass(b, v):
                first = b * 2 * GROUPS + GROUPS

                def norm(g, q):
                    act.wait_ge(pe_xt, CREDIT + first + g - 1)
                    if isinstance(g, int):
                        act.wait_ge(pe_g, CREDIT + b * GROUPS + GROUPS - 1 + g)
                    for k in range(GRP):
                        normed(v, g, q, k).then_inc(xn_done, 1)

                def tiles(g, q, left):
                    if left:
                        to_xt(first + g + 1, 1 - q, 1, xt_high)
                    if left > 1:
                        norm(g + 2, q)

                norm(0, 0)
                norm(1, 1)
                to_xt(first, 0, 1, xt_high)
                groups(act, tiles)
                act.wait_ge(dve_var, 2 * b + 2)
                A(LN[:, 4, :], LN[:, 3, :], ACT.Sqrt).then_inc(act_std, 1)

            def routing_pass(b, v):
                act.wait_ge(dve_lx, b + 1)
                A(EX[:, :, :].rearrange("p i e -> p (i e)"), LX[:, :, :].rearrange("p i e -> p (i e)"),
                  ACT.Exp).then_inc(act_ex, 1)
                store_tokens(act, b, v, QUARTERS - 1)

            with act.Fori(0, NB // 2) as bb:
                for v in range(2):
                    for n, stage in enumerate((feature_pass, map_pass, window_pass, key_pass, context_pass,
                                               attention_pass, routing_pass)):
                        if n not in (0, 5):
                            pass_starts(act, "act", (2 * bb + v) * NPASS + n)
                        stage(2 * bb + v, v)
                        pass_ends(act, "act")

            def high_part(out, raw, done, used, n):
                act.wait_ge(used, n)
                A(out, raw, ACT.Copy).then_inc(done, 1)

            def normed_rows(t, q):
                act.wait_ge(r_in[q], 48 * (t // 2 + 1) if isinstance(t, int) else 24 * (t + 2 - q))
                act.wait_ge(pe_ht, CREDIT + t)
                for k in range(GRP):
                    last = A(HN[:, k, :], XR[:, q, k, 0:C], ACT.Identity, bias=XR[:, q, k, SHIFT:SHIFT + 1],
                             scale=XR[:, q, k, RSTD:RSTD + 1])
                act.drain().then_inc(act_hn, 1)

            def high_w1(t, q):
                act.wait_ge(raw_in, 32 * (t + 1))
                high_part(W1H[:, q, :, :].rearrange("p a f -> p (a f)"), W1R[:, :, :].rearrange("p a f -> p (a f)"),
                          act_w1, pe_h, CREDIT + (t - 1) * FB)

            def high_w2(t, q):
                high_part(W2H[:, q, :, :].rearrange("p a f -> p (a f)"), W2R[:, :, :].rearrange("p a f -> p (a f)"),
                          act_w2, pe_y, CREDIT + (t - 1) * 2)

            def high_rows(t, q):
                act.wait_ge(pe_ht, CREDIT + t + 1)
                for a in range(HALVES):
                    A(HTH[:, q, a, :], B[a][:, :], ACT.Copy)
                act.drain().then_inc(act_ht, 1)

            high_w1(0, 0)
            normed_rows(0, 0)
            high_rows(0, 0)
            high_w2(0, 0)
            with act.Fori(0, NT // 2) as h:
                for q in range(2):
                    t = 2 * h + q
                    for f in range(FB):
                        act.wait_ge(pe_h, CREDIT + t * FB + f + 1)
                        bank = B[(2, 3, 4, 7)[f % 4]][:, :]
                        A(HSF[:, f, :], bank, ACT.Relu, bias=B1[:, q, f:f + 1])
                        A(HSH[:, f, :], bank, ACT.Relu, bias=B1[:, q, f:f + 1]).then_inc(act_h, 1)
                    high_w1(t + 1, 1 - q)
                    normed_rows(t + 1, 1 - q)
                    high_rows(t + 1, 1 - q)
                    high_w2(t + 1, 1 - q)

            with act.Fori(0, NB * GROUPS // 2) as h:
                for q in range(2):
                    act.wait_ge(pe_ot, CREDIT + 2 * h + q + 1)
                    act.wait_ge(o_out[q], STORES + 16 * h)
                    A(OB[:, q, 1, :], B[2 * q + 1][:, :], ACT.Copy).then_inc(act_ot, 1)

        @block.vector
        def _(dve):
            V = nc.vector
            for c in dve_credit:
                dve.sem_inc(c, CREDIT)
            dve.sem_inc(pass_done["dve"], 1)
            dve.sem_inc(bank_free, GROUPS // 2)
            V.memset(ONES[:, :], 1.0)
            V.memset(ZEROS[:, :], 0.0)
            V.memset(FT[:, :, :], 0.0)
            V.memset(FH[0:R, :], 0.0)
            V.memset(ER[:, :, :], 0.0)
            V.memset(CARRY[:, :], 0.0)
            V.memset(OH[:, :, :], 0.0)
            V.memset(TT[:, :, :, C:ROW], 0.0)
            dve.drain()
            V.memset(FT[:, 2:TILES + 2, R:R + 1], 1.0)
            dve.drain().then_inc(dve_prep, 1)
            dve.sem_inc(dve_oh, 1)
            dve.wait_ge(k_in, 16 * NCONST)
            dve.wait_ge(pe_prep, 1)
            V.tensor_copy(WR[:, :, :].rearrange("p a r -> p (a r)"), B[0][:, 0:HALVES * R])
            V.tensor_copy(WP[:, :], B[1][0:R, 0:C])
            V.tensor_copy(WQT[:, :], B[2][:, 0:C])
            V.tensor_copy(B1T[:, :], B[3][:, 0:NE * FB])
            for a in range(HALVES):
                V.tensor_copy(WOT[a][:, 0:P], B[4][:, a * P:(a + 1) * P])
                V.tensor_copy(BOT[a][:, 0:P], B[5][:, a * P:(a + 1) * P])
                V.tensor_copy(AW[:, a, C + NE:CX], GW[:, a, :])
            dve.drain().then_inc(dve_prep, 1)
            dve.wait_ge(pe_prep, 2)
            V.tensor_copy(WO[:, C:C + NE], B[6][:, 0:NE])
            V.tensor_copy(BG[:, :], B[6][:, NE:2 * NE])
            V.tensor_copy(CG[:, :], B[6][:, 2 * NE:3 * NE])
            dve.drain().then_inc(dve_prep, 1)
            prepared(dve)

            def tile_of(v, i):
                return TT[:, v, bass.ds(i, 1), 0:C].rearrange("p o c -> p (o c)")

            def feature_pass(b, v):
                with dve.Fori(0, GROUPS // 2) as h:
                    i = h * 2 * GRP
                    dve.wait_ge(pe_feat, CREDIT + b * TILES + i + 2 * GRP)
                    V.tensor_copy(FT[:, bass.ds(i + 2, 2 * GRP), 0:R],
                                  PS[:, bass.ds(h * GC + 4 * GC, GC)].rearrange("p (i r) -> p i r", r=R)).then_inc(dve_feat, 1)
                with dve.Fori(0, GROUPS // 2) as h:
                    dve.wait_ge(act_sq, CREDIT + b * (GROUPS // 2) + h + 1)
                    V.reduce_sum(SS[:, bass.ds(h * 2 * GRP, 2 * GRP)], SQ[:, bass.ds(h * 2 * GRP, 2 * GRP), :], AX)
                dve.drain()
                V.tensor_scalar_max(SSM[:, :], SS[:, :], 1e-16).then_inc(dve_ssm, 1)
                dve.wait_ge(act_nrm, b + 1)
                V.reciprocal(RN[:, :], NRM[:, :])
                dve.drain()

            def map_pass(b, v):
                with dve.Fori(0, GROUPS // 2) as h:
                    for q in range(2):
                        dve.wait_ge(pe_fh, CREDIT + b * GROUPS + 2 * h + q - 1)
                        i = h * 2 * GRP + q * GRP
                        V.tensor_tensor(FN[:, q, :, :], FT[:, bass.ds(i + 2, GRP), 0:R],
                                        RN[:, bass.ds(i, GRP)].unsqueeze(2).to_broadcast([P, GRP, R]),
                                        ALU.mult).then_inc(dve_fn, 1)

            def statistics(b, which):
                eps = 1e-5
                dve.drain()
                V.tensor_tensor(LN[:, 0, :], ST[:, :, 1], ST[:, :, 4], ALU.add)
                V.tensor_tensor(LN[:, 1, :], ST[:, :, 1], ST[:, :, 4], ALU.subtract)
                V.tensor_tensor(LN[:, 2, :], ST[:, :, 2], ST[:, :, 5], ALU.add)
                dve.drain()
                V.scalar_tensor_tensor(LN[:, 1, :], LN[:, 1, :], 0.25, LN[:, 1, :], ALU.mult, ALU.mult)
                V.tensor_scalar(LN[:, 2, :], LN[:, 2, :], 1.0 / C, eps, ALU.mult, ALU.add)
                V.tensor_scalar_mul(LN[:, 0, :], LN[:, 0, :], 0.5)
                dve.drain()
                V.tensor_tensor(LN[:, 3, :], LN[:, 1, :], LN[:, 2, :], ALU.add).then_inc(dve_var, 1)
                dve.wait_ge(act_std, 2 * b + which + 1)
                V.reciprocal(LN[:, 5, :], LN[:, 4, :])
                dve.drain()
                V.scalar_tensor_tensor(NMR[:, :], LN[:, 0, :], -1.0, LN[:, 5, :], ALU.mult, ALU.mult)
                dve.drain()

            def window_pass(b, v):
                def finish(p, j):
                    dve.wait_ge(pe_proj, CREDIT + b * PAIRS + p + 1)
                    for t in range(2):
                        i = 2 * p + t
                        V.scalar_tensor_tensor(tile_of(v, i), B[5 + j % 2][:, bass.ts(t, C)], RD[:, j % 2, t:t + 1],
                                               tile_of(v, i), ALU.mult, ALU.add)
                    dve.drain().then_inc(dve_t, 1)
                    for t in range(2):
                        i = 2 * p + t
                        V.bn_stats(ST[:, bass.ds(i, 1), :].rearrange("p o c -> p (o c)"), tile_of(v, i))

                def pairs(h, peeled):
                    for j in range(4):
                        p = 4 * h + j
                        n = b * PAIRS + p
                        dve.wait_ge(pe_corr, CREDIT + n + 1)
                        dve.wait_ge(pe_ct, CREDIT + n - 1)
                        V.tensor_copy(CR[:, j % 2, :], B[2 + j % 2][:, 0:2 * (R + 1)]).then_inc(dve_cr, 1)
                        dve.drain()
                        V.tensor_tensor(DEN[:, j % 2, :],
                                        CR[:, j % 2, :].rearrange("p (t c) -> p t c", t=2)[:, :, R],
                                        npad[:, bass.ds(2 * p, 2)], ALU.add)
                        dve.drain()
                        V.reciprocal(RD[:, j % 2, :], DEN[:, j % 2, :])
                        if j or not peeled:
                            finish(p - 1, j + 1)

                pairs(0, True)
                with dve.Fori(0, PAIRS // 4 - 1) as h:
                    pairs(h + 1, False)
                finish(PAIRS - 1, 3)
                statistics(b, 0)

            def norm(v, g, q, tiles=GRP):
                for k in range(tiles):
                    i = g * GRP + k
                    last = V.tensor_scalar(XN[:, q, k, :], tile_of(v, i), LN[:, 0, bass.ds(i, 1)], LN[:, 5, bass.ds(i, 1)],
                                           ALU.subtract, ALU.mult)
                    if tiles == GRP:
                        last.then_inc(xn_done, 1)

            def key_pass(b, v):
                first = b * 2 * GROUPS

                def tiles(g, q, left):
                    if left > 1:
                        dve.wait_ge(pe_xt, CREDIT + first + g + 1)
                        norm(v, g + 2, q)
                    dve.wait_ge(act_kc, CREDIT + b * GROUPS + g + 1)
                    V.reduce_max(KMX[:, bass.ds(g, 1)], KC[:, bass.ds(g * GC, GC)], AX)

                norm(v, 0, 0)
                norm(v, 1, 1)
                groups(dve, tiles)
                dve.drain()
                V.reduce_max(KNM[:, :], KMX[:, :], AX)
                dve.drain()
                V.tensor_scalar_mul(KNM[:, :], KNM[:, :], -1.0).then_inc(dve_knm, 1)

            def context_pass(b, v):
                with dve.Fori(0, GROUPS // 2) as h:
                    for q in range(2):
                        n = b * GROUPS + 2 * h + q
                        dve.wait_ge(pe_g, CREDIT + n - 1)
                        norm(v, 2 * h + q, q, 2)
                        dve.wait_ge(pe_kt, CREDIT + n + 1)
                        V.tensor_copy(KT[:, q, :], B[q][:, :])
                        dve.drain().then_inc(dve_kt, 1)
                dve.wait_ge(pe_g, CREDIT + (b + 1) * GROUPS)
                V.tensor_copy(GT[:, :, :].rearrange("p a d -> p (a d)"), B[6][:, 0:HALVES * HD]).then_inc(dve_fold, 1)
                dve.wait_ge(act_ke, CREDIT + (b + 1) * GROUPS)
                V.reduce_sum(KDEN[:, :], KSUM[:, :], AX)
                dve.drain()
                V.reciprocal(KRD[:, :], KDEN[:, :])
                dve.wait_ge(pe_fold, 3 * b + 1)
                V.tensor_tensor(CTM[:, :], B[4][:, 0:HD], blockmask, ALU.mult).then_inc(dve_fold, 1)
                dve.drain()
                dve.wait_ge(pe_fold, 3 * b + 2)
                V.tensor_scalar_mul(M1[:, :], B[5][:, 0:C + NE], KRD[:, :]).then_inc(dve_fold, 1)
                dve.wait_ge(pe_fold, 3 * b + 3)
                for a in range(HALVES):
                    V.tensor_copy(AW[:, a, 0:C + NE], B[(7, 4)[a]][:, 0:C + NE])
                dve.drain().then_inc(dve_fold, 1)

            def attention_pass(b, v):
                first = b * 2 * GROUPS + GROUPS

                def to_xt(n, q):
                    dve.wait_ge(pe_xt, CREDIT + n + 1)
                    V.tensor_copy(XT[:, q, 0, :], B[2 * q][:, :]).then_inc(xt_low, 1)

                def tiles(g, q, left):
                    if left:
                        to_xt(first + g + 1, 1 - q)
                    for k in range(GRP):
                        i = g * GRP + k
                        dve.wait_ge(pe_attn, CREDIT + b * TILES + i + 1)
                        V.tensor_copy(GP[:, bass.ds(i, 1), :].rearrange("p o e -> p (o e)"), B[4 + k][:, C:CX])
                        dve.wait_ge(pool_bias, CREDIT + b * TILES + i + 1)
                        V.tensor_tensor(tile_of(v, i), B[4 + k][:, 0:C], tile_of(v, i), ALU.add).then_inc(dve_t2, 1)
                        if k % 2 == 1:
                            dve.drain()
                            for j in (i - 1, i):
                                V.bn_stats(ST[:, bass.ds(j, 1), :].rearrange("p o c -> p (o c)"), tile_of(v, j))

                V.tensor_copy(LN1[:, 0, :], LN[:, 0, :])
                V.tensor_copy(LN1[:, 1, :], LN[:, 4, :])
                to_xt(first, 0)
                groups(dve, tiles)
                statistics(b, 1)

            def routing_pass(b, v):
                dve.sem_inc(bank_free, 3)
                wide = [P, TILES, NE]

                def by_token(a):
                    return a.unsqueeze(2).to_broadcast(wide)

                def by_expert(a):
                    return a.unsqueeze(1).to_broadcast(wide)

                V.tensor_tensor(LG[:, :, :], GP[:, :, NE:2 * NE], by_token(LN1[:, 1, :]), ALU.mult)
                V.tensor_tensor(LN1[:, 0, :], LN1[:, 0, :], LN[:, 0, :], ALU.subtract)
                dve.drain()
                V.tensor_tensor(LG[:, :, :], LG[:, :, :], GP[:, :, 0:NE], ALU.add)
                V.tensor_tensor(LX[:, :, :], by_token(LN1[:, 0, :]), by_expert(CG[:, :]), ALU.mult)
                dve.drain()
                V.tensor_tensor(LG[:, :, :], LG[:, :, :], by_expert(BG[:, :]), ALU.add)
                dve.drain()
                V.tensor_tensor(LG[:, :, :], LG[:, :, :], LX[:, :, :], ALU.add)
                dve.drain()
                V.tensor_tensor(LG[:, :, :], LG[:, :, :], by_token(LN[:, 5, :]), ALU.mult)
                dve.drain()
                V.tensor_tensor(LG[:, :, :], LG[:, :, :], by_expert(GB[:, :]), ALU.add)
                dve.drain()
                V.reduce_max(MX[:, :], LG[:, :, :], AX)
                dve.drain()
                top = MX[:, :].unsqueeze(2).to_broadcast(wide)
                V.tensor_tensor(LX[:, :, :], LG[:, :, :], top, ALU.subtract).then_inc(dve_lx, 1)
                V.tensor_tensor(OH[:, :, :], LG[:, :, :], top, ALU.is_ge)
                dve.drain()
                V.tensor_tensor(LG[:, :, :], OH[:, :, :], w8.unsqueeze(1).to_broadcast(wide), ALU.mult)
                dve.drain()
                V.reduce_max(MX[:, :], LG[:, :, :], AX)
                dve.drain()
                V.tensor_tensor(OH[:, :, :], LG[:, :, :], top, ALU.is_equal).then_inc(dve_oh, 1)
                dve.wait_ge(act_ex, b + 1)
                V.reduce_sum(PRBS[:, :], EX[:, :, :], AX)
                dve.drain()
                V.reciprocal(TT[:, v, :, PRB], PRBS[:, :])
                V.tensor_copy(TT[:, v, :, SHIFT], NMR[:, :])
                V.tensor_copy(TT[:, v, :, RSTD], LN[:, 5, :])
                sc = SC[:, :].rearrange("p (e j) -> p e j", e=NE)
                so = SO[:, :].rearrange("p (e j) -> p e j", e=NE)
                V.tensor_copy(sc[:, :, 0], CARRY[:, :])
                dve.wait_ge(pe_count, b + 2)
                V.tensor_copy(sc[:, :, 1:TILES + 1], B[7][:, TILES * NE:2 * TILES * NE].rearrange("p (i e) -> p e i", e=NE))
                dve.drain()
                V.tensor_tensor_scan(SO[:, :], scanmask, SC[:, :], 0.0, ALU.mult, ALU.add)
                dve.drain()
                V.tensor_copy(CARRY[:, :], so[:, :, TILES])
                V.tensor_tensor(LX[:, :, :], B[7][:, 0:TILES * NE].rearrange("p (i e) -> p i e", e=NE),
                                so[:, :, 0:TILES].rearrange("p e i -> p i e"), ALU.add)
                dve.drain().then_inc(bank_free, 1)
                V.tensor_tensor(LX[:, :, :], LX[:, :, :], OH[:, :, :], ALU.mult)
                V.tensor_tensor(LG[:, :, :], OH[:, :, :], ebase.unsqueeze(1).to_broadcast(wide), ALU.mult)
                dve.drain()
                V.reduce_sum(POS[:, 0, :], LX[:, :, :], AX)
                V.reduce_sum(POS[:, 1, :], LG[:, :, :], AX)
                dve.drain()
                V.tensor_scalar(POS[:, 2, :], POS[:, 0, :], float(CAP) + 0.5, None, ALU.is_lt)
                V.scalar_tensor_tensor(POS[:, 3, :], POS[:, 0, :], -1.0, POS[:, 1, :], ALU.add, ALU.add)
                dve.drain()
                V.tensor_scalar_add(POS[:, 3, :], POS[:, 3, :], -NOWHERE)
                dve.drain()
                V.tensor_tensor(POS[:, 3, :], POS[:, 3, :], POS[:, 2, :], ALU.mult)
                dve.drain()
                V.tensor_scalar_add(POS[:, 3, :], POS[:, 3, :], NOWHERE)
                dve.drain()
                V.tensor_copy(SLI[:, :], POS[:, 3, :])
                V.tensor_copy(TT[:, v, :, TOK], tok)
                dve.drain()
                V.tensor_scalar_add(tok, tok, float(TILES * P))
                dve.drain().then_inc(dve_slot, 1)

            with dve.Fori(0, NB // 2) as bb:
                for v in range(2):
                    for n, stage in enumerate((feature_pass, map_pass, window_pass, key_pass, context_pass,
                                               attention_pass, routing_pass)):
                        if n not in (0, 5):
                            pass_starts(dve, "dve", (2 * bb + v) * NPASS + n)
                        stage(2 * bb + v, v)
                        pass_ends(dve, "dve")

            V.tensor_scalar_min(NROW[:, :], CARRY[:, :], float(CAP))
            dve.drain()
            V.tensor_tensor(TMP8[:, :, :], NROW[:, :].unsqueeze(2).to_broadcast([P, NE, 16]),
                            ecnt.unsqueeze(1).to_broadcast([P, NE, 16]), ALU.is_gt)
            dve.drain()
            V.reduce_sum(TCNT[:, :], TMP8[:, :, :], AX)
            V.tensor_tensor(NROW[:, :], NROW[:, :], ebase, ALU.add)
            dve.drain()
            V.tensor_copy(NROWI[:, :], NROW[:, :])
            V.tensor_tensor_scan(TCUM[:, :], ONES[:, 0:NE], TCNT[:, :], 0.0, ALU.mult, ALU.add)
            dve.drain()
            V.tensor_tensor(TT8[:, :, :], ttab.unsqueeze(2).to_broadcast([P, 80, NE]),
                            TCUM[:, :].unsqueeze(1).to_broadcast([P, 80, NE]), ALU.is_ge)
            V.tensor_scalar(TCNT[:, :], TCNT[:, :], -float(STILE), float(CP), ALU.mult, ALU.add)
            dve.drain()
            V.reduce_sum(TAB[:, 0, :], TT8[:, :, :], AX)
            V.tensor_copy(TAB[:, 1, :], TT8[:, :, NE - 1])
            dve.drain()
            V.tensor_tensor(TT8[:, :, :], TT8[:, :, :], TCNT[:, :].unsqueeze(1).to_broadcast([P, 80, NE]), ALU.mult)
            dve.drain()
            V.reduce_sum(TAB[:, 2, :], TT8[:, :, :], AX)
            V.tensor_scalar_min(TAB[:, 0, :], TAB[:, 0, :], float(NE - 1))
            dve.drain()
            V.scalar_tensor_tensor(TAB[:, 2, :], ttab, float(STILE), TAB[:, 2, :], ALU.mult, ALU.add)
            dve.drain()
            V.tensor_scalar(TT8[:, :, 0], TAB[:, 2, :], -1.0, float(s["zero"]), ALU.mult, ALU.add)
            dve.drain()
            V.tensor_tensor(TAB[:, 1, :], TAB[:, 1, :], TT8[:, :, 0], ALU.mult)
            dve.drain()
            V.tensor_tensor(TAB[:, 1, :], TAB[:, 1, :], TAB[:, 2, :], ALU.add)
            dve.drain()
            V.tensor_copy(TABI[:, :, :].rearrange("p a t -> p (a t)"), TAB[:, :, :].rearrange("p a t -> p (a t)"))
            for q in range(2):
                dve.wait_ge(scat[q], STORES + 16 * GRP * NB * GROUPS // 2)
            for e in ("pe", "act"):
                dve.wait_ge(pass_done[e], NB * NPASS + 1)
            for c in t_out:
                dve.wait_ge(c, STORES + 16 * QUARTERS * NB // 2)
            V.memset(ZR, 0.0)
            dve.drain()
            V.memset(ZR.rearrange("p (k c) -> p k c", c=ROW)[:, :, TOK], NOWHERE)
            dve.drain().then_inc(tab_done, 1)

            def low_rows(t, q):
                dve.wait_ge(act_ht, CREDIT + t + 1)
                for a in range(HALVES):
                    V.tensor_tensor(HTL[:, q, a, :], B[a][:, :], HTH[:, q, a, :].bitcast(F32), ALU.subtract)
                dve.drain().then_inc(dve_ht, 1)

            def outputs(t, q, g, h):
                pair = [P, 2, C]
                dve.wait_ge(pe_y, CREDIT + 2 * t + g + 1)
                V.tensor_tensor(YU[:, g, :, :], B[5 + g][:, :].rearrange("p (k c) -> p k c", c=C),
                                B2[:, q, :].unsqueeze(1).to_broadcast(pair), ALU.add).then_inc(dve_yp, 1)
                dve.drain()
                for k in range(2):
                    V.tensor_scalar_mul(YU[:, g, k, :], YU[:, g, k, :], XR[:, q, 2 * g + k, PRB:PRB + 1])
                dve.drain()
                V.tensor_scalar(YV[:, g, :, :], YU[:, g, :, :], 5000.0, -5000.0, ALU.min, ALU.max)
                V.tensor_scalar(YW[:, g, :, :], YU[:, g, :, :], -5000.0, 5000.0, ALU.max, ALU.min)
                V.tensor_scalar(YM[:, g, :, :], YU[:, g, :, :].bitcast(U32), 0xFFFFFFFF, 0x7F800000,
                                ALU.bitwise_xor, ALU.bitwise_and)
                dve.drain()
                V.tensor_tensor(YV[:, g, :, :], YV[:, g, :, :], YW[:, g, :, :], ALU.add)
                dve.drain()
                V.copy_predicated(YV[:, g, :, :], YM[:, g, :, :], YU[:, g, :, :])
                if g == 0:
                    dve.wait_ge(y_out[q], STORES + 16 * GRP * h)
                    V.tensor_copy(IDX[:, q, :], XR[:, q, :, TOK])
                dve.drain()
                V.tensor_tensor(YO[:, q, 2 * g:2 * g + 2, :], YV[:, g, :, :], XR[:, q, 2 * g:2 * g + 2, 0:C], ALU.add)
                dve.drain().then_inc(dve_y, 1)

            low_rows(0, 0)
            with dve.Fori(0, NT // 2) as h:
                for q in range(2):
                    t = 2 * h + q
                    for f in range(FB):
                        dve.wait_ge(act_h, CREDIT + t * FB + f + 1)
                        V.tensor_tensor(HSL[:, f, :], HSF[:, f, :], HSH[:, f, :].bitcast(F32),
                                        ALU.subtract).then_inc(dve_hl, 1)
                    outputs(t, q, 0, h)
                    low_rows(t + 1, 1 - q)
                    outputs(t, q, 1, h)

            with dve.Fori(0, NB * GROUPS // 2) as h:
                for q in range(2):
                    dve.wait_ge(pe_ot, CREDIT + 2 * h + q + 1)
                    dve.wait_ge(o_out[q], STORES + 16 * h)
                    V.tensor_copy(OB[:, q, 0, :], B[2 * q][:, :]).then_inc(dve_ot, 1)

        @block.gpsimd
        def _(pool):
            G = nc.gpsimd
            for c in pool_credit:
                pool.sem_inc(c, CREDIT)
            pool.memset(primed[:, :], 0.0)
            pool.drain()
            pool.sem_inc(pool_prep, 1)
            for n, c in enumerate((*scat, *y_out, *o_out)):
                pool.dma_start(primer[n:n + 1, :], primed[0:1, :]).then_inc(c, STORES)
            prepared(pool)

            def window_pass(b, v):
                nm = TILES + 4

                def centre(m, k):
                    n = b * nm + m
                    pool.wait_ge(pe_gram, CREDIT + n - 3)
                    stand_alone(pool)
                    G.tensor_copy(MS[0:R, k % 4, :], FH[0:R, bass.ds(m * P + HALO, P)]).then_inc(pool_ms, 1)

                def cut(m, k):
                    pool.wait_ge(act_e, CREDIT + b * nm + m + 1)
                    stand_alone(pool)
                    G.memset(ER[0:W, k % 8, 512:512 + W], 0.0)
                    G.memset(ER[W:P, k % 8, W:2 * W], 0.0)
                    pool.drain().then_inc(pool_mask, 1)

                for m in range(4):
                    centre(m, m)
                for m in range(4):
                    cut(m, m)
                with pool.Fori(0, PAIRS // 4) as h:
                    for j in range(4):
                        m = 8 * h + 2 * j + 4
                        for t in range(2):
                            centre(m + t, 2 * j + 4 + t)
                        for t in range(2):
                            cut(m + t, 2 * j + 4 + t)

            def attention_pass(b, v):
                with pool.Fori(0, GROUPS // 2) as h:
                    for k in range(2 * GRP):
                        i = h * 2 * GRP + k
                        pool.wait_ge(xn_done, (b * 2 + 1) * TILES + i + 1)
                        tile = TT[:, v, bass.ds(i, 1), 0:C].rearrange("p o c -> p (o c)")
                        G.tensor_tensor(tile, tile, BO[:, :], ALU.add).then_inc(pool_bias, 1)

            def scatter(b, v):
                pool.wait_ge(dve_slot, b + 1)
                for g in range(GROUPS):
                    q = g % 2
                    pool.wait_ge(scat[q], STORES + 16 * GRP * (b * (GROUPS // 2) + g // 2))
                    stand_alone(pool)
                    for k in range(GRP):
                        i = g * GRP + k
                        G.indirect_dma_start(rows, bass.IndirectOffsetOnAxis(ap=SLI[:, i:i + 1].bitcast(U32), axis=0),
                                             TT[:, v, i, :], None, bounds_check=s["rows"] - 1, oob_is_err=False).then_inc(scat[q], 16)
                for q in range(2):
                    pool.wait_ge(scat[q], STORES + 16 * GRP * (b + 1) * (GROUPS // 2))
                stand_alone(pool)

            with pool.Fori(0, NB // 2) as bb:
                for v in range(2):
                    b = 2 * bb + v
                    pass_starts(pool, "pool", b * NPASS + 2)
                    window_pass(b, v)
                    pass_starts(pool, "pool", b * NPASS + 5)
                    attention_pass(b, v)
                    scatter(b, v)

            def low_w1(t, q):
                pool.wait_ge(act_w1, CREDIT + t + 1)
                stand_alone(pool)
                G.tensor_tensor(W1L[:, q, :, :].rearrange("p a f -> p (a f)"), W1R[:, :, :].rearrange("p a f -> p (a f)"),
                                W1H[:, q, :, :].bitcast(F32).rearrange("p a f -> p (a f)"),
                                ALU.subtract).then_inc(pool_w1, 1)

            def low_w2(t, q):
                pool.wait_ge(act_w2, CREDIT + t + 1)
                stand_alone(pool)
                G.tensor_tensor(W2L[:, q, :, :].rearrange("p a f -> p (a f)"), W2R[:, :, :].rearrange("p a f -> p (a f)"),
                                W2H[:, q, :, :].bitcast(F32).rearrange("p a f -> p (a f)"),
                                ALU.subtract).then_inc(pool_w2, 1)

            low_w1(0, 0)
            low_w2(0, 0)
            with pool.Fori(0, NT // 2) as h:
                for q in range(2):
                    t = 2 * h + q
                    low_w1(t + 1, 1 - q)
                    low_w2(t + 1, 1 - q)
                    for k in range(GRP):
                        if k % 2 == 0:
                            pool.wait_ge(dve_y, CREDIT + t * 2 + k // 2 + 1)
                            stand_alone(pool)
                        G.indirect_dma_start(toks, bass.IndirectOffsetOnAxis(ap=IDX[:, q, k:k + 1].bitcast(U32), axis=0),
                                             YO[:, q, k, :], None, bounds_check=s["tokens"] - 1,
                                             oob_is_err=False).then_inc(y_out[q], 16)
            with pool.Fori(0, NB) as b:
                with pool.Fori(0, GROUPS // 2) as h:
                    for q in range(2):
                        pool.wait_ge(act_ot, b * GROUPS + 2 * h + q + 1 + CREDIT)
                        pool.wait_ge(dve_ot, b * GROUPS + 2 * h + q + 1 + CREDIT)
                        stand_alone(pool)
                        pool.dma_start(out_v[bass.ds(b, 1), :, :, bass.ds(h * 2 * GC + q * GC, GC)]
                                       .rearrange("o c a n -> c (o a) n"), OB[:, q, :, :]).then_inc(o_out[q], 16)
            for q in range(2):
                pool.wait_ge(o_out[q], STORES + 16 * NB * GROUPS // 2)


_INS = ["x", "L0_conv_W_reduce", "L0_conv_W_proj", "L1_attn_W_qkv", "L1_attn_W_out", "L1_attn_b_out",
        "L1_ffn_gate_w", "L1_ffn_gate_b", "L1_ffn_w1", "L1_ffn_b1", "L1_ffn_w2", "L1_ffn_b2"]


def kernel(**inputs):
    import numpy as _np
    import concourse.bacc as _bacc
    from concourse import mybir as _mybir
    from concourse.bass_utils import run_bass_kernel_spmd as _run

    nc = _bacc.Bacc("TRN2", target_bir_lowering=False, num_devices=1)
    s = sizes(inputs["x"].shape[0])
    arrays, args = {}, []
    named = [(n, _np.ascontiguousarray(inputs[n])) for n in _INS]
    named += list(zip(("konst", "band"), constants(_np, s)))
    for name, a in named:
        arrays[f"in_{name}_dram"] = a
        args.append(nc.dram_tensor(f"in_{name}_dram", a.shape, _mybir.dt.from_np(a.dtype), kind="ExternalInput").ap())
    out = nc.dram_tensor("out_0_dram", inputs["x"].shape, _mybir.dt.float32, kind="ExternalOutput").ap()
    build(nc, s, *args, out)
    r = _run(nc, [arrays], core_ids=[0])
    return r.results[0]["out_0_dram"]
```
